# Optimizing a Trainium2 kernel written in Bass

```python
import numpy as np
import jax
import jax.numpy as jnp

def _softmax(x, axis=-1):
    return jax.nn.softmax(x, axis=axis)

def _gelu(x):
    return jax.nn.gelu(x, approximate=True)

def _silu(x):
    return jax.nn.silu(x)

def _sigmoid(x):
    return jax.nn.sigmoid(x)

def _layernorm(x, axis=-1, eps=1e-05):
    m = jnp.mean(x, axis=axis, keepdims=True)
    v = jnp.var(x, axis=axis, keepdims=True)
    return (x - m) / jnp.sqrt(v + eps)

def _scatter_add(tgt, idx, src, axis=0):
    return tgt.at[idx].add(src)

def _segment_sum(src, seg, n):
    return jax.ops.segment_sum(src, seg, n)
kernel_name = 'mk_flamingo_gated_d1_seqx_r4_cc9605'

def setup_inputs(seed: int=0):
    np.random.seed(seed)
    _w = jnp.asarray

    def _rec_inputs():
        import jax
        import jax.numpy as jnp
        _rk = jax.random.key(seed)
        x = 7.22e-05 + 1 * jax.random.normal(jax.random.fold_in(_rk, 1), (32, 112, 256), jnp.float32)
        _lenS = 112 - jax.random.randint(jax.random.fold_in(_rk, 7), (32,), 0, max(1, 112 // 4) + 1, jnp.int32)
        _lenS2 = 375 - jax.random.randint(jax.random.fold_in(_rk, 8), (32,), 0, max(1, 375 // 4) + 1, jnp.int32)
        _ctx_1024P = jax.random.normal(jax.random.fold_in(_rk, 11), (32, 16, 256), jnp.float32)
        _ctx_1024c = jax.random.dirichlet(jax.random.fold_in(_rk, 511), 0.3 * jnp.ones((16,), jnp.float32), (32, 375))
        _ctx_1024t = jnp.einsum('bsk,bkd->bsd', _ctx_1024c, _ctx_1024P)
        _ctx_1024t = _ctx_1024t * jax.lax.rsqrt(jnp.mean(jnp.square(_ctx_1024t)) + 1e-12) * 0.953939
        ctx_1024 = 4.13588e-05 + 0.999923 * (_ctx_1024t + 0.3 * jax.random.normal(jax.random.fold_in(_rk, 611), (32, 375, 256), jnp.float32))
        _g = jax.random.normal(jax.random.fold_in(_rk, 9001), (2, 1), jnp.float32)
        _g = jnp.sign(_g) * jnp.maximum(jnp.abs(_g), 1.0) + (_g == 0) * 1.0
        g_xattn = _g[0]
        g_ffn = _g[1]
        return (x, ctx_1024, g_xattn, g_ffn)
    x, ctx_1024, g_xattn, g_ffn = _rec_inputs()

    def _L0_xattn_setup():
        import jax, jax.numpy as jnp
        import numpy as np
        B, N, D, H = (4, 512, 256, 16)
        HD = D // H

        def _heads(x):
            b, n, _ = x.shape
            return x.reshape(b, n, H, HD).transpose(0, 2, 1, 3)
        key = jax.random.key(seed)
        ks = jax.random.split(key, 11)
        s = 1.0 / np.sqrt(D)
        return {'q': jax.random.normal(ks[0], (B, N, D), jnp.float32), 'k': jax.random.normal(ks[1], (B, N, D), jnp.float32), 'v': jax.random.normal(ks[2], (B, N, D), jnp.float32), 'Wq': jax.random.normal(ks[3], (D, D), jnp.float32) * s, 'bq': jnp.zeros((D,), jnp.float32), 'Wk': jax.random.normal(ks[4], (D, D), jnp.float32) * s, 'bk': jnp.zeros((D,), jnp.float32), 'Wv': jax.random.normal(ks[5], (D, D), jnp.float32) * s, 'bv': jnp.zeros((D,), jnp.float32), 'Wo': jax.random.normal(ks[6], (D, D), jnp.float32) * s, 'bo': jnp.zeros((D,), jnp.float32)}
    _L0_xattn_all = _L0_xattn_setup()
    _L0_xattn_in = {k: v for k, v in _L0_xattn_all.items() if k in ('Wq', 'bq', 'Wk', 'bk', 'Wv', 'bv', 'Wo', 'bo')}
    del _L0_xattn_all

    def _L0_ffn_setup():
        import jax, jax.numpy as jnp
        import numpy as np
        D_MODEL = 256
        NHEAD = 16
        HEAD_DIM = D_MODEL // NHEAD
        FF = 512
        NUM_EXPERTS = 8
        EPS = 1e-05

        def _ln(x, g, b):
            m = x.mean(-1, keepdims=True)
            v = ((x - m) ** 2).mean(-1, keepdims=True)
            return (x - m) / jnp.sqrt(v + EPS) * g + b

        def _attention(src, Wq, bq, Wk, bk, Wv, bv, Wo, bo):
            B, T, d = src.shape
            scale = HEAD_DIM ** (-0.5)
            q = (src @ Wq + bq).reshape(B, T, NHEAD, HEAD_DIM)
            k = (src @ Wk + bk).reshape(B, T, NHEAD, HEAD_DIM)
            v = (src @ Wv + bv).reshape(B, T, NHEAD, HEAD_DIM)
            scores = jnp.einsum('bqhd,bkhd->bhqk', q, k) * scale
            probs = jax.nn.softmax(scores, axis=-1)
            out = jnp.einsum('bhqk,bkhd->bqhd', probs, v).reshape(B, T, d)
            return out @ Wo + bo

        def _moe(x, gW, gb, W1, b1, W2, b2):
            B, T, d = x.shape
            xf = x.reshape(-1, d)
            gates = jax.nn.softmax(xf @ gW + gb, axis=-1)
            top2_scores, top2_idx = jax.lax.top_k(gates, 2)
            w = (jax.nn.one_hot(top2_idx, NUM_EXPERTS, dtype=xf.dtype) * top2_scores[..., None]).sum(1)
            h = jax.nn.relu(jnp.einsum('nd,edf->enf', xf, W1) + b1[:, None, :])
            y = jnp.einsum('enf,efd->end', h, W2) + b2[:, None, :]
            out = jnp.einsum('ne,end->nd', w, y)
            return out.reshape(B, T, d)
        key = jax.random.key(seed)
        ks = jax.random.split(key, 12)
        s = 0.02
        d, f, E = (D_MODEL, FF, NUM_EXPERTS)
        return {'src': jax.random.normal(ks[0], (8, 128, d), dtype=jnp.float32), 'Wq': jax.random.normal(ks[1], (d, d), dtype=jnp.float32) * s, 'bq': jnp.zeros((d,), jnp.float32), 'Wk': jax.random.normal(ks[2], (d, d), dtype=jnp.float32) * s, 'bk': jnp.zeros((d,), jnp.float32), 'Wv': jax.random.normal(ks[3], (d, d), dtype=jnp.float32) * s, 'bv': jnp.zeros((d,), jnp.float32), 'Wo': jax.random.normal(ks[4], (d, d), dtype=jnp.float32) * s, 'bo': jnp.zeros((d,), jnp.float32), 'gW': jax.random.normal(ks[5], (d, E), dtype=jnp.float32) * s, 'gb': jnp.zeros((E,), jnp.float32), 'W1': jax.random.normal(ks[6], (E, d, f), dtype=jnp.float32) * s, 'b1': jnp.zeros((E, f), jnp.float32), 'W2': jax.random.normal(ks[7], (E, f, d), dtype=jnp.float32) * s, 'b2': jnp.zeros((E, d), jnp.float32), 'ln1_g': jnp.ones((d,), jnp.float32), 'ln1_b': jnp.zeros((d,), jnp.float32), 'ln2_g': jnp.ones((d,), jnp.float32), 'ln2_b': jnp.zeros((d,), jnp.float32)}
    _L0_ffn_all = _L0_ffn_setup()
    _L0_ffn_in = {k: v for k, v in _L0_ffn_all.items() if k in ('Wq', 'bq', 'Wk', 'bk', 'Wv', 'bv', 'Wo', 'bo', 'gW', 'gb', 'W1', 'b1', 'W2', 'b2', 'ln1_g', 'ln1_b', 'ln2_g', 'ln2_b')}
    del _L0_ffn_all
    return {'x': x, 'ctx_1024': ctx_1024, 'g_xattn': g_xattn, 'g_ffn': g_ffn, 'L0_xattn_Wq': _L0_xattn_in['Wq'], 'L0_xattn_bq': _L0_xattn_in['bq'], 'L0_xattn_Wk': _L0_xattn_in['Wk'], 'L0_xattn_bk': _L0_xattn_in['bk'], 'L0_xattn_Wv': _L0_xattn_in['Wv'], 'L0_xattn_bv': _L0_xattn_in['bv'], 'L0_xattn_Wo': _L0_xattn_in['Wo'], 'L0_xattn_bo': _L0_xattn_in['bo'], 'L0_ffn_Wq': _L0_ffn_in['Wq'], 'L0_ffn_bq': _L0_ffn_in['bq'], 'L0_ffn_Wk': _L0_ffn_in['Wk'], 'L0_ffn_bk': _L0_ffn_in['bk'], 'L0_ffn_Wv': _L0_ffn_in['Wv'], 'L0_ffn_bv': _L0_ffn_in['bv'], 'L0_ffn_Wo': _L0_ffn_in['Wo'], 'L0_ffn_bo': _L0_ffn_in['bo'], 'L0_ffn_gW': _L0_ffn_in['gW'], 'L0_ffn_gb': _L0_ffn_in['gb'], 'L0_ffn_W1': _L0_ffn_in['W1'], 'L0_ffn_b1': _L0_ffn_in['b1'], 'L0_ffn_W2': _L0_ffn_in['W2'], 'L0_ffn_b2': _L0_ffn_in['b2'], 'L0_ffn_ln1_g': _L0_ffn_in['ln1_g'], 'L0_ffn_ln1_b': _L0_ffn_in['ln1_b'], 'L0_ffn_ln2_g': _L0_ffn_in['ln2_g'], 'L0_ffn_ln2_b': _L0_ffn_in['ln2_b']}

def reference(x, ctx_1024, g_xattn, g_ffn, L0_xattn_Wq, L0_xattn_bq, L0_xattn_Wk, L0_xattn_bk, L0_xattn_Wv, L0_xattn_bv, L0_xattn_Wo, L0_xattn_bo, L0_ffn_Wq, L0_ffn_bq, L0_ffn_Wk, L0_ffn_bk, L0_ffn_Wv, L0_ffn_bv, L0_ffn_Wo, L0_ffn_bo, L0_ffn_gW, L0_ffn_gb, L0_ffn_W1, L0_ffn_b1, L0_ffn_W2, L0_ffn_b2, L0_ffn_ln1_g, L0_ffn_ln1_b, L0_ffn_ln2_g, L0_ffn_ln2_b):
    import jax
    import jax.numpy as jnp

    def _L0_xattn_ref(q, k, v, Wq, bq, Wk, bk, Wv, bv, Wo, bo):
        import jax, jax.numpy as jnp
        import numpy as np
        B, N, D, H = (4, 512, 256, 16)
        HD = D // H

        def _heads(x):
            b, n, _ = x.shape
            return x.reshape(b, n, H, HD).transpose(0, 2, 1, 3)
        qh = _heads(q @ Wq.T + bq)
        kh = _heads(k @ Wk.T + bk)
        vh = _heads(v @ Wv.T + bv)
        scores = jnp.einsum('bhqd,bhkd->bhqk', qh, kh) / np.sqrt(HD).astype(np.float32)
        probs = jax.nn.softmax(scores, axis=-1)
        out = jnp.einsum('bhqk,bhkd->bhqd', probs, vh)
        out = out.transpose(0, 2, 1, 3).reshape(q.shape[0], q.shape[1], D)
        return out @ Wo.T + bo

    def _L0_ffn_ref(src, Wq, bq, Wk, bk, Wv, bv, Wo, bo, gW, gb, W1, b1, W2, b2, ln1_g, ln1_b, ln2_g, ln2_b):
        import jax, jax.numpy as jnp
        import numpy as np
        D_MODEL = 256
        NHEAD = 16
        HEAD_DIM = D_MODEL // NHEAD
        FF = 512
        NUM_EXPERTS = 8
        EPS = 1e-05

        def _ln(x, g, b):
            m = x.mean(-1, keepdims=True)
            v = ((x - m) ** 2).mean(-1, keepdims=True)
            return (x - m) / jnp.sqrt(v + EPS) * g + b

        def _attention(src, Wq, bq, Wk, bk, Wv, bv, Wo, bo):
            B, T, d = src.shape
            scale = HEAD_DIM ** (-0.5)
            q = (src @ Wq + bq).reshape(B, T, NHEAD, HEAD_DIM)
            k = (src @ Wk + bk).reshape(B, T, NHEAD, HEAD_DIM)
            v = (src @ Wv + bv).reshape(B, T, NHEAD, HEAD_DIM)
            scores = jnp.einsum('bqhd,bkhd->bhqk', q, k) * scale
            probs = jax.nn.softmax(scores, axis=-1)
            out = jnp.einsum('bhqk,bkhd->bqhd', probs, v).reshape(B, T, d)
            return out @ Wo + bo

        def _moe(x, gW, gb, W1, b1, W2, b2):
            B, T, d = x.shape
            xf = x.reshape(-1, d)
            gates = jax.nn.softmax(xf @ gW + gb, axis=-1)
            top2_scores, top2_idx = jax.lax.top_k(gates, 2)
            w = (jax.nn.one_hot(top2_idx, NUM_EXPERTS, dtype=xf.dtype) * top2_scores[..., None]).sum(1)
            h = jax.nn.relu(jnp.einsum('nd,edf->enf', xf, W1) + b1[:, None, :])
            y = jnp.einsum('enf,efd->end', h, W2) + b2[:, None, :]
            out = jnp.einsum('ne,end->nd', w, y)
            return out.reshape(B, T, d)
        attn_out = _attention(src, Wq, bq, Wk, bk, Wv, bv, Wo, bo)
        x = _ln(src + attn_out, ln1_g, ln1_b)
        ff = _moe(x, gW, gb, W1, b1, W2, b2)
        return _ln(x + ff, ln2_g, ln2_b)
    x = x + jnp.tanh(g_xattn[0]) * _L0_xattn_ref(_layernorm(x, axis=-1), ctx_1024, ctx_1024, L0_xattn_Wq, L0_xattn_bq, L0_xattn_Wk, L0_xattn_bk, L0_xattn_Wv, L0_xattn_bv, L0_xattn_Wo, L0_xattn_bo)
    x = x + jnp.tanh(g_ffn[0]) * _L0_ffn_ref(_layernorm(x, axis=-1), L0_ffn_Wq, L0_ffn_bq, L0_ffn_Wk, L0_ffn_bk, L0_ffn_Wv, L0_ffn_bv, L0_ffn_Wo, L0_ffn_bo, L0_ffn_gW, L0_ffn_gb, L0_ffn_W1, L0_ffn_b1, L0_ffn_W2, L0_ffn_b2, L0_ffn_ln1_g, L0_ffn_ln1_b, L0_ffn_ln2_g, L0_ffn_ln2_b)
    return x

_drawn_inputs = setup_inputs


def setup_inputs(seed=0):
    import zlib

    import numpy as np

    out = dict(_drawn_inputs(seed))
    spreads = {'L0_xattn_bq': (0.0, 0.412),
     'L0_xattn_bk': (0.0, 0.8),
     'L0_xattn_bv': (0.0, 0.1),
     'L0_xattn_bo': (0.0, 0.1),
     'L0_ffn_bq': (0.0, 0.8),
     'L0_ffn_bk': (0.0, 0.8),
     'L0_ffn_bv': (0.0, 0.1),
     'L0_ffn_bo': (0.0, 0.1),
     'L0_ffn_gb': (0.0, 0.1),
     'L0_ffn_b1': (0.0, 0.405),
     'L0_ffn_b2': (0.0, 0.1),
     'L0_ffn_ln1_g': (1.0, 0.2),
     'L0_ffn_ln1_b': (0.0, 0.1),
     'L0_ffn_ln2_g': (1.0, 0.2),
     'L0_ffn_ln2_b': (0.0, 0.1)}
    factors = {'L0_ffn_Wq': 8.0, 'L0_ffn_Wk': 8.0}
    for name, (base, spread) in spreads.items():
        noise = np.random.default_rng([zlib.crc32(name.encode()), seed]).standard_normal(out[name].shape)
        drawn = base * np.exp(spread * noise) if base else spread * noise
        out[name] = jnp.asarray(drawn.astype(out[name].dtype))
    for name, factor in factors.items():
        out[name] = (out[name] * factor).astype(out[name].dtype)
    return out
```

```python
import concourse.bass as bass
from concourse import mybir
from contextlib import ExitStack

F32 = mybir.dt.float32
I32 = mybir.dt.int32
U32 = mybir.dt.uint32
BF16 = mybir.dt.bfloat16
ALU = mybir.AluOpType
ACT = mybir.ActivationFunctionType
AX_X = mybir.AxisListType.X

NB, T, D = 32, 112, 256
S = 375
H, HD = 16, 16
P = 128
DC = D // P
SC, NSC = 125, 3
HC = P // HD
G = 4
GT = G * T
NG = H // G
VW = 32
BANK = 512
EPS = 1e-5
POS_STEPS = 20
SCALE = HD ** -0.5
DMA = 16

E = 8
F = 512
FC = F // P
TOP = 2
REGION = NB * T + P
NT = 64
assert NT >= NB * T * TOP // P + E - 1 and NT % 2 == 0


def kind_of(step):
    return step.rstrip("0123456789")


def index_of(step):
    return int(step[len(kind_of(step)):] or 0)


class Plan:

    def __init__(self, items, peeled, lag, order, pools):
        self.items, self.peeled, self.lag, self.order, self.pools = items, peeled, lag, order, pools
        self.turns = items + max(lag.values())
        self.passes = (items - peeled) // 2
        assert (items - peeled) % 2 == 0
        self.repeats = {kind_of(s): sum(kind_of(x) == kind_of(s) for x in order) for s in order}

    def run(self, eng, do):
        for b in range(self.peeled):
            do(Turn(self, b))
        with eng.Fori(0, self.passes) as p:
            for b in range(self.peeled, self.peeled + 2):
                do(Turn(self, b, p))
        for b in range(self.items, self.turns):
            do(Turn(self, b))


class Turn:

    def __init__(self, plan, base, p=None):
        self.plan, self.base, self.p = plan, base, p

    def last(self):
        return Turn(self.plan, self.base - 1, self.p)

    def active(self, stage):
        return 0 <= self.base - self.plan.lag[stage] < self.plan.items

    def steps(self):
        return [s for s in self.plan.order if self.active(s[0])]

    def item(self, stage, times=1, plus=0):
        const = (self.base - self.plan.lag[stage]) * times + plus
        return const if self.p is None else self.p * (2 * times) + const

    def later(self, stage, lag):
        return self.base - self.plan.lag[stage] >= lag

    def parity(self, stage):
        return (self.base - self.plan.lag[stage]) % 2

    def dmas(self, stage, plus=1, each=1):
        const = ((self.base - self.plan.lag[stage]) // 2 + plus) * DMA * each
        return const if self.p is None else self.p * (DMA * each) + const

    def count(self, step, plus=1):
        return self.item(step[0], self.plan.repeats[kind_of(step)], index_of(step) + plus)

    def uses(self, pool, step):
        kinds = self.plan.pools[pool][1]
        uses = [(b, s) for b in range(self.base + 1) for s in Turn(self.plan, b).steps() if kind_of(s) in kinds]
        return uses[:uses.index((self.base, step)) + 1]

    def buffer(self, pool, step):
        return (len(self.uses(pool, step)) - 1) % self.plan.pools[pool][0]

    def before(self, pool, step):
        uses = self.uses(pool, step)
        depth = self.plan.pools[pool][0]
        if len(uses) <= depth:
            return None
        b, s = uses[-1 - depth]
        return Turn(self.plan, b, self.p), s


ATTENTION = Plan(
    NB, 8, {"N": 0, "A": 1, "B": 2, "C": 3, "D": 4, "E": 5},
    ["B.s0", "A.xT", "A.ctxT", "B.s1", "B.pv0", "A.q", "B.s2", "B.pv1", "E.oN", "A.k",
     "B.s3", "B.pv2", "C.yT", "A.v", "B.s4", "B.pv3", "E.aT", "B.s5", "B.pv4", "A.narrow", "E.out",
     "A.max0", "C.qk", "B.s6", "B.pv5", "A.max1", "C.v", "B.s7", "B.pv6", "A.max2", "E.norm",
     "B.s8", "B.pv7", "A.max3", "B.s9", "B.pv8", "E.xT", "A.max4", "N.ln", "C.narrow", "B.s10", "B.pv9",
     "A.max5", "C.max0", "E.gate", "B.s11", "B.pv10", "A.max6", "C.max1", "D.s0", "B.pv11", "A.max7",
     "D.s1", "C.mT", "B.oN", "E.pick", "D.s2", "D.pv0", "B.aT", "A.mT", "E.rank", "D.s3", "D.pv1",
     "B.out", "D.pv2", "B.norm", "E.send", "D.pv3"],
    {"wide": (2, {"A.ctxT", "A.k", "A.v", "A.max", "C.qk", "C.max"}),
     "score": (2, {"B.s", "D.s"}),
     "turned": (1, {"A.xT", "A.q", "A.mT", "B.oN", "B.aT", "B.out", "C.yT", "C.v", "C.mT",
                    "E.oN", "E.aT", "E.out", "E.xT", "E.gate", "E.rank"}),
     "probs": (4, {"B.s", "D.s"})})

EXPERTS = Plan(NT, 6, {"A": 0, "B": 1, "C": 2, "D": 3}, ["A.x", "B.h", "C.hT", "D.y"], {})

JOIN = Plan(NB, 4, {"A": 0, "B": 1}, ["A.add", "B.norm"], {})


def build(nc, io):
    ctx = ExitStack()
    with ctx:
        def sb(name, shape, dt=F32):
            return ctx.enter_context(nc.sbuf_tensor(name, shape, dt))

        def sem(name):
            return ctx.enter_context(nc.semaphore(name))

        ident = sb("ident", [P, P])
        head_mask = sb("head_mask", [P, HC])
        pick = sb("pick", [H, H, SC], BF16)
        minus_half = sb("minus_half", [P, 1])
        spare_dve, spare_pool = sb("spare_dve", [P, 3]), sb("spare_pool", [P, 3])
        tile_no = sb("tile_no", [P, 1], I32)
        wxq, wxk, wxv, wxo = (sb(n, [P, DC, D]) for n in ("wxq", "wxk", "wxv", "wxo"))
        wsq, wsk, wsv, wso = (sb(n, [P, DC, D]) for n in ("wsq", "wsk", "wsv", "wso"))
        bxq, bxk, bsq, bsk = (sb(n, [P, DC]) for n in ("bxq", "bxk", "bsq", "bsk"))
        bxv, bxo, bsv, bso = (sb(n, [P, D]) for n in ("bxv", "bxo", "bsv", "bso"))
        ln1_g, ln1_b = sb("ln1_g", [P, D]), sb("ln1_b", [P, D])
        ln2_g, ln2_b = sb("ln2_g", [P, D]), sb("ln2_b", [P, D])
        ln2_gain, ln2_shift = sb("ln2_gain", [P, D]), sb("ln2_shift", [P, D])
        gates = sb("gates", [P, 2])
        tanh_g = sb("tanh_g", [P, 2])

        gate_w = sb("gate_w", [P, DC, E])
        gate_b = sb("gate_b", [P, E])
        hidden_w = sb("hidden_w", [P, DC, E * F])
        hidden_b = sb("hidden_b", [P, FC, E])
        output_w = sb("output_w", [P, FC, E * D])
        below = sb("below", [P, P], BF16)
        ones = sb("ones", [P, P], BF16)
        count_up = sb("count_up", [P, E], I32)
        expert_ids = sb("expert_ids", [P, E])
        region_of = sb("region_of", [P, E])
        next_row = sb("next_row", [P, E])
        routes = sb("routes", [T, 3 * TOP, NB])

        wide = [ctx.enter_context(nc.psum_tensor(f"wide{i}", [P, 2, BANK], F32)) for i in range(2)]
        score = [ctx.enter_context(nc.psum_tensor(f"score{i}", [P, BANK], F32)) for i in range(2)]
        turned = ctx.enter_context(nc.psum_tensor("turned", [P, BANK], F32))
        sums = ctx.enter_context(nc.psum_tensor("sums", [P, BANK], F32))

        rows_bank = [turned, sums]

        scope = ExitStack()

        def sb(name, shape, dt=F32):
            return scope.enter_context(nc.sbuf_tensor(name, shape, dt))

        x_in = sb("x_in", [T, 2, D])
        ctx_in = sb("ctx_in", [SC, 2, NSC, D])
        x_res = sb("x_res", [T, 2, D])
        stats = {s: sb("stats_" + s, [T, 6]) for s in "NBE"}
        moments = {s: sb("moments_" + s, [T, 2]) for s in "NBE"}
        inv_std = {s: sb("inv_std_" + s, [T, 1]) for s in "NBE"}
        x_norm = sb("x_norm", [T, D])
        x_normT = sb("x_normT", [P, DC, T])
        ctxT = sb("ctxT", [P, DC, S])
        qT = {s: sb("qT_" + s, [P, DC, T]) for s in "AC"}
        q_block = {s: sb("q_block_" + s, [P, 2, H, T]) for s in "AC"}
        q_block16 = {s: sb("q_block16_" + s, [P, H, T], BF16) for s in "AC"}
        kT = {"A": sb("kT_A", [P, 2, DC, S]), "C": sb("kT_C", [P, 2, DC, T])}
        kT16 = {"A": sb("kT16_A", [P, DC, S], BF16), "C": sb("kT16_C", [P, DC, T], BF16)}
        values = {"A": sb("values_A", [SC, 2, NSC, H, VW]), "C": sb("values_C", [T, 2, 1, H, VW])}
        row_max = {s: sb("row_max_" + s, [T, H]) for s in "AC"}
        maxT = {s: sb("maxT_" + s, [H, 2, T], BF16) for s in "AC"}
        probs = sb("probs", [SC, ATTENTION.pools["probs"][0], GT])
        outT = {s: sb("outT_" + s, [P, GT]) for s in "BE"}
        inv_sum = {s: sb("inv_sum_" + s, [T, H]) for s in "BE"}
        att = {s: sb("att_" + s, [T, D]) for s in "BE"}
        attT = {s: sb("attT_" + s, [P, DC, T]) for s in "BE"}
        proj = sb("proj", [T, D])
        x1 = sb("x1", [T, 2, D])
        x1_shift = sb("x1_shift", [T, 2, D])
        y = sb("y", [T, 2, D])
        yT = sb("yT", [P, DC, T])
        y_bias = sb("y_bias", [T, 2, D])
        r = sb("r", [T, D])
        r_norm = sb("r_norm", [T, D])
        r_gain = sb("r_gain", [T, D])
        xm = sb("xm", [T, 2, D])

        xmT = sb("xmT", [P, DC, T])
        logits = sb("logits", [T, E])
        top_logits = sb("top_logits", [T, 8])
        minus_max = sb("minus_max", [T, 1])
        gate_exp = sb("gate_exp", [T, E])
        gate_sum = sb("gate_sum", [T, 1])
        gate_inv = sb("gate_inv", [T, 1])
        gate = sb("gate", [T, E])
        top_gate = sb("top_gate", [T, 8])
        top_expert = sb("top_expert", [T, 8], U32)
        chosen = sb("chosen", [T, TOP, E])
        chosen_any = sb("chosen_any", [T, E], BF16)
        rows_here = sb("rows_here", [T, E])
        rows_pick = sb("rows_pick", [T, TOP, E])
        route = sb("route", [T, 3 * TOP])
        send_row = sb("send_row", [T, 2, TOP], U32)

        scope.close()
        scope = ctx.enter_context(ExitStack())
        zero_rows = sb("zero_rows", [P, D])
        output_b = sb("output_b", [P, E * D])
        counts = sb("counts", [P, E])
        tiles_i = sb("tiles_i", [P, E], I32)
        tiles = sb("tiles", [P, E])
        tiles_end = sb("tiles_end", [P, E])
        ones_f = sb("ones_f", [P, E])
        to_tiles = sb("to_tiles", [P, E])
        next_i = sb("next_i", [P, E], I32)
        tile_f = sb("tile_f", [P, 1])
        past = sb("past", [P, E])
        count_step = sb("count_step", [P, E])
        junk = sb("junk", [P, 3, E])
        tile_expert, tile_base, tile_count = (sb(n, [P, 1]) for n in ("tile_expert", "tile_base", "tile_count"))
        tile_row, tile_rest = sb("tile_row", [P, 1]), sb("tile_rest", [P, 1])
        table = sb("table", [1, 2 * NT], I32)
        is_expert = sb("is_expert", [T, TOP, NB])
        positions_f = sb("positions_f", [T, E + 1, TOP, NB])
        positions = sb("positions", [T, TOP, NB], U32)
        tile_in = sb("tile_in", [P, 2, D])
        tile_inT = sb("tile_inT", [P, 2, DC, P])
        hidden = sb("hidden", [P, 2, F])
        hiddenT = sb("hiddenT", [P, 2, FC, P])
        tile_out = sb("tile_out", [P, 2, D])
        xm_in = sb("xm_in", [T, 2, D])
        x1_in = sb("x1_in", [T, 2, D])
        take_row = sb("take_row", [T, 2, TOP], U32)
        taken_out = sb("taken_out", [T, 2, TOP, D])
        added = sb("added", [T, 2, TOP, D])
        join_stats = sb("join_stats", [T, 6])
        join_moments = sb("join_moments", [T, 2, 2])
        join_inv = sb("join_inv", [T, 2, 1])
        join_norm = sb("join_norm", [T, D])
        join_gain = sb("join_gain", [T, D])
        result = sb("result", [T, 2, D])

        made = {k: sem("made_" + k.replace(".", "_")) for k in ATTENTION.repeats}
        taken = {k: sem("taken_" + k.replace(".", "_")) for k in ATTENTION.repeats}
        gates_exped = sem("gates_exped")
        gate_steps = sem("gate_steps")
        row_steps = sem("row_steps")
        sent = [sem(f"sent{i}") for i in range(2)]
        routed = sem("routed")
        moe_loaded = sem("moe_loaded")
        output_b_loaded = sem("output_b_loaded")
        plan_steps = sem("plan_steps")
        zero_set = sem("zero_set")
        tails_zeroed = sem("tails_zeroed")
        table_turned = sem("table_turned")
        table_ready = sem("table_ready")
        pos_steps = sem("pos_steps")
        tile_loaded = [sem(f"tile_loaded{i}") for i in range(2)]
        out_stored = [sem(f"out_stored{i}") for i in range(2)]
        ex_made = {k: sem("ex_made_" + k.replace(".", "_")) for k in EXPERTS.repeats}
        ex_taken = {k: sem("ex_taken_" + k.replace(".", "_")) for k in EXPERTS.repeats}
        rows_copied = sem("rows_copied")
        gathered = [sem(f"gathered{i}") for i in range(2)]
        join_loaded = [sem(f"join_loaded{i}") for i in range(2)]
        result_stored = [sem(f"result_stored{i}") for i in range(2)]
        join_steps = sem("join_steps")
        join_inverted = sem("join_inverted")
        result_steps = sem("result_steps")
        w_loaded = {n: sem("w_loaded_" + n) for n in ("A", "B", "C")}
        x_loaded = [sem(f"x_loaded{i}") for i in range(2)]
        ctx_loaded = [sem(f"ctx_loaded{i}") for i in range(2)]
        res_loaded = [sem(f"res_loaded{i}") for i in range(2)]
        x1_stored = [sem(f"x1_stored{i}") for i in range(2)]
        xm_stored = [sem(f"xm_stored{i}") for i in range(2)]
        zeroed = sem("zeroed")
        vset = sem("vset")
        consts = sem("consts")
        tanh_done = sem("tanh_done")
        measured = {s: sem("measured_" + s) for s in "NBE"}
        inverted = {s: sem("inverted_" + s) for s in "NBE"}
        normed = {s: sem("normed_" + s) for s in "NBE"}
        blocked = {s: sem("blocked_" + s) for s in "AC"}
        q16 = {s: sem("q16_" + s) for s in "AC"}
        k16 = {s: sem("k16_" + s) for s in "AC"}
        inv_sums = {s: sem("inv_sums_" + s) for s in "BE"}
        averaged = {s: sem("averaged_" + s) for s in "BE"}
        resid = sem("resid")
        y_biased = sem("y_biased")
        shifted = sem("shifted")
        gained = sem("gained")

        def buffer_free(eng, t, pool, step, by):
            last = t.before(pool, step)
            if last is not None:
                eng.wait_ge(by[kind_of(last[1])], last[0].count(last[1]))

        def alone(eng, spare):
            eng.tensor_tensor(spare[0:1, 0:1], spare[0:1, 1:2], spare[0:1, 2:3], ALU.add)

        def attention_over(eng):
            for k in range(2):
                eng.wait_ge(sent[k], NB // 2 * DMA * TOP)

        def experts_over(eng):
            for k in range(2):
                eng.wait_ge(out_stored[k], NT // 2 * DMA)

        block = ctx.enter_context(nc.Block())

        @block.sync
        def _(sp):
            def square(w, a):
                return sp.dma_start(w[:, :, :], a.rearrange("(c p) n -> p c n", p=P))

            def column(b, a):
                return sp.dma_start(b[:, :], a.rearrange("(c p) -> p c", p=P), allow_slow_non_contiguous=True)

            def row(b, a):
                return sp.dma_start(b[:, :], a.partition_broadcast(P))

            def load(t):
                n, k = t.item("N"), t.parity("N")
                if t.later("N", 2):
                    sp.wait_ge(normed["N"], t.item("N", 1, -1))
                sp.dma_start(x_in[:, k, :], io["x"][bass.ds(n * T, T), :]).then_inc(x_loaded[k], DMA)
                if t.later("N", 2):
                    sp.wait_ge(made["A.ctxT"], t.item("N", 1, -1))
                sp.dma_start(ctx_in[:, k, :, :],
                             io["ctx"][bass.ds(n * S, S), :].rearrange("(j p) d -> p j d", p=SC)
                             ).then_inc(ctx_loaded[k], DMA)

            def turn(t):
                if t.active("N"):
                    load(t)
                if t.base == 3:
                    for e in range(E):
                        sp.dma_start(hidden_w[:, :, e * F:(e + 1) * F],
                                     io["hidden_w"][e].rearrange("(c p) f -> p c f", p=P)).then_inc(moe_loaded, DMA)
                        sp.dma_start(output_w[:, :, e * D:(e + 1) * D],
                                     io["output_w"][e].rearrange("(c p) d -> p c d", p=P)).then_inc(moe_loaded, DMA)
                        sp.dma_start(hidden_b[:, :, e:e + 1], io["hidden_b"][e].rearrange("(c p one) -> p c one", p=P, one=1),
                                     allow_slow_non_contiguous=True).then_inc(moe_loaded, DMA)
                if t.active("B"):
                    n, k = t.item("B"), t.parity("B")
                    if t.later("B", 2):
                        sp.wait_ge(resid, t.item("B", 1, -1))
                    sp.dma_start(x_res[:, k, :], io["x"][bass.ds(n * T, T), :]).then_inc(res_loaded[k], DMA)
                if t.active("E"):
                    n, k = t.item("E"), t.parity("E")
                    sp.wait_ge(gained, t.item("E", 2, 2))
                    sp.dma_start(io["xm"][bass.ds(n * T, T), :], xm[:, k, :]).then_inc(xm_stored[k], DMA)
                if t.active("B"):
                    n, k = t.item("B"), t.parity("B")
                    sp.wait_ge(shifted, t.item("B", 1, 1))
                    sp.dma_start(io["x1"][bass.ds(n * T, T), :], x1_shift[:, k, :]).then_inc(x1_stored[k], DMA)

            square(wxk, io["wxk"]).then_inc(w_loaded["A"], DMA)
            square(wxq, io["wxq"]).then_inc(w_loaded["A"], DMA)
            square(wxv, io["wxv"]).then_inc(w_loaded["A"], DMA)
            column(bxk, io["bxk"]).then_inc(w_loaded["A"], DMA)
            column(bxq, io["bxq"]).then_inc(w_loaded["A"], DMA)
            row(bxv, io["bxv"]).then_inc(w_loaded["A"], DMA)
            square(wxo, io["wxo"]).then_inc(w_loaded["B"], DMA)
            row(bxo, io["bxo"]).then_inc(w_loaded["B"], DMA)
            sp.dma_start(gates[:, 0:1], io["g_xattn"].partition_broadcast(P)).then_inc(w_loaded["B"], DMA)
            sp.dma_start(gates[:, 1:2], io["g_ffn"].partition_broadcast(P)).then_inc(w_loaded["B"], DMA)
            for w, a in ((wsq, "wsq"), (wsk, "wsk"), (wsv, "wsv"), (wso, "wso")):
                square(w, io[a]).then_inc(w_loaded["C"], DMA)
            for b, a in ((bsq, "bsq"), (bsk, "bsk")):
                column(b, io[a]).then_inc(w_loaded["C"], DMA)
            for b, a in ((bsv, "bsv"), (bso, "bso"), (gate_b, "gate_b"), (ln1_g, "ln1_g"), (ln1_b, "ln1_b"), (ln2_g, "ln2_g"),
                         (ln2_b, "ln2_b")):
                row(b, io[a]).then_inc(w_loaded["C"], DMA)
            sp.dma_start(gate_w[:, :, :], io["gate_w"].rearrange("(c p) e -> p c e", p=P)).then_inc(w_loaded["C"], DMA)
            ATTENTION.run(sp, turn)
            attention_over(sp)
            sp.dma_start(output_b[:, :], io["output_b"].rearrange("e d -> (e d)").partition_broadcast(P)
                         ).then_inc(output_b_loaded, DMA)
            sp.wait_ge(zero_set, 1)
            sp.wait_ge(plan_steps, 1)
            for e in range(E):
                row_no = sp.value_load(next_i[0:1, e:e + 1], min_val=e * REGION, max_val=e * REGION + NB * T)
                sp.dma_start(io["sent"][bass.ds(row_no, P), :], zero_rows[:, :]).then_inc(tails_zeroed, DMA)
            sp.wait_ge(tails_zeroed, E * DMA)
            sp.wait_ge(table_ready, 1)

            def expert_turn(t):
                if t.active("A"):
                    n, k = t.item("A"), t.parity("A")
                    first = sp.value_load(table[0:1, bass.ds(n + NT, 1)], min_val=0, max_val=E * REGION - P)
                    if t.later("A", 2):
                        sp.wait_ge(ex_made["A.x"], t.item("A", 1, -1))
                    sp.dma_start(tile_in[:, k, :], io["sent"][bass.ds(first, P), :]).then_inc(tile_loaded[k], DMA)

            EXPERTS.run(sp, expert_turn)
            for k in range(2):
                sp.wait_ge(x1_stored[k], NB // 2 * DMA)
                sp.wait_ge(xm_stored[k], NB // 2 * DMA)

            def join_turn(t):
                if t.active("A"):
                    n, k = t.item("A"), t.parity("A")
                    if t.later("A", 2):
                        sp.wait_ge(result_steps, t.item("A", 3, -3))
                    sp.dma_start(xm_in[:, k, :], io["xm"][bass.ds(n * T, T), :]).then_inc(join_loaded[k], DMA)
                    sp.dma_start(x1_in[:, k, :], io["x1"][bass.ds(n * T, T), :]).then_inc(join_loaded[k], DMA)
                if t.active("B"):
                    n, k = t.item("B"), t.parity("B")
                    sp.wait_ge(result_steps, t.item("B", 3, 3))
                    sp.dma_start(io["out"][bass.ds(n * T, T), :], result[:, k, :]).then_inc(result_stored[k], DMA)

            JOIN.run(sp, join_turn)
            for k in range(2):
                sp.wait_ge(result_stored[k], NB // 2 * DMA)

        @block.gpsimd
        def _(pool):
            pool.memset(ident[:, :], 0.0).then_inc(zeroed, 1)
            pool.memset(head_mask[:, :], 1.0).then_inc(zeroed, 1)
            pool.memset(pick[:, :, :], 0.0).then_inc(zeroed, 1)
            pool.memset(below[:, :], 1.0).then_inc(zeroed, 1)
            pool.memset(ones[:, :], 1.0).then_inc(zeroed, 1)
            pool.memset(spare_dve[:, :], 0.0).then_inc(zeroed, 1)
            pool.memset(spare_pool[:, :], 0.0).then_inc(zeroed, 1)
            pool.memset(minus_half[:, :], -0.5).then_inc(consts, 1)
            pool.wait_ge(zeroed, 7)
            pool.affine_select(out=ident[:, :], in_=ident[:, :], compare_op=ALU.not_equal, fill=1.0, base=0,
                               pattern=[[-1, P]], channel_multiplier=1).then_inc(consts, 1)
            pool.affine_select(out=head_mask[:, :], in_=head_mask[:, :], compare_op=ALU.is_ge, fill=0.0, base=0,
                               pattern=[[-HD, HC]], channel_multiplier=1).then_inc(zeroed, 1)
            pool.wait_ge(zeroed, 8)
            pool.affine_select(out=head_mask[:, :], in_=head_mask[:, :], compare_op=ALU.is_ge, fill=0.0,
                               base=HD - 1, pattern=[[HD, HC]], channel_multiplier=-1).then_inc(consts, 1)
            pool.affine_select(out=pick[:, :, :], in_=pick[:, :, :], compare_op=ALU.not_equal, fill=-1.0, base=0,
                               pattern=[[-1, H], [0, SC]], channel_multiplier=1).then_inc(consts, 1)
            pool.affine_select(out=below[:, :], in_=below[:, :], compare_op=ALU.is_gt, fill=0.0, base=0,
                               pattern=[[1, P]], channel_multiplier=-1).then_inc(consts, 1)
            pool.iota(count_up[:, :], pattern=[[1, E]], base=0, channel_multiplier=0).then_inc(consts, 1)
            pool.iota(tile_no[:, :], pattern=[[0, 1]], base=0, channel_multiplier=1).then_inc(consts, 1)
            pool.wait_ge(consts, 7)

            def invert(t, s):
                pool.wait_ge(measured[s], t.item(s, 3, 3))
                if t.later(s, 1):
                    pool.wait_ge(normed[s], t.item(s))
                pool.tensor_tensor(inv_std[s][:, :], moments[s][:, 1:2], minus_half[0:T, :],
                                   ALU.pow).then_inc(inverted[s], 1)

            def block_out(t, s, q_step, scores):
                k = t.parity(s)
                pool.wait_ge(taken[q_step], t.item(s, 1, 1))
                if t.later(s, 2):
                    pool.wait_ge(made[scores], t.item(s, ATTENTION.repeats[scores], -ATTENTION.repeats[scores]))
                for c in range(DC):
                    pool.tensor_tensor(q_block[s][:, k, c * HC:(c + 1) * HC, :],
                                       qT[s][:, c, :].unsqueeze(1).to_broadcast([P, HC, T]),
                                       head_mask[:, :].unsqueeze(2).to_broadcast([P, HC, T]),
                                       ALU.mult).then_inc(blocked[s], 1)

            def turn(t):
                for step in t.steps():
                    if step == "N.ln":
                        invert(t, "N")
                    elif step == "A.q":
                        block_out(t, "A", "A.q", "B.s")
                    elif step == "C.qk":
                        block_out(t, "C", "C.qk", "D.s")
                    elif step == "E.norm":
                        invert(t, "E")
                    elif step == "C.v":
                        k = t.parity("C")
                        pool.wait_ge(w_loaded["C"], 14 * DMA)
                        pool.wait_ge(normed["B"], t.item("C", 1, 1))
                        if t.later("C", 2):
                            pool.wait_ge(taken["E.out"], t.item("C", 1, -1))
                        pool.tensor_tensor(y_bias[:, k, :], y[:, k, :], bso[0:T, :], ALU.add).then_inc(y_biased, 1)
                    elif step == "E.send":
                        n, k = t.item("E"), t.parity("E")
                        pool.wait_ge(row_steps, t.item("E", 6, 6))
                        alone(pool, spare_pool)
                        for i in range(TOP):
                            pool.indirect_dma_start(out=io["sent"], out_offset=bass.IndirectOffsetOnAxis(
                                ap=send_row[:, k, i:i + 1], axis=0), in_=xm[:, k, :], in_offset=None).then_inc(sent[k], DMA)
                    elif step == "B.norm":
                        invert(t, "B")

            ATTENTION.run(pool, turn)
            attention_over(pool)
            pool.memset(zero_rows[:, :], 0.0).then_inc(zero_set, 1)

            def expert_turn(t):
                if t.active("D"):
                    n, k = t.item("D"), t.parity("D")
                    pool.wait_ge(ex_taken["D.y"], t.item("D", 1, 1))
                    pool.dma_start(io["expert_out"][bass.ds(n * P, P), :], tile_out[:, k, :]).then_inc(out_stored[k], DMA)

            EXPERTS.run(pool, expert_turn)
            experts_over(pool)
            pool.wait_ge(pos_steps, POS_STEPS)

            def join_turn(t):
                if t.active("A"):
                    n, k = t.item("A"), t.parity("A")
                    if t.later("A", 2):
                        pool.wait_ge(gathered[k], t.dmas("A", 0, TOP))
                        pool.wait_ge(join_steps, t.item("A", 5, -5))
                    pool.tensor_copy(take_row[:, k, :].unsqueeze(2), positions[:, :, bass.ds(n, 1)]).then_inc(rows_copied, 1)
                    pool.wait_ge(rows_copied, t.item("A", 1, 1))
                    alone(pool, spare_pool)
                    for i in range(TOP):
                        pool.indirect_dma_start(out=taken_out[:, k, i, :], out_offset=None, in_=io["expert_out"],
                                                in_offset=bass.IndirectOffsetOnAxis(ap=take_row[:, k, i:i + 1], axis=0)
                                                ).then_inc(gathered[k], DMA)
                if t.active("B"):
                    k = t.parity("B")
                    pool.wait_ge(join_steps, t.item("B", 5, 5))
                    if t.later("B", 2):
                        pool.wait_ge(result_steps, t.item("B", 3, -3))
                    pool.tensor_tensor(join_inv[:, k, :], join_moments[:, k, 1:2], minus_half[0:T, :],
                                       ALU.pow).then_inc(join_inverted, 1)

            JOIN.run(pool, join_turn)

        @block.scalar
        def _(act):
            def drain(t, step, out, in_, bias=None, last=True, first=True):
                if first:
                    act.wait_ge(made[kind_of(step)], t.count(step))
                if bias is None:
                    ins = act.activation(out, in_, ACT.Copy)
                else:
                    ins = act.activation(out, in_, ACT.Identity, bias=bias)
                if last:
                    ins.then_inc(taken[kind_of(step)], 1)

            def exps(t, step, rows):
                act.wait_ge(made[kind_of(step)], t.count(step))
                last = t.before("probs", step)
                if last is not None:
                    pv = last[1].replace(".s", ".pv")
                    act.wait_ge(made[kind_of(pv)], last[0].count(pv))
                act.activation(probs[0:rows, t.buffer("probs", step), :],
                               score[t.buffer("score", step)][0:rows, 0:GT], ACT.Exp,
                               scale=SCALE).then_inc(taken[kind_of(step)], 1)

            def turn(t):
                for step in t.steps():
                    s, kind = step[0], kind_of(step)
                    n1 = lambda: t.item(s)
                    if step == "A.ctxT":
                        if t.later("A", 1):
                            act.wait_ge(made["A.v"], n1())
                        drain(t, step, ctxT[:, :, :], wide[t.buffer("wide", step)][:, :, 0:S])
                    elif step == "A.xT":
                        if t.later("A", 1):
                            act.wait_ge(made["A.q"], n1())
                        drain(t, step, x_normT[:, :, :].rearrange("p c t -> p (c t)"), turned[:, 0:DC * T])
                    elif step == "A.k":
                        if t.later("A", 2):
                            act.wait_ge(made["B.s"], t.item("A", ATTENTION.repeats["B.s"], -ATTENTION.repeats["B.s"]))
                        if t.later("A", 1):
                            act.wait_ge(k16["A"], n1())
                        for c in range(DC):
                            drain(t, step, kT["A"][:, t.parity("A"), c, :],
                                  wide[t.buffer("wide", step)][:, c, 0:S], bxk[:, c:c + 1],
                                  last=c == DC - 1, first=c == 0)
                    elif step == "A.q":
                        if t.later("A", 1):
                            act.wait_ge(blocked["A"], t.item("A", 2))
                        for c in range(DC):
                            drain(t, step, qT["A"][:, c, :], turned[:, c * T:(c + 1) * T], bxq[:, c:c + 1],
                                  last=c == DC - 1, first=c == 0)
                    elif step == "C.yT":
                        if t.later("C", 1):
                            act.wait_ge(made["C.v"], n1())
                        drain(t, step, yT[:, :, :].rearrange("p c t -> p (c t)"), turned[:, 0:DC * T])
                    elif step == "C.qk":
                        if t.later("C", 1):
                            act.wait_ge(blocked["C"], t.item("C", 2))
                        if t.later("C", 2):
                            act.wait_ge(made["D.s"], t.item("C", ATTENTION.repeats["D.s"], -ATTENTION.repeats["D.s"]))
                        b = wide[t.buffer("wide", step)]
                        for c in range(DC):
                            drain(t, step, qT["C"][:, c, :], b[:, 0, c * T:(c + 1) * T], bsq[:, c:c + 1],
                                  last=False, first=c == 0)
                        for c in range(DC):
                            drain(t, step, kT["C"][:, t.parity("C"), c, :], b[:, 1, c * T:(c + 1) * T],
                                  bsk[:, c:c + 1], last=c == DC - 1, first=False)
                    elif step == "E.xT":
                        if t.later("E", 1):
                            act.wait_ge(made["E.gate"], n1())
                        drain(t, step, xmT[:, :, :].rearrange("p c t -> p (c t)"), turned[:, 0:DC * T])
                    elif step == "E.gate":
                        act.wait_ge(gate_steps, t.item("E", 9, 2))
                        act.activation(gate_exp[:, :], logits[:, :], ACT.Exp, bias=minus_max[:, :],
                                       accum_out=gate_sum[:, :]).then_inc(gates_exped, 1)
                    elif kind == "B.s":
                        exps(t, step, SC)
                    elif kind == "D.s":
                        exps(t, step, T)
                    elif step in ("B.pv11", "D.pv3"):
                        o = "B" if s == "B" else "E"
                        act.wait_ge(made[kind], t.count(step))
                        if t.later(s, 1):
                            act.wait_ge(made[o + ".oN"], n1())
                        act.activation(outT[o][:, :], sums[:, 0:GT], ACT.Copy).then_inc(taken[kind], 1)
                    elif kind in ("B.aT", "E.aT"):
                        if t.later(s, 1):
                            act.wait_ge(made[s + ".out"], n1())
                        drain(t, step, attT[s][:, :, :].rearrange("p c t -> p (c t)"), turned[:, 0:DC * T])

            act.wait_ge(w_loaded["B"], 4 * DMA)
            act.activation(tanh_g[:, :], gates[:, :], ACT.Tanh).then_inc(tanh_done, 1)
            act.wait_ge(w_loaded["A"], 6 * DMA)
            act.wait_ge(w_loaded["C"], 14 * DMA)
            ATTENTION.run(act, turn)
            attention_over(act)

            def expert_turn(t):
                if t.active("A"):
                    k = t.parity("A")
                    act.wait_ge(ex_made["A.x"], t.item("A", 1, 1))
                    if t.later("A", 2):
                        act.wait_ge(ex_made["B.h"], t.item("A", 1, -1))
                    act.activation(tile_inT[:, k, :, :].rearrange("p c t -> p (c t)"), rows_bank[k][:, 0:D],
                                   ACT.Copy).then_inc(ex_taken["A.x"], 1)
                if t.active("B"):
                    k = t.parity("B")
                    act.wait_ge(ex_made["B.h"], t.item("B", 1, 1))
                    if t.later("B", 2):
                        act.wait_ge(ex_made["C.hT"], t.item("B", 1, -1))
                    act.activation(hidden[:, k, :], wide[k][:, 0, 0:F], ACT.Copy).then_inc(ex_taken["B.h"], 1)

            EXPERTS.run(act, expert_turn)

        @block.vector
        def _(dve):
            dve.wait_ge(consts, 7)
            for k in range(2):
                dve.memset(values["A"][:, k, :, :, :], 0.0).then_inc(vset, 1)
                dve.memset(values["C"][:, k, :, :, :], 0.0).then_inc(vset, 1)
            dve.wait_ge(vset, 4)
            for k in range(2):
                dve.memset(values["A"][:, k, :, :, HD:HD + 1], 1.0).then_inc(vset, 1)
                dve.memset(values["C"][:, k, :, :, HD:HD + 1], 1.0).then_inc(vset, 1)
            dve.wait_ge(vset, 8)
            dve.wait_ge(w_loaded["A"], 6 * DMA)
            dve.wait_ge(w_loaded["B"], 4 * DMA)
            dve.wait_ge(w_loaded["C"], 14 * DMA)
            dve.wait_ge(tanh_done, 1)

            def measure(t, s, src):
                if t.later(s, 1):
                    dve.wait_ge(normed[s], t.item(s))
                dve.bn_stats(stats[s][:, :], src).then_inc(measured[s], 1)
                dve.wait_ge(measured[s], t.item(s, 3, 1))
                alone(dve, spare_dve)
                dve.bn_aggr(moments[s][:, :], stats[s][:, :]).then_inc(measured[s], 1)
                dve.wait_ge(measured[s], t.item(s, 3, 2))
                dve.tensor_scalar(moments[s][:, 1:2], moments[s][:, 1:2], EPS, None, ALU.add).then_inc(measured[s], 1)

            def normalize(t, s, src, dst):
                dve.wait_ge(inverted[s], t.item(s, 1, 1))
                dve.tensor_scalar(dst, src, moments[s][:, 0:1], inv_std[s][:, :], ALU.subtract,
                                  ALU.mult).then_inc(normed[s], 1)

            def narrow_q(t, s, maxima):
                dve.wait_ge(blocked[s], t.item(s, 2, 2))
                if t.later(s, 1):
                    dve.wait_ge(made[maxima], t.item(s, ATTENTION.repeats[maxima]))
                dve.tensor_copy(q_block16[s][:, :, :], q_block[s][:, t.parity(s), :, :]).then_inc(q16[s], 1)

            def narrow_k(t, s, step, maxima):
                dve.wait_ge(taken[step], t.count(step))
                if t.later(s, 1):
                    dve.wait_ge(made[maxima], t.item(s, ATTENTION.repeats[maxima]))
                dve.tensor_copy(kT16[s][:, :, :], kT[s][:, t.parity(s), :, :]).then_inc(k16[s], 1)

            def average(t, s):
                step = s + ".oN"
                dve.wait_ge(made[step], t.count(step))
                heads = turned[0:T, :].rearrange("t (h w) -> t h w", w=VW)
                if t.later(s, 1):
                    dve.wait_ge(made[s + ".aT"], t.item(s))
                dve.reciprocal(inv_sum[s][:, :].unsqueeze(2), heads[:, :, HD:HD + 1]).then_inc(inv_sums[s], 1)
                dve.wait_ge(inv_sums[s], t.item(s, 1, 1))
                dve.tensor_tensor(att[s][:, :].rearrange("t (h w) -> t h w", w=HD), heads[:, :, 0:HD],
                                  inv_sum[s][:, :].unsqueeze(2).to_broadcast([T, H, HD]),
                                  ALU.mult).then_inc(taken[step], 1)

            def turn(t):
                for step in t.steps():
                    s, kind = step[0], kind_of(step)
                    k = t.parity(s)
                    if step == "N.ln":
                        dve.wait_ge(x_loaded[k], t.dmas("N"))
                        if t.later("N", 1):
                            dve.wait_ge(made["A.xT"], t.item("N"))
                        measure(t, "N", x_in[:, k, :])
                        normalize(t, "N", x_in[:, k, :], x_norm[:, :])
                    elif step == "A.v":
                        dve.wait_ge(made["A.v"], t.count(step))
                        if t.later("A", 2):
                            dve.wait_ge(made["B.pv"], t.item("A", ATTENTION.repeats["B.pv"], -ATTENTION.repeats["B.pv"]))
                        b = wide[t.buffer("wide", step)][0:SC, :, :].rearrange("s b n -> s (b n)")
                        dve.tensor_tensor(values["A"][:, k, :, :, 0:HD],
                                          b[:, 0:NSC * D].rearrange("s (j h w) -> s j h w", j=NSC, w=HD),
                                          bxv[0:SC, :].rearrange("s (h w) -> s h w", w=HD).unsqueeze(1)
                                          .to_broadcast([SC, NSC, H, HD]), ALU.add).then_inc(taken["A.v"], 1)
                    elif step == "A.narrow":
                        narrow_k(t, "A", "A.k", "A.max")
                        narrow_q(t, "A", "A.max")
                    elif step == "C.v":
                        dve.wait_ge(made["C.v"], t.count(step))
                        if t.later("C", 2):
                            dve.wait_ge(made["D.pv"], t.item("C", ATTENTION.repeats["D.pv"], -ATTENTION.repeats["D.pv"]))
                        dve.tensor_tensor(values["C"][:, k, 0, :, 0:HD],
                                          turned[0:T, 0:D].rearrange("s (h w) -> s h w", w=HD),
                                          bsv[0:T, :].rearrange("s (h w) -> s h w", w=HD),
                                          ALU.add).then_inc(taken["C.v"], 1)
                    elif step == "C.narrow":
                        narrow_k(t, "C", "C.qk", "C.max")
                        narrow_q(t, "C", "C.max")
                    elif kind == "A.max":
                        i = index_of(step)
                        dve.wait_ge(made[kind], t.count(step))
                        if i == 0 and t.later("A", 1):
                            dve.wait_ge(made["A.mT"], t.item("A"))
                        dve.tensor_reduce(row_max["A"][:, 2 * i:2 * i + 2],
                                          wide[t.buffer("wide", step)][0:T, :, 0:S], AX_X,
                                          ALU.max).then_inc(taken[kind], 1)
                    elif kind == "C.max":
                        i = index_of(step)
                        dve.wait_ge(made[kind], t.count(step))
                        if i == 0 and t.later("C", 1):
                            dve.wait_ge(made["C.mT"], t.item("C"))
                        dve.tensor_reduce(row_max["C"][:, 8 * i:8 * i + 8].rearrange("t (b h) -> t b h", b=2),
                                          wide[t.buffer("wide", step)][0:T, :, 0:GT]
                                          .rearrange("t b (h s) -> t b h s", s=T), AX_X,
                                          ALU.max).then_inc(taken[kind], 1)
                    elif kind in ("A.mT", "C.mT"):
                        dve.wait_ge(made[kind], t.count(step))
                        if t.later(s, 2):
                            u = "B.s" if s == "A" else "D.s"
                            dve.wait_ge(made[u], t.item(s, ATTENTION.repeats[u], -ATTENTION.repeats[u]))
                        dve.tensor_copy(maxT[s][:, k, :], turned[0:H, 0:T]).then_inc(taken[kind], 1)
                    elif kind in ("B.oN", "E.oN"):
                        average(t, s)
                    elif step == "E.gate":
                        dve.wait_ge(made["E.gate"], t.count(step))
                        if t.later("E", 1):
                            dve.wait_ge(gates_exped, t.item("E"))
                        dve.tensor_tensor(logits[:, :], turned[0:T, 0:E], gate_b[0:T, :], ALU.add).then_inc(taken["E.gate"], 1)
                        dve.wait_ge(taken["E.gate"], t.count(step))
                        alone(dve, spare_dve)
                        dve.max(top_logits[:, :], logits[:, :]).then_inc(gate_steps, 1)
                        dve.wait_ge(gate_steps, t.item("E", 9, 1))
                        dve.tensor_scalar(minus_max[:, :], top_logits[:, 0:1], -1.0, None, ALU.mult).then_inc(gate_steps, 1)
                    elif step == "E.pick":
                        dve.wait_ge(gates_exped, t.item("E", 1, 1))
                        dve.reciprocal(gate_inv[:, :], gate_sum[:, :]).then_inc(gate_steps, 1)
                        dve.wait_ge(gate_steps, t.item("E", 9, 3))
                        dve.tensor_scalar(gate[:, :], gate_exp[:, :], gate_inv[:, :], None, ALU.mult).then_inc(gate_steps, 1)
                        dve.wait_ge(gate_steps, t.item("E", 9, 4))
                        alone(dve, spare_dve)
                        dve.max(top_gate[:, :], gate[:, :]).then_inc(gate_steps, 1)
                        dve.wait_ge(gate_steps, t.item("E", 9, 5))
                        alone(dve, spare_dve)
                        dve.max_index(top_expert[:, :], top_gate[:, :], gate[:, :]).then_inc(gate_steps, 1)
                        dve.wait_ge(gate_steps, t.item("E", 9, 6))
                        if t.later("E", 1):
                            dve.wait_ge(routed, t.item("E"))
                            dve.wait_ge(made["E.rank"], t.item("E"))
                            dve.wait_ge(row_steps, t.item("E", 6))
                        dve.tensor_copy(route[:, TOP:2 * TOP], top_expert[:, 0:TOP]).then_inc(gate_steps, 1)
                        dve.wait_ge(gate_steps, t.item("E", 9, 7))
                        for i in range(TOP):
                            ins = dve.tensor_scalar(chosen[:, i, :], expert_ids[0:T, :], route[:, TOP + i:TOP + i + 1], None,
                                                    ALU.is_equal)
                        ins.then_inc(gate_steps, 1)
                        dve.wait_ge(gate_steps, t.item("E", 9, 8))
                        dve.tensor_tensor(chosen_any[:, :], chosen[:, 0, :], chosen[:, 1, :], ALU.add).then_inc(gate_steps, 1)
                        dve.tensor_copy(route[:, 2 * TOP:3 * TOP], top_gate[:, 0:TOP]).then_inc(row_steps, 1)
                    elif step == "E.rank":
                        dve.wait_ge(made["E.rank"], t.count(step))
                        dve.tensor_tensor(rows_here[:, :], turned[0:T, 0:E], next_row[0:T, :], ALU.add).then_inc(row_steps, 1)
                        dve.wait_ge(row_steps, t.item("E", 6, 2))
                        dve.tensor_tensor(next_row[:, :], turned[:, E:2 * E], next_row[:, :], ALU.add).then_inc(taken["E.rank"], 1)
                        dve.wait_ge(taken["E.rank"], t.count(step))
                        dve.tensor_tensor(rows_pick[:, :, :], chosen[:, :, :], rows_here[:, :].unsqueeze(1)
                                          .to_broadcast([T, TOP, E]), ALU.mult).then_inc(row_steps, 1)
                        dve.wait_ge(row_steps, t.item("E", 6, 3))
                        dve.tensor_reduce(route[:, 0:TOP], rows_pick[:, :, :], AX_X, ALU.add).then_inc(row_steps, 1)
                        dve.wait_ge(row_steps, t.item("E", 6, 4))
                        if t.later("E", 2):
                            dve.wait_ge(sent[k], t.dmas("E", 0, TOP))
                        dve.tensor_copy(routes[:, :, bass.ds(t.item("E"), 1)], route[:, :].unsqueeze(2)).then_inc(routed, 1)
                        dve.tensor_copy(send_row[:, k, :], route[:, 0:TOP]).then_inc(row_steps, 2)
                    elif step == "B.out":
                        dve.wait_ge(made["B.out"], t.count(step))
                        if t.later("B", 1):
                            dve.wait_ge(resid, t.item("B"))
                        dve.tensor_tensor(proj[:, :], turned[0:T, 0:D], bxo[0:T, :], ALU.add).then_inc(taken["B.out"], 1)
                        dve.wait_ge(taken["B.out"], t.count(step))
                        dve.wait_ge(res_loaded[k], t.dmas("B"))
                        if t.later("B", 2):
                            dve.wait_ge(normed["B"], t.item("B", 1, -1))
                        dve.scalar_tensor_tensor(x1[:, k, :], proj[:, :], tanh_g[0:T, 0:1], x_res[:, k, :],
                                                 ALU.mult, ALU.add).then_inc(resid, 1)
                        dve.wait_ge(resid, t.item("B", 1, 1))
                        measure(t, "B", x1[:, k, :])
                        if t.later("B", 2):
                            dve.wait_ge(x1_stored[k], t.dmas("B", 0))
                        dve.tensor_tensor(x1_shift[:, k, :], x1[:, k, :], ln2_shift[0:T, :], ALU.add).then_inc(shifted, 1)
                    elif step == "B.norm":
                        if t.later("B", 2):
                            dve.wait_ge(made["C.yT"], t.item("B", 1, -1))
                            dve.wait_ge(y_biased, t.item("B", 1, -1))
                        normalize(t, "B", x1[:, k, :], y[:, k, :])
                    elif step == "E.out":
                        dve.wait_ge(made["E.out"], t.count(step))
                        dve.wait_ge(y_biased, t.item("E", 1, 1))
                        if t.later("E", 1):
                            dve.wait_ge(normed["E"], t.item("E"))
                        dve.tensor_tensor(r[:, :], turned[0:T, 0:D], y_bias[:, k, :], ALU.add).then_inc(taken["E.out"], 1)
                        dve.wait_ge(taken["E.out"], t.count(step))
                        measure(t, "E", r[:, :])
                    elif step == "E.norm":
                        if t.later("E", 1):
                            dve.wait_ge(gained, t.item("E", 2))
                        normalize(t, "E", r[:, :], r_norm[:, :])
                        dve.wait_ge(normed["E"], t.item("E", 1, 1))
                        dve.tensor_tensor(r_gain[:, :], r_norm[:, :], ln1_g[0:T, :], ALU.mult).then_inc(gained, 1)
                        dve.wait_ge(gained, t.item("E", 2, 1))
                        if t.later("E", 2):
                            dve.wait_ge(xm_stored[k], t.dmas("E", 0))
                            dve.wait_ge(sent[k], t.dmas("E", 0, TOP))
                        dve.tensor_tensor(xm[:, k, :], r_gain[:, :], ln1_b[0:T, :], ALU.add).then_inc(gained, 1)

            dve.wait_ge(consts, 7)
            dve.tensor_copy(expert_ids[:, :], count_up[:, :]).then_inc(vset, 1)
            dve.wait_ge(vset, 9)
            dve.tensor_scalar(region_of[:, :], expert_ids[:, :], float(REGION), None, ALU.mult).then_inc(vset, 1)
            dve.wait_ge(vset, 10)
            dve.tensor_copy(next_row[:, :], region_of[:, :]).then_inc(vset, 1)
            for out, a in ((ln2_gain, ln2_g), (ln2_shift, ln2_b)):
                dve.tensor_scalar(out[:, :], a[:, :], tanh_g[:, 1:2], None, ALU.mult).then_inc(vset, 1)
            dve.wait_ge(vset, 13)
            ATTENTION.run(dve, turn)
            attention_over(dve)

            def step(*waits):
                dve.wait_ge(plan_steps, *waits)

            dve.tensor_copy(next_i[:, :], next_row[:, :]).then_inc(plan_steps, 1)
            dve.tensor_tensor(counts[:, :], next_row[:, :], region_of[:, :], ALU.subtract).then_inc(plan_steps, 1)
            dve.memset(ones_f[:, :], 1.0).then_inc(plan_steps, 1)
            dve.tensor_copy(tile_f[:, :], tile_no[:, :]).then_inc(plan_steps, 1)
            step(4)
            dve.tensor_scalar(tiles_i[:, :], counts[:, :], float(P - 1), None, ALU.add).then_inc(plan_steps, 1)
            step(5)
            dve.tensor_scalar(tiles_i[:, :], tiles_i[:, :], P.bit_length() - 1, None, ALU.arith_shift_right).then_inc(plan_steps, 1)
            step(6)
            dve.tensor_copy(tiles[:, :], tiles_i[:, :]).then_inc(plan_steps, 1)
            step(7)
            dve.tensor_tensor_scan(tiles_end[:, :], ones_f[:, :], tiles[:, :], 0.0, ALU.mult, ALU.add).then_inc(plan_steps, 1)
            step(8)
            dve.tensor_scalar(past[:, :], tiles_end[:, :], tile_f[:, :], None, ALU.is_le).then_inc(plan_steps, 1)
            dve.tensor_tensor(count_step[:, 0:E - 1], counts[:, 1:E], counts[:, 0:E - 1], ALU.subtract).then_inc(plan_steps, 1)
            step(10)
            for i, (w, out) in enumerate(((ones_f, tile_expert), (tiles, tile_base), (count_step, tile_count))):
                dve.tensor_tensor_reduce(junk[:, i, 0:E - 1], past[:, 0:E - 1], w[:, 0:E - 1], 1.0, 0.0, ALU.mult, ALU.add,
                                         out[:, :]).then_inc(plan_steps, 1)
            step(13)
            dve.tensor_tensor(tile_row[:, :], tile_f[:, :], tile_base[:, :], ALU.subtract).then_inc(plan_steps, 1)
            dve.tensor_tensor(tile_rest[:, :], tile_count[:, :], counts[:, 0:1], ALU.add).then_inc(plan_steps, 1)
            step(15)
            dve.scalar_tensor_tensor(tile_row[:, :], tile_row[:, :], float(P), tile_rest[:, :], ALU.mult,
                                     ALU.min).then_inc(plan_steps, 1)
            step(16)
            dve.scalar_tensor_tensor(tile_row[:, :], tile_expert[:, :], float(REGION), tile_row[:, :], ALU.mult,
                                     ALU.add).then_inc(plan_steps, 1)
            dve.wait_ge(table_turned, 1)
            dve.tensor_copy(table[:, :], turned[0:1, 0:2 * NT]).then_inc(table_ready, 1)
            dve.tensor_tensor(to_tiles[:, :], tiles_end[:, :], tiles[:, :], ALU.subtract).then_inc(pos_steps, 1)
            dve.wait_ge(pos_steps, 1)
            dve.scalar_tensor_tensor(to_tiles[:, :], to_tiles[:, :], float(P), region_of[:, :], ALU.mult,
                                     ALU.subtract).then_inc(pos_steps, 1)
            dve.tensor_copy(positions_f[:, 0, :, :], routes[:, 0:TOP, :]).then_inc(pos_steps, 1)
            for e in range(E):
                dve.wait_ge(pos_steps, 3 + 2 * e)
                dve.tensor_scalar(is_expert[:, :, :], routes[:, TOP:2 * TOP, :], float(e), to_tiles[0:T, e:e + 1],
                                  ALU.is_equal, ALU.mult).then_inc(pos_steps, 1)
                dve.wait_ge(pos_steps, 4 + 2 * e)
                dve.tensor_tensor(positions_f[:, e + 1, :, :], positions_f[:, e, :, :], is_expert[:, :, :],
                                  ALU.add).then_inc(pos_steps, 1)
            dve.wait_ge(pos_steps, POS_STEPS - 1)
            dve.tensor_copy(positions[:, :, :], positions_f[:, E, :, :]).then_inc(pos_steps, 1)
            dve.wait_ge(output_b_loaded, DMA)
            dve.wait_ge(moe_loaded, 3 * E * DMA)
            dve.wait_ge(table_ready, 1)

            def expert_turn(t):
                if t.active("C"):
                    n, k = t.item("C"), t.parity("C")
                    e = dve.value_load(table[0:1, bass.ds(n, 1)], min_val=0, max_val=E - 1)
                    dve.wait_ge(ex_made["C.hT"], t.item("C", 1, 1))
                    if t.later("C", 2):
                        dve.wait_ge(ex_made["D.y"], t.item("C", 1, -1))
                    for f in range(FC):
                        ins = dve.tensor_scalar(hiddenT[:, k, f, :], score[k][:, f * P:(f + 1) * P],
                                                hidden_b[:, f, bass.ds(e, 1)], 0.0, ALU.add, ALU.max)
                    ins.then_inc(ex_taken["C.hT"], 1)
                if t.active("D"):
                    n, k = t.item("D"), t.parity("D")
                    e = dve.value_load(table[0:1, bass.ds(n, 1)], min_val=0, max_val=E - 1)
                    dve.wait_ge(ex_made["D.y"], t.item("D", 1, 1))
                    if t.later("D", 2):
                        dve.wait_ge(out_stored[k], t.dmas("D", 0))
                    dve.tensor_tensor(tile_out[:, k, :], wide[k][:, 1, 0:D], output_b[:, bass.ds(e * D, D)],
                                      ALU.add).then_inc(ex_taken["D.y"], 1)

            EXPERTS.run(dve, expert_turn)

            def join_turn(t):
                if t.active("A"):
                    n, k = t.item("A"), t.parity("A")
                    steps = lambda i: t.item("A", 5, i)
                    dve.wait_ge(join_loaded[k], t.dmas("A", 1, 2))
                    dve.wait_ge(gathered[k], t.dmas("A", 1, TOP))
                    if t.later("A", 2):
                        dve.wait_ge(result_steps, t.item("A", 3, -3))
                    if t.later("A", 1):
                        dve.wait_ge(join_steps, t.item("A", 5))
                    dve.scalar_tensor_tensor(added[:, k, 0, :], taken_out[:, k, 0, :], routes[:, 2 * TOP, bass.ds(n, 1)],
                                             xm_in[:, k, :], ALU.mult, ALU.add).then_inc(join_steps, 1)
                    dve.wait_ge(join_steps, steps(1))
                    dve.scalar_tensor_tensor(added[:, k, 1, :], taken_out[:, k, 1, :], routes[:, 2 * TOP + 1, bass.ds(n, 1)],
                                             added[:, k, 0, :], ALU.mult, ALU.add).then_inc(join_steps, 1)
                    dve.wait_ge(join_steps, steps(2))
                    dve.bn_stats(join_stats[:, :], added[:, k, 1, :]).then_inc(join_steps, 1)
                    dve.wait_ge(join_steps, steps(3))
                    alone(dve, spare_dve)
                    dve.bn_aggr(join_moments[:, k, :], join_stats[:, :]).then_inc(join_steps, 1)
                    dve.wait_ge(join_steps, steps(4))
                    dve.tensor_scalar(join_moments[:, k, 1:2], join_moments[:, k, 1:2], EPS, None, ALU.add).then_inc(join_steps, 1)
                if t.active("B"):
                    k = t.parity("B")
                    steps = lambda i: t.item("B", 3, i)
                    dve.wait_ge(join_inverted, t.item("B", 1, 1))
                    if t.later("B", 1):
                        dve.wait_ge(result_steps, t.item("B", 3))
                    dve.tensor_scalar(join_norm[:, :], added[:, k, 1, :], join_moments[:, k, 0:1], join_inv[:, k, :],
                                      ALU.subtract, ALU.mult).then_inc(result_steps, 1)
                    dve.wait_ge(result_steps, steps(1))
                    dve.tensor_tensor(join_gain[:, :], join_norm[:, :], ln2_gain[0:T, :], ALU.mult).then_inc(result_steps, 1)
                    dve.wait_ge(result_steps, steps(2))
                    if t.later("B", 2):
                        dve.wait_ge(result_stored[k], t.dmas("B", 0))
                    dve.tensor_tensor(result[:, k, :], join_gain[:, :], x1_in[:, k, :], ALU.add).then_inc(result_steps, 1)

            JOIN.run(dve, join_turn)

        @block.tensor
        def _(pe):
            def transpose_cols(t, step, src, rows, n):
                for c in range(n):
                    mm = pe.transpose(turned[:, c * rows:(c + 1) * rows], src[:, c * P:(c + 1) * P],
                                      ident[0:rows, 0:rows])
                mm.then_inc(made[kind_of(step)], 1)

            def project(out, w, actT, m):
                for c in range(DC):
                    mm = pe.matmul(out, w[:, c, m * P:(m + 1) * P], actT[:, c, :], start=c == 0, stop=c == DC - 1)
                return mm

            def scores(t, step, a, rows):
                i = index_of(step)
                g, j = i // (NSC if a == "A" else 1), i % (NSC if a == "A" else 1)
                k = t.parity(step[0])
                if i == 0:
                    pe.wait_ge(taken[a + ".mT"], t.item(step[0], 1, 1))
                buffer_free(pe, t, "score", step, taken)
                b = score[t.buffer("score", step)]
                keys = slice(j * rows, (j + 1) * rows)
                pe.matmul(b[0:rows, 0:GT], kT[a][:, k, g * G // HC, keys],
                          q_block[a][:, k, g * G:(g + 1) * G, :], start=True, stop=False, skip_group_check=True)
                for h in range(G):
                    mm = pe.matmul(b[0:rows, h * T:(h + 1) * T], pick[:, g * G + h, 0:rows], maxT[a][:, k, :],
                                   start=False, stop=h == G - 1, skip_group_check=True)
                mm.then_inc(made[kind_of(step)], 1)

            def weigh(t, step, a, rows):
                i, n = index_of(step), (NSC if a == "A" else 1)
                g, j = i // n, i % n
                k = t.parity(step[0])
                of = step.replace(".pv", ".s")
                pe.wait_ge(taken[kind_of(of)], t.count(of))
                if i == 0:
                    if step[0] == "B" and t.base > 0 and t.last().active("D"):
                        pe.wait_ge(taken["D.pv"], t.last().item("D", 1, 1))
                    elif t.later(step[0], 1):
                        pe.wait_ge(taken[step[0] + ".pv"], t.item(step[0]))
                    if step[0] == "D" and t.active("B"):
                        pe.wait_ge(taken["B.pv"], t.item("B", 1, 1))
                b = t.buffer("probs", of)
                for h in range(G):
                    mm = pe.matmul(sums[h * VW:(h + 1) * VW, g * T:(g + 1) * T], values[a][0:rows, k, j, g * G + h, :],
                                   probs[0:rows, b, h * T:(h + 1) * T], start=j == 0, stop=j == n - 1)
                mm.then_inc(made[kind_of(step)], 1)

            def turn(t):
                for step in t.steps():
                    s, kind = step[0], kind_of(step)
                    k = t.parity(s)
                    if kind in ATTENTION.pools["turned"][1]:
                        buffer_free(pe, t, "turned", step, taken)
                    if kind in ATTENTION.pools["wide"][1]:
                        buffer_free(pe, t, "wide", step, taken)
                        b = wide[t.buffer("wide", step)]
                    if step == "A.ctxT":
                        pe.wait_ge(ctx_loaded[k], t.dmas("A"))
                        for c in range(DC):
                            for j in range(NSC):
                                mm = pe.transpose(b[:, c, j * SC:(j + 1) * SC], ctx_in[:, k, j, c * P:(c + 1) * P],
                                                  ident[0:SC, 0:SC])
                        mm.then_inc(made[kind], 1)
                    elif step == "A.xT":
                        pe.wait_ge(normed["N"], t.item("A", 1, 1))
                        transpose_cols(t, step, x_norm, T, DC)
                    elif step == "A.k":
                        pe.wait_ge(taken["A.ctxT"], t.item("A", 1, 1))
                        for m in range(DC):
                            mm = project(b[:, m, 0:S], wxk, ctxT, m)
                        mm.then_inc(made[kind], 1)
                    elif step == "A.q":
                        pe.wait_ge(taken["A.xT"], t.item("A", 1, 1))
                        for m in range(DC):
                            mm = project(turned[:, m * T:(m + 1) * T], wxq, x_normT, m)
                        mm.then_inc(made[kind], 1)
                    elif step == "A.v":
                        for j in range(NSC):
                            for c in range(DC):
                                mm = pe.matmul(b[0:SC, j // 2, (j % 2) * D:(j % 2 + 1) * D],
                                               ctxT[:, c, j * SC:(j + 1) * SC], wxv[:, c, :],
                                               start=c == 0, stop=c == DC - 1)
                        mm.then_inc(made[kind], 1)
                    elif kind == "A.max":
                        i = index_of(step)
                        if i == 0:
                            pe.wait_ge(k16["A"], t.item("A", 1, 1))
                            pe.wait_ge(q16["A"], t.item("A", 1, 1))
                        for h in range(2 * i, 2 * i + 2):
                            mm = pe.matmul(b[0:T, h % 2, 0:S], q_block16["A"][:, h, :], kT16["A"][:, h // HC, :],
                                           start=True, stop=True)
                        mm.then_inc(made[kind], 1)
                    elif kind == "C.max":
                        i = index_of(step)
                        if i == 0:
                            pe.wait_ge(k16["C"], t.item("C", 1, 1))
                            pe.wait_ge(q16["C"], t.item("C", 1, 1))
                        for h in range(8):
                            mm = pe.matmul(b[0:T, h // G, h % G * T:(h % G + 1) * T], q_block16["C"][:, 8 * i + h, :],
                                           kT16["C"][:, (8 * i + h) // HC, :], start=True, stop=True)
                        mm.then_inc(made[kind], 1)
                    elif kind in ("A.mT", "C.mT"):
                        pe.wait_ge(taken[s + ".max"], t.item(s, ATTENTION.repeats[s + ".max"], ATTENTION.repeats[s + ".max"]))
                        pe.transpose(turned[0:H, 0:T], row_max[s][:, :], ident[0:T, 0:T]).then_inc(made[kind], 1)
                    elif kind == "B.s":
                        scores(t, step, "A", SC)
                    elif kind == "D.s":
                        scores(t, step, "C", T)
                    elif kind == "B.pv":
                        weigh(t, step, "A", SC)
                    elif kind == "D.pv":
                        weigh(t, step, "C", T)
                    elif kind in ("B.oN", "E.oN"):
                        pe.wait_ge(taken["B.pv" if s == "B" else "D.pv"], t.item(s, 1, 1))
                        for g in range(NG):
                            mm = pe.transpose(turned[0:T, g * P:(g + 1) * P], outT[s][:, g * T:(g + 1) * T], ident[:, :])
                        mm.then_inc(made[kind], 1)
                    elif kind in ("B.aT", "E.aT"):
                        pe.wait_ge(taken[s + ".oN"], t.item(s, 1, 1))
                        transpose_cols(t, step, att[s], T, DC)
                    elif kind in ("B.out", "E.out"):
                        pe.wait_ge(taken[s + ".aT"], t.item(s, 1, 1))
                        for c in range(DC):
                            mm = pe.matmul(turned[0:T, 0:D], attT[s][:, c, :], (wxo if s == "B" else wso)[:, c, :],
                                           start=c == 0, stop=c == DC - 1)
                        mm.then_inc(made[kind], 1)
                    elif step == "E.xT":
                        pe.wait_ge(gained, t.item("E", 2, 2))
                        transpose_cols(t, step, xm[:, k, :], T, DC)
                    elif step == "E.gate":
                        pe.wait_ge(taken["E.xT"], t.item("E", 1, 1))
                        for c in range(DC):
                            mm = pe.matmul(turned[0:T, 0:E], xmT[:, c, :], gate_w[:, c, :], start=c == 0, stop=c == DC - 1)
                        mm.then_inc(made[kind], 1)
                    elif step == "E.rank":
                        pe.wait_ge(gate_steps, t.item("E", 9, 9))
                        pe.matmul(turned[0:T, 0:E], below[0:T, 0:T], chosen_any[:, :], start=True, stop=True)
                        pe.matmul(turned[:, E:2 * E], ones[0:T, :], chosen_any[:, :], start=True, stop=True,
                                  skip_group_check=True).then_inc(made[kind], 1)
                    elif step == "C.yT":
                        pe.wait_ge(normed["B"], t.item("C", 1, 1))
                        transpose_cols(t, step, y[:, k, :], T, DC)
                    elif step == "C.qk":
                        pe.wait_ge(taken["C.yT"], t.item("C", 1, 1))
                        for m in range(DC):
                            project(b[:, 0, m * T:(m + 1) * T], wsq, yT, m)
                        for m in range(DC):
                            mm = project(b[:, 1, m * T:(m + 1) * T], wsk, yT, m)
                        mm.then_inc(made[kind], 1)
                    elif step == "C.v":
                        for c in range(DC):
                            mm = pe.matmul(turned[0:T, 0:D], yT[:, c, :], wsv[:, c, :], start=c == 0, stop=c == DC - 1)
                        mm.then_inc(made[kind], 1)

            pe.wait_ge(consts, 7)
            pe.wait_ge(vset, 8)
            pe.wait_ge(w_loaded["A"], 6 * DMA)
            pe.wait_ge(w_loaded["B"], 4 * DMA)
            pe.wait_ge(w_loaded["C"], 14 * DMA)
            ATTENTION.run(pe, turn)
            attention_over(pe)
            pe.wait_ge(plan_steps, 17)
            pe.transpose(turned[0:1, 0:NT], tile_expert[0:NT, :], ident[0:NT, 0:NT])
            pe.transpose(turned[0:1, NT:2 * NT], tile_row[0:NT, :], ident[0:NT, 0:NT]).then_inc(table_turned, 1)
            pe.wait_ge(moe_loaded, 3 * E * DMA)
            pe.wait_ge(table_ready, 1)

            def expert_turn(t):
                if t.active("A"):
                    k = t.parity("A")
                    pe.wait_ge(tile_loaded[k], t.dmas("A"))
                    if t.later("A", 2):
                        pe.wait_ge(ex_taken["A.x"], t.item("A", 1, -1))
                    for c in range(DC):
                        mm = pe.transpose(rows_bank[k][:, c * P:(c + 1) * P], tile_in[:, k, c * P:(c + 1) * P], ident[:, :])
                    mm.then_inc(ex_made["A.x"], 1)
                if t.active("B"):
                    n, k = t.item("B"), t.parity("B")
                    e = pe.value_load(table[0:1, bass.ds(n, 1)], min_val=0, max_val=E - 1)
                    pe.wait_ge(ex_taken["A.x"], t.item("B", 1, 1))
                    if t.later("B", 2):
                        pe.wait_ge(ex_taken["B.h"], t.item("B", 1, -1))
                    for c in range(DC):
                        mm = pe.matmul(wide[k][:, 0, 0:F], tile_inT[:, k, c, :], hidden_w[:, c, bass.ds(e * F, F)],
                                       start=c == 0, stop=c == DC - 1)
                    mm.then_inc(ex_made["B.h"], 1)
                if t.active("C"):
                    k = t.parity("C")
                    pe.wait_ge(ex_taken["B.h"], t.item("C", 1, 1))
                    if t.later("C", 2):
                        pe.wait_ge(ex_taken["C.hT"], t.item("C", 1, -1))
                    for f in range(FC):
                        mm = pe.transpose(score[k][:, f * P:(f + 1) * P], hidden[:, k, f * P:(f + 1) * P], ident[:, :])
                    mm.then_inc(ex_made["C.hT"], 1)
                if t.active("D"):
                    n, k = t.item("D"), t.parity("D")
                    e = pe.value_load(table[0:1, bass.ds(n, 1)], min_val=0, max_val=E - 1)
                    pe.wait_ge(ex_taken["C.hT"], t.item("D", 1, 1))
                    if t.later("D", 2):
                        pe.wait_ge(ex_taken["D.y"], t.item("D", 1, -1))
                    for f in range(FC):
                        mm = pe.matmul(wide[k][:, 1, 0:D], hiddenT[:, k, f, :], output_w[:, f, bass.ds(e * D, D)],
                                       start=f == 0, stop=f == FC - 1)
                    mm.then_inc(ex_made["D.y"], 1)

            EXPERTS.run(pe, expert_turn)


WEIGHTS = {"ln1_g": "L0_ffn_ln1_g", "ln1_b": "L0_ffn_ln1_b", "ln2_g": "L0_ffn_ln2_g", "ln2_b": "L0_ffn_ln2_b",
           "gate_w": "L0_ffn_gW", "gate_b": "L0_ffn_gb", "hidden_w": "L0_ffn_W1", "hidden_b": "L0_ffn_b1",
           "output_w": "L0_ffn_W2", "output_b": "L0_ffn_b2", "g_xattn": "g_xattn", "g_ffn": "g_ffn"}


def kernel(**inputs):
    import numpy as np
    import concourse.bacc as bacc
    from concourse.bass_utils import run_bass_kernel_spmd

    arrays = {"x": np.asarray(inputs["x"]).reshape(NB * T, D), "ctx": np.asarray(inputs["ctx_1024"]).reshape(NB * S, D)}
    for name, source in WEIGHTS.items():
        arrays[name] = np.asarray(inputs[source])
    for c in "qkvo":
        arrays["wx" + c] = np.asarray(inputs["L0_xattn_W" + c]).T
        arrays["bx" + c] = np.asarray(inputs["L0_xattn_b" + c])
        arrays["ws" + c] = np.asarray(inputs["L0_ffn_W" + c])
        arrays["bs" + c] = np.asarray(inputs["L0_ffn_b" + c])
    nc = bacc.Bacc("TRN2", target_bir_lowering=False, num_devices=1)
    io, feed = {}, {}
    for name, a in arrays.items():
        feed[f"in_{name}_dram"] = np.ascontiguousarray(a)
        io[name] = nc.dram_tensor(f"in_{name}_dram", a.shape, F32, kind="ExternalInput").ap()
    io["out"] = nc.dram_tensor("out_dram", (NB * T, D), F32, kind="ExternalOutput").ap()
    for name, rows in (("x1", NB * T), ("xm", NB * T), ("sent", E * REGION), ("expert_out", NT * P)):
        io[name] = nc.dram_tensor(f"{name}_dram", (rows, D), F32).ap()
    build(nc, io)
    r = run_bass_kernel_spmd(nc, [feed], core_ids=[0])
    return r.results[0]["out_dram"].reshape(NB, T, D)
```

```python
import concourse.bass as bass
from concourse import mybir
from contextlib import ExitStack

F32 = mybir.dt.float32
I32 = mybir.dt.int32
U32 = mybir.dt.uint32
BF16 = mybir.dt.bfloat16
ALU = mybir.AluOpType
ACT = mybir.ActivationFunctionType
AX_X = mybir.AxisListType.X

NB, T, D = 32, 112, 256
S = 375
H, HD = 16, 16
P = 128
DC = D // P
SC, NSC = 125, 3
HC = P // HD
G = 4
GT = G * T
NG = H // G
VW = 32
BANK = 512
EPS = 1e-5
SCALE = HD ** -0.5
DMA = 16

E = 8
F = 512
FC = F // P
TOP = 2
SENT, AT_GATE, AT_BACK = D + 2, D, D + 1
KEPT, AT_XM, AT_X1 = TOP + 2, TOP, TOP + 1
SPILL = NB * T * KEPT
REGION = NB * T + P
NT = 64
assert NT >= NB * T * TOP // P + E - 1 and NT % 2 == 0


def kind_of(step):
    return step.rstrip("0123456789")


def index_of(step):
    return int(step[len(kind_of(step)):] or 0)


class Plan:

    def __init__(self, items, peeled, lag, order, pools):
        self.items, self.peeled, self.lag, self.order, self.pools = items, peeled, lag, order, pools
        self.turns = items + max(lag.values())
        self.passes = (items - peeled) // 2
        assert (items - peeled) % 2 == 0
        self.repeats = {kind_of(s): sum(kind_of(x) == kind_of(s) for x in order) for s in order}

    def run(self, eng, do):
        for b in range(self.peeled):
            do(Turn(self, b))
        with eng.Fori(0, self.passes) as p:
            for b in range(self.peeled, self.peeled + 2):
                do(Turn(self, b, p))
        for b in range(self.items, self.turns):
            do(Turn(self, b))


class Turn:

    def __init__(self, plan, base, p=None):
        self.plan, self.base, self.p = plan, base, p

    def last(self):
        return Turn(self.plan, self.base - 1, self.p)

    def active(self, stage):
        return 0 <= self.base - self.plan.lag[stage] < self.plan.items

    def steps(self):
        return [s for s in self.plan.order if self.active(s[0])]

    def item(self, stage, times=1, plus=0):
        const = (self.base - self.plan.lag[stage]) * times + plus
        return const if self.p is None else self.p * (2 * times) + const

    def later(self, stage, lag):
        return self.base - self.plan.lag[stage] >= lag

    def parity(self, stage):
        return (self.base - self.plan.lag[stage]) % 2

    def dmas(self, stage, plus=1, each=1):
        const = ((self.base - self.plan.lag[stage]) // 2 + plus) * DMA * each
        return const if self.p is None else self.p * (DMA * each) + const

    def count(self, step, plus=1):
        return self.item(step[0], self.plan.repeats[kind_of(step)], index_of(step) + plus)

    def uses(self, pool, step):
        kinds = self.plan.pools[pool][1]
        uses = [(b, s) for b in range(self.base + 1) for s in Turn(self.plan, b).steps() if kind_of(s) in kinds]
        return uses[:uses.index((self.base, step)) + 1]

    def buffer(self, pool, step):
        return (len(self.uses(pool, step)) - 1) % self.plan.pools[pool][0]

    def before(self, pool, step):
        uses = self.uses(pool, step)
        depth = self.plan.pools[pool][0]
        if len(uses) <= depth:
            return None
        b, s = uses[-1 - depth]
        return Turn(self.plan, b, self.p), s


ATTENTION = Plan(
    NB, 8, {"N": 0, "A": 1, "B": 2, "C": 3, "D": 4, "E": 5},
    ["B.s0", "A.xT", "A.ctxT", "B.s1", "B.pv0", "A.q", "B.s2", "B.pv1", "E.oN", "A.k",
     "B.s3", "B.pv2", "C.yT", "A.v", "B.s4", "B.pv3", "E.aT", "B.s5", "B.pv4", "A.narrow", "E.out",
     "A.max0", "C.qk", "B.s6", "B.pv5", "A.max1", "C.v", "B.s7", "B.pv6", "A.max2", "E.norm",
     "B.s8", "B.pv7", "A.max3", "B.s9", "B.pv8", "E.xT", "A.max4", "N.ln", "C.narrow", "B.s10", "B.pv9",
     "A.max5", "C.max0", "E.gate", "B.s11", "B.pv10", "A.max6", "C.max1", "D.s0", "B.pv11", "A.max7",
     "D.s1", "C.mT", "B.oN", "E.pick", "D.s2", "D.pv0", "B.aT", "A.mT", "E.rank", "D.s3", "D.pv1",
     "B.out", "D.pv2", "B.norm", "E.send", "D.pv3"],
    {"wide": (2, {"A.ctxT", "A.k", "A.v", "A.max", "C.qk", "C.max"}),
     "score": (2, {"B.s", "D.s"}),
     "turned": (1, {"A.xT", "A.q", "A.mT", "B.oN", "B.aT", "B.out", "C.yT", "C.v", "C.mT",
                    "E.oN", "E.aT", "E.out", "E.xT", "E.gate", "E.rank"}),
     "probs": (4, {"B.s", "D.s"})})

EXPERTS = Plan(NT, 6, {"A": 0, "B": 1, "C": 2, "D": 3}, ["A.x", "B.h", "C.hT", "D.y"], {})

JT = NB * T // P
JOIN = Plan(JT, 4, {"A": 0, "B": 1}, ["A.add", "B.norm"], {})


def build(nc, io):
    ctx = ExitStack()
    with ctx:
        def sb(name, shape, dt=F32):
            return ctx.enter_context(nc.sbuf_tensor(name, shape, dt))

        def sem(name):
            return ctx.enter_context(nc.semaphore(name))

        ident = sb("ident", [P, P])
        head_mask = sb("head_mask", [P, HC])
        pick = sb("pick", [H, H, SC], BF16)
        minus_half = sb("minus_half", [P, 1])
        spare_dve, spare_pool = sb("spare_dve", [P, 3]), sb("spare_pool", [P, 3])
        tile_no = sb("tile_no", [P, 1], I32)
        wxq, wxk, wxv, wxo = (sb(n, [P, DC, D]) for n in ("wxq", "wxk", "wxv", "wxo"))
        wsq, wsk, wsv, wso = (sb(n, [P, DC, D]) for n in ("wsq", "wsk", "wsv", "wso"))
        bxq, bxk, bsq, bsk = (sb(n, [P, DC]) for n in ("bxq", "bxk", "bsq", "bsk"))
        bxv, bxo, bsv, bso = (sb(n, [P, D]) for n in ("bxv", "bxo", "bsv", "bso"))
        ln1_g, ln1_b = sb("ln1_g", [P, D]), sb("ln1_b", [P, D])
        ln2_g, ln2_b = sb("ln2_g", [P, D]), sb("ln2_b", [P, D])
        ln2_gain, ln2_shift = sb("ln2_gain", [P, D]), sb("ln2_shift", [P, D])
        gates = sb("gates", [P, 2])
        tanh_g = sb("tanh_g", [P, 2])

        gate_w = sb("gate_w", [P, DC, E])
        gate_b = sb("gate_b", [P, E])
        hidden_w = sb("hidden_w", [P, DC, E * F])
        hidden_b = sb("hidden_b", [P, FC, E])
        output_w = sb("output_w", [P, FC, E * D])
        below = sb("below", [P, P], BF16)
        ones = sb("ones", [P, P], BF16)
        count_up = sb("count_up", [P, E], I32)
        expert_ids = sb("expert_ids", [P, E])
        region_of = sb("region_of", [P, E])
        next_row = sb("next_row", [P, E])
        back_row = sb("back_row", [T, TOP])
        back_i = sb("back_i", [T, TOP], I32)
        spill_row = sb("spill_row", [P, 1])

        wide = [ctx.enter_context(nc.psum_tensor(f"wide{i}", [P, 2, BANK], F32)) for i in range(2)]
        score = [ctx.enter_context(nc.psum_tensor(f"score{i}", [P, BANK], F32)) for i in range(2)]
        turned = ctx.enter_context(nc.psum_tensor("turned", [P, BANK], F32))
        sums = ctx.enter_context(nc.psum_tensor("sums", [P, BANK], F32))

        rows_bank = [turned, sums]

        scope = ExitStack()

        def sb(name, shape, dt=F32):
            return scope.enter_context(nc.sbuf_tensor(name, shape, dt))

        x_in = sb("x_in", [T, 2, D])
        ctx_in = sb("ctx_in", [SC, 2, NSC, D])
        x_res = sb("x_res", [T, 2, D])
        stats = {s: sb("stats_" + s, [T, 6]) for s in "NBE"}
        moments = {s: sb("moments_" + s, [T, 2]) for s in "NBE"}
        inv_std = {s: sb("inv_std_" + s, [T, 1]) for s in "NBE"}
        x_norm = sb("x_norm", [T, D])
        x_normT = sb("x_normT", [P, DC, T])
        ctxT = sb("ctxT", [P, DC, S])
        qT = {s: sb("qT_" + s, [P, DC, T]) for s in "AC"}
        q_block = {s: sb("q_block_" + s, [P, 2, H, T]) for s in "AC"}
        q_block16 = {s: sb("q_block16_" + s, [P, H, T], BF16) for s in "AC"}
        kT = {"A": sb("kT_A", [P, 2, DC, S]), "C": sb("kT_C", [P, 2, DC, T])}
        kT16 = {"A": sb("kT16_A", [P, DC, S], BF16), "C": sb("kT16_C", [P, DC, T], BF16)}
        values = {"A": sb("values_A", [SC, 2, NSC, H, VW]), "C": sb("values_C", [T, 2, 1, H, VW])}
        row_max = {s: sb("row_max_" + s, [T, H]) for s in "AC"}
        maxT = {s: sb("maxT_" + s, [H, 2, T], BF16) for s in "AC"}
        probs = sb("probs", [SC, ATTENTION.pools["probs"][0], GT])
        outT = {s: sb("outT_" + s, [P, GT]) for s in "BE"}
        inv_sum = {s: sb("inv_sum_" + s, [T, H]) for s in "BE"}
        att = {s: sb("att_" + s, [T, D]) for s in "BE"}
        attT = {s: sb("attT_" + s, [P, DC, T]) for s in "BE"}
        proj = sb("proj", [T, D])
        x1 = sb("x1", [T, 2, D])
        x1_shift = sb("x1_shift", [T, 2, D])
        y = sb("y", [T, 2, D])
        yT = sb("yT", [P, DC, T])
        y_bias = sb("y_bias", [T, 2, D])
        r = sb("r", [T, D])
        r_gain = sb("r_gain", [T, D])
        xm = sb("xm", [T, 2, TOP, SENT])

        xmT = sb("xmT", [P, DC, T])
        logits = sb("logits", [T, E])
        top_logits = sb("top_logits", [T, 8])
        minus_max = sb("minus_max", [T, 1])
        gate_exp = sb("gate_exp", [T, E])
        gate_sum = sb("gate_sum", [T, 1])
        gate_inv = sb("gate_inv", [T, 1])
        gate = sb("gate", [T, E])
        top_gate = sb("top_gate", [T, 8])
        top_expert = sb("top_expert", [T, 8], U32)
        chosen = sb("chosen", [T, TOP, E])
        chosen_any = sb("chosen_any", [T, E], BF16)
        rows_here = sb("rows_here", [T, E])
        rows_pick = sb("rows_pick", [T, TOP, E])
        route = sb("route", [T, 2 * TOP])
        send_row = sb("send_row", [T, 2, TOP], U32)

        scope.close()
        scope = ctx.enter_context(ExitStack())
        zero_rows = sb("zero_rows", [P, SENT])
        output_b = sb("output_b", [P, E * D])
        counts = sb("counts", [P, E])
        tiles_i = sb("tiles_i", [P, E], I32)
        tiles = sb("tiles", [P, E])
        tiles_end = sb("tiles_end", [P, E])
        ones_f = sb("ones_f", [P, E])
        next_i = sb("next_i", [P, E], I32)
        tile_f = sb("tile_f", [P, 1])
        past = sb("past", [P, E])
        count_step = sb("count_step", [P, E])
        junk = sb("junk", [P, 3, E])
        tile_expert, tile_base, tile_count = (sb(n, [P, 1]) for n in ("tile_expert", "tile_base", "tile_count"))
        tile_row, tile_rest = sb("tile_row", [P, 1]), sb("tile_rest", [P, 1])
        table = sb("table", [1, 2 * NT], I32)
        tile_in = sb("tile_in", [P, 2, SENT])
        tile_meta = sb("tile_meta", [P, 2, 2])
        tile_ends = sb("tile_ends", [P, 2, 2])
        tile_inT = sb("tile_inT", [P, 2, DC, P])
        hidden = sb("hidden", [P, 2, F])
        hiddenT = sb("hiddenT", [P, 2, FC, P])
        tile_sum = sb("tile_sum", [P, 2, D])
        tile_out = sb("tile_out", [P, 2, D])
        is_spill = sb("is_spill", [P, 1])
        take_back = sb("take_back", [P, 2, 1], U32)
        join_in = sb("join_in", [P, 2, AT_X1, D])
        x1_in = sb("x1_in", [P, 2, D])
        added = sb("added", [P, 2, TOP, D])
        join_stats = sb("join_stats", [P, 6])
        join_moments = sb("join_moments", [P, 2, 2])
        join_inv = sb("join_inv", [P, 2, 1])
        join_gain = sb("join_gain", [P, D])
        result = sb("result", [P, 2, D])

        made = {k: sem("made_" + k.replace(".", "_")) for k in ATTENTION.repeats}
        taken = {k: sem("taken_" + k.replace(".", "_")) for k in ATTENTION.repeats}
        gates_exped = sem("gates_exped")
        gate_steps = sem("gate_steps")
        row_steps = sem("row_steps")
        sent = [sem(f"sent{i}") for i in range(2)]
        moe_loaded = sem("moe_loaded")
        output_b_loaded = sem("output_b_loaded")
        plan_steps = sem("plan_steps")
        zero_set = sem("zero_set")
        tails_zeroed = sem("tails_zeroed")
        xm_copied = sem("xm_copied")
        back_moved = sem("back_moved")
        spill_steps = sem("spill_steps")
        scatter_begun = sem("scatter_begun")
        tile_done = sem("tile_done")
        tile_kept = sem("tile_kept")
        tile_moved = sem("tile_moved")
        table_turned = sem("table_turned")
        table_ready = sem("table_ready")
        tile_loaded = [sem(f"tile_loaded{i}") for i in range(2)]
        out_stored = [sem(f"out_stored{i}") for i in range(2)]
        ex_made = {k: sem("ex_made_" + k.replace(".", "_")) for k in EXPERTS.repeats}
        ex_taken = {k: sem("ex_taken_" + k.replace(".", "_")) for k in EXPERTS.repeats}
        x1_loaded = [sem(f"x1_loaded{i}") for i in range(2)]
        join_loaded = [sem(f"join_loaded{i}") for i in range(2)]
        result_stored = [sem(f"result_stored{i}") for i in range(2)]
        join_steps = sem("join_steps")
        join_inverted = sem("join_inverted")
        result_steps = sem("result_steps")
        w_loaded = {n: sem("w_loaded_" + n) for n in ("A", "B", "C")}
        x_loaded = [sem(f"x_loaded{i}") for i in range(2)]
        ctx_loaded = [sem(f"ctx_loaded{i}") for i in range(2)]
        res_loaded = [sem(f"res_loaded{i}") for i in range(2)]
        x1_stored = [sem(f"x1_stored{i}") for i in range(2)]
        xm_stored = [sem(f"xm_stored{i}") for i in range(2)]
        zeroed = sem("zeroed")
        vset = sem("vset")
        consts = sem("consts")
        tanh_done = sem("tanh_done")
        measured = {s: sem("measured_" + s) for s in "NBE"}
        inverted = {s: sem("inverted_" + s) for s in "NBE"}
        normed = {s: sem("normed_" + s) for s in "NBE"}
        blocked = {s: sem("blocked_" + s) for s in "AC"}
        q16 = {s: sem("q16_" + s) for s in "AC"}
        k16 = {s: sem("k16_" + s) for s in "AC"}
        inv_sums = {s: sem("inv_sums_" + s) for s in "BE"}
        averaged = {s: sem("averaged_" + s) for s in "BE"}
        resid = sem("resid")
        y_biased = sem("y_biased")
        shifted = sem("shifted")
        gained = sem("gained")

        def buffer_free(eng, t, pool, step, by):
            last = t.before(pool, step)
            if last is not None:
                eng.wait_ge(by[kind_of(last[1])], last[0].count(last[1]))

        def alone(eng, spare):
            return eng.tensor_tensor(spare[0:1, 0:1], spare[0:1, 1:2], spare[0:1, 2:3], ALU.add)

        kept = io["kept"][0:SPILL, :].rearrange("(n r) d -> n r d", r=KEPT)

        def kept_rows(n, row):
            return kept[bass.ds(n * T, T), row, :]

        def attention_over(eng):
            for k in range(2):
                eng.wait_ge(sent[k], NB // 2 * DMA * TOP)

        def experts_over(eng):
            for k in range(2):
                eng.wait_ge(out_stored[k], NT // 2 * DMA)

        block = ctx.enter_context(nc.Block())

        @block.sync
        def _(sp):
            def square(w, a):
                return sp.dma_start(w[:, :, :], a.rearrange("(c p) n -> p c n", p=P))

            def column(b, a):
                return sp.dma_start(b[:, :], a.rearrange("(c p) -> p c", p=P), allow_slow_non_contiguous=True)

            def row(b, a):
                return sp.dma_start(b[:, :], a.partition_broadcast(P))

            def load(t):
                n, k = t.item("N"), t.parity("N")
                if t.later("N", 2):
                    sp.wait_ge(normed["N"], t.item("N", 1, -1))
                sp.dma_start(x_in[:, k, :], io["x"][bass.ds(n * T, T), :]).then_inc(x_loaded[k], DMA)
                if t.later("N", 2):
                    sp.wait_ge(made["A.ctxT"], t.item("N", 1, -1))
                sp.dma_start(ctx_in[:, k, :, :],
                             io["ctx"][bass.ds(n * S, S), :].rearrange("(j p) d -> p j d", p=SC)
                             ).then_inc(ctx_loaded[k], DMA)

            def turn(t):
                if t.active("N"):
                    load(t)
                if t.base == 3:
                    for e in range(E):
                        sp.dma_start(hidden_w[:, :, e * F:(e + 1) * F],
                                     io["hidden_w"][e].rearrange("(c p) f -> p c f", p=P)).then_inc(moe_loaded, DMA)
                        sp.dma_start(output_w[:, :, e * D:(e + 1) * D],
                                     io["output_w"][e].rearrange("(c p) d -> p c d", p=P)).then_inc(moe_loaded, DMA)
                        sp.dma_start(hidden_b[:, :, e:e + 1], io["hidden_b"][e].rearrange("(c p one) -> p c one", p=P, one=1),
                                     allow_slow_non_contiguous=True).then_inc(moe_loaded, DMA)
                if t.active("B"):
                    n, k = t.item("B"), t.parity("B")
                    if t.later("B", 2):
                        sp.wait_ge(resid, t.item("B", 1, -1))
                    sp.dma_start(x_res[:, k, :], io["x"][bass.ds(n * T, T), :]).then_inc(res_loaded[k], DMA)
                if t.active("E"):
                    n, k = t.item("E"), t.parity("E")
                    sp.wait_ge(gained, t.item("E", 2, 2))
                    sp.dma_start(kept_rows(n, AT_XM), xm[:, k, 0, 0:D]).then_inc(xm_stored[k], DMA)
                if t.active("B"):
                    n, k = t.item("B"), t.parity("B")
                    sp.wait_ge(shifted, t.item("B", 1, 1))
                    sp.dma_start(kept_rows(n, AT_X1), x1_shift[:, k, :]).then_inc(x1_stored[k], DMA)

            square(wxk, io["wxk"]).then_inc(w_loaded["A"], DMA)
            square(wxq, io["wxq"]).then_inc(w_loaded["A"], DMA)
            square(wxv, io["wxv"]).then_inc(w_loaded["A"], DMA)
            column(bxk, io["bxk"]).then_inc(w_loaded["A"], DMA)
            column(bxq, io["bxq"]).then_inc(w_loaded["A"], DMA)
            row(bxv, io["bxv"]).then_inc(w_loaded["A"], DMA)
            square(wxo, io["wxo"]).then_inc(w_loaded["B"], DMA)
            row(bxo, io["bxo"]).then_inc(w_loaded["B"], DMA)
            sp.dma_start(gates[:, 0:1], io["g_xattn"].partition_broadcast(P)).then_inc(w_loaded["B"], DMA)
            sp.dma_start(gates[:, 1:2], io["g_ffn"].partition_broadcast(P)).then_inc(w_loaded["B"], DMA)
            for w, a in ((wsq, "wsq"), (wsk, "wsk"), (wsv, "wsv"), (wso, "wso")):
                square(w, io[a]).then_inc(w_loaded["C"], DMA)
            for b, a in ((bsq, "bsq"), (bsk, "bsk")):
                column(b, io[a]).then_inc(w_loaded["C"], DMA)
            for b, a in ((bsv, "bsv"), (bso, "bso"), (gate_b, "gate_b"), (ln1_g, "ln1_g"), (ln1_b, "ln1_b"), (ln2_g, "ln2_g"),
                         (ln2_b, "ln2_b")):
                row(b, io[a]).then_inc(w_loaded["C"], DMA)
            sp.dma_start(gate_w[:, :, :], io["gate_w"].rearrange("(c p) e -> p c e", p=P)).then_inc(w_loaded["C"], DMA)
            ATTENTION.run(sp, turn)
            attention_over(sp)
            sp.dma_start(output_b[:, :], io["output_b"].rearrange("e d -> (e d)").partition_broadcast(P)
                         ).then_inc(output_b_loaded, DMA)
            sp.wait_ge(zero_set, 1)
            sp.wait_ge(plan_steps, 1)
            for e in range(E):
                row_no = sp.value_load(next_i[0:1, e:e + 1], min_val=e * REGION, max_val=e * REGION + NB * T)
                sp.dma_start(io["sent"][bass.ds(row_no, P), :], zero_rows[:, :]).then_inc(tails_zeroed, DMA)
            sp.wait_ge(tails_zeroed, E * DMA)
            sp.wait_ge(table_ready, 1)

            def expert_turn(t):
                if t.active("A"):
                    n, k = t.item("A"), t.parity("A")
                    first = sp.value_load(table[0:1, bass.ds(n + NT, 1)], min_val=0, max_val=E * REGION - P)
                    if t.later("A", 2):
                        sp.wait_ge(ex_made["A.x"], t.item("A", 1, -1))
                        sp.wait_ge(tile_kept, t.item("A", 1, -1))
                    sp.dma_start(tile_in[:, k, :], io["sent"][bass.ds(first, P), :]).then_inc(tile_loaded[k], DMA)

            EXPERTS.run(sp, expert_turn)
            experts_over(sp)
            for k in range(2):
                sp.wait_ge(x1_stored[k], NB // 2 * DMA)
                sp.wait_ge(xm_stored[k], NB // 2 * DMA)

            def join_turn(t):
                if t.active("A"):
                    n, k = t.item("A"), t.parity("A")
                    if t.later("A", 2):
                        sp.wait_ge(join_steps, t.item("A", 5, -8))
                    sp.dma_start(join_in[:, k, :, :], kept[bass.ds(n * P, P), 0:AT_X1, :]).then_inc(join_loaded[k], DMA)
                    if t.later("A", 2):
                        sp.wait_ge(result_steps, t.item("A", 2, -2))
                    sp.dma_start(x1_in[:, k, :], kept[bass.ds(n * P, P), AT_X1, :]).then_inc(x1_loaded[k], DMA)

            JOIN.run(sp, join_turn)

        @block.gpsimd
        def _(pool):
            pool.memset(ident[:, :], 0.0).then_inc(zeroed, 1)
            pool.memset(head_mask[:, :], 1.0).then_inc(zeroed, 1)
            pool.memset(pick[:, :, :], 0.0).then_inc(zeroed, 1)
            pool.memset(below[:, :], 1.0).then_inc(zeroed, 1)
            pool.memset(ones[:, :], 1.0).then_inc(zeroed, 1)
            pool.memset(spare_dve[:, :], 0.0).then_inc(zeroed, 1)
            pool.memset(spare_pool[:, :], 0.0).then_inc(zeroed, 1)
            pool.memset(minus_half[:, :], -0.5).then_inc(consts, 1)
            pool.wait_ge(zeroed, 7)
            pool.affine_select(out=ident[:, :], in_=ident[:, :], compare_op=ALU.not_equal, fill=1.0, base=0,
                               pattern=[[-1, P]], channel_multiplier=1).then_inc(consts, 1)
            pool.affine_select(out=head_mask[:, :], in_=head_mask[:, :], compare_op=ALU.is_ge, fill=0.0, base=0,
                               pattern=[[-HD, HC]], channel_multiplier=1).then_inc(zeroed, 1)
            pool.wait_ge(zeroed, 8)
            pool.affine_select(out=head_mask[:, :], in_=head_mask[:, :], compare_op=ALU.is_ge, fill=0.0,
                               base=HD - 1, pattern=[[HD, HC]], channel_multiplier=-1).then_inc(consts, 1)
            pool.affine_select(out=pick[:, :, :], in_=pick[:, :, :], compare_op=ALU.not_equal, fill=-1.0, base=0,
                               pattern=[[-1, H], [0, SC]], channel_multiplier=1).then_inc(consts, 1)
            pool.affine_select(out=below[:, :], in_=below[:, :], compare_op=ALU.is_gt, fill=0.0, base=0,
                               pattern=[[1, P]], channel_multiplier=-1).then_inc(consts, 1)
            pool.iota(count_up[:, :], pattern=[[1, E]], base=0, channel_multiplier=0).then_inc(consts, 1)
            pool.iota(tile_no[:, :], pattern=[[0, 1]], base=0, channel_multiplier=1).then_inc(consts, 1)
            pool.iota(back_i[:, :], pattern=[[1, TOP]], base=1, channel_multiplier=KEPT).then_inc(consts, 1)
            pool.wait_ge(consts, 8)

            def invert(t, s):
                pool.wait_ge(measured[s], t.item(s, 3, 3))
                if t.later(s, 1):
                    if s == "E":
                        pool.wait_ge(gained, t.item(s, 2))
                    else:
                        pool.wait_ge(normed[s], t.item(s))
                pool.tensor_tensor(inv_std[s][:, :], moments[s][:, 1:2], minus_half[0:T, :],
                                   ALU.pow).then_inc(inverted[s], 1)

            def block_out(t, s, q_step, scores):
                k = t.parity(s)
                pool.wait_ge(taken[q_step], t.item(s, 1, 1))
                if t.later(s, 2):
                    pool.wait_ge(made[scores], t.item(s, ATTENTION.repeats[scores], -ATTENTION.repeats[scores]))
                for c in range(DC):
                    pool.tensor_tensor(q_block[s][:, k, c * HC:(c + 1) * HC, :],
                                       qT[s][:, c, :].unsqueeze(1).to_broadcast([P, HC, T]),
                                       head_mask[:, :].unsqueeze(2).to_broadcast([P, HC, T]),
                                       ALU.mult).then_inc(blocked[s], 1)

            def turn(t):
                for step in t.steps():
                    if step == "N.ln":
                        invert(t, "N")
                    elif step == "A.q":
                        block_out(t, "A", "A.q", "B.s")
                    elif step == "C.qk":
                        block_out(t, "C", "C.qk", "D.s")
                    elif step == "E.norm":
                        invert(t, "E")
                    elif step == "C.v":
                        k = t.parity("C")
                        pool.wait_ge(w_loaded["C"], 14 * DMA)
                        pool.wait_ge(normed["B"], t.item("C", 1, 1))
                        if t.later("C", 2):
                            pool.wait_ge(taken["E.out"], t.item("C", 1, -1))
                        pool.tensor_tensor(y_bias[:, k, :], y[:, k, :], bso[0:T, :], ALU.add).then_inc(y_biased, 1)
                    elif step == "E.send":
                        n, k = t.item("E"), t.parity("E")
                        pool.wait_ge(xm_copied, t.item("E", 1, 1))
                        pool.wait_ge(row_steps, t.item("E", 6, 6))
                        alone(pool, spare_pool)
                        for i in range(TOP):
                            pool.indirect_dma_start(out=io["sent"], out_offset=bass.IndirectOffsetOnAxis(
                                ap=send_row[:, k, i:i + 1], axis=0), in_=xm[:, k, i, :], in_offset=None).then_inc(sent[k], DMA)
                    elif step == "B.norm":
                        invert(t, "B")

            ATTENTION.run(pool, turn)
            attention_over(pool)
            pool.memset(zero_rows[:, :], 0.0).then_inc(zero_set, 1)

            def expert_turn(t):
                if t.active("D"):
                    k = t.parity("D")
                    if t.later("D", 1):
                        pool.wait_ge(scatter_begun, t.item("D"))
                    pool.wait_ge(spill_steps, t.item("D", 3, 3))
                    pool.wait_ge(tile_done, t.item("D", 1, 1))
                    alone(pool, spare_pool).then_inc(scatter_begun, 1)
                    pool.indirect_dma_start(out=io["kept"], out_offset=bass.IndirectOffsetOnAxis(
                        ap=take_back[:, k, :], axis=0), in_=tile_out[:, k, :], in_offset=None).then_inc(out_stored[k], DMA)

            EXPERTS.run(pool, expert_turn)

            def join_turn(t):
                if t.active("B"):
                    k = t.parity("B")
                    pool.wait_ge(join_steps, t.item("B", 5, 5))
                    if t.later("B", 2):
                        pool.wait_ge(result_steps, t.item("B", 2, -2))
                    pool.tensor_tensor(join_inv[:, k, :], join_moments[:, k, 1:2], minus_half[:, :],
                                       ALU.pow).then_inc(join_inverted, 1)

            JOIN.run(pool, join_turn)

        @block.scalar
        def _(act):
            def drain(t, step, out, in_, bias=None, last=True, first=True):
                if first:
                    act.wait_ge(made[kind_of(step)], t.count(step))
                if bias is None:
                    ins = act.activation(out, in_, ACT.Copy)
                else:
                    ins = act.activation(out, in_, ACT.Identity, bias=bias)
                if last:
                    ins.then_inc(taken[kind_of(step)], 1)

            def exps(t, step, rows):
                act.wait_ge(made[kind_of(step)], t.count(step))
                last = t.before("probs", step)
                if last is not None:
                    pv = last[1].replace(".s", ".pv")
                    act.wait_ge(made[kind_of(pv)], last[0].count(pv))
                act.activation(probs[0:rows, t.buffer("probs", step), :],
                               score[t.buffer("score", step)][0:rows, 0:GT], ACT.Exp,
                               scale=SCALE).then_inc(taken[kind_of(step)], 1)

            def turn(t):
                for step in t.steps():
                    s, kind = step[0], kind_of(step)
                    k = t.parity(s)
                    n1 = lambda: t.item(s)
                    if step == "A.ctxT":
                        if t.later("A", 1):
                            act.wait_ge(made["A.v"], n1())
                        drain(t, step, ctxT[:, :, :], wide[t.buffer("wide", step)][:, :, 0:S])
                    elif step == "A.xT":
                        if t.later("A", 1):
                            act.wait_ge(made["A.q"], n1())
                        drain(t, step, x_normT[:, :, :].rearrange("p c t -> p (c t)"), turned[:, 0:DC * T])
                    elif step == "A.k":
                        if t.later("A", 2):
                            act.wait_ge(made["B.s"], t.item("A", ATTENTION.repeats["B.s"], -ATTENTION.repeats["B.s"]))
                        if t.later("A", 1):
                            act.wait_ge(k16["A"], n1())
                        for c in range(DC):
                            drain(t, step, kT["A"][:, t.parity("A"), c, :],
                                  wide[t.buffer("wide", step)][:, c, 0:S], bxk[:, c:c + 1],
                                  last=c == DC - 1, first=c == 0)
                    elif step == "A.q":
                        if t.later("A", 1):
                            act.wait_ge(blocked["A"], t.item("A", 2))
                        for c in range(DC):
                            drain(t, step, qT["A"][:, c, :], turned[:, c * T:(c + 1) * T], bxq[:, c:c + 1],
                                  last=c == DC - 1, first=c == 0)
                    elif step == "C.yT":
                        if t.later("C", 1):
                            act.wait_ge(made["C.v"], n1())
                        drain(t, step, yT[:, :, :].rearrange("p c t -> p (c t)"), turned[:, 0:DC * T])
                    elif step == "C.qk":
                        if t.later("C", 1):
                            act.wait_ge(blocked["C"], t.item("C", 2))
                        if t.later("C", 2):
                            act.wait_ge(made["D.s"], t.item("C", ATTENTION.repeats["D.s"], -ATTENTION.repeats["D.s"]))
                        b = wide[t.buffer("wide", step)]
                        for c in range(DC):
                            drain(t, step, qT["C"][:, c, :], b[:, 0, c * T:(c + 1) * T], bsq[:, c:c + 1],
                                  last=False, first=c == 0)
                        for c in range(DC):
                            drain(t, step, kT["C"][:, t.parity("C"), c, :], b[:, 1, c * T:(c + 1) * T],
                                  bsk[:, c:c + 1], last=c == DC - 1, first=False)
                    elif step == "E.xT":
                        act.wait_ge(gained, t.item("E", 2, 2))
                        if t.later("E", 2):
                            act.wait_ge(sent[k], t.dmas("E", 0, TOP))
                        act.activation(xm[:, k, 1, 0:D], xm[:, k, 0, 0:D], ACT.Copy).then_inc(xm_copied, 1)
                        if t.later("E", 1):
                            act.wait_ge(made["E.gate"], n1())
                        drain(t, step, xmT[:, :, :].rearrange("p c t -> p (c t)"), turned[:, 0:DC * T])
                    elif step == "E.gate":
                        act.wait_ge(gate_steps, t.item("E", 9, 2))
                        act.activation(gate_exp[:, :], logits[:, :], ACT.Exp, bias=minus_max[:, :],
                                       accum_out=gate_sum[:, :]).then_inc(gates_exped, 1)
                    elif kind == "B.s":
                        exps(t, step, SC)
                    elif kind == "D.s":
                        exps(t, step, T)
                    elif step in ("B.pv11", "D.pv3"):
                        o = "B" if s == "B" else "E"
                        act.wait_ge(made[kind], t.count(step))
                        if t.later(s, 1):
                            act.wait_ge(made[o + ".oN"], n1())
                        act.activation(outT[o][:, :], sums[:, 0:GT], ACT.Copy).then_inc(taken[kind], 1)
                    elif kind in ("B.aT", "E.aT"):
                        if t.later(s, 1):
                            act.wait_ge(made[s + ".out"], n1())
                        drain(t, step, attT[s][:, :, :].rearrange("p c t -> p (c t)"), turned[:, 0:DC * T])

            act.wait_ge(w_loaded["B"], 4 * DMA)
            act.activation(tanh_g[:, :], gates[:, :], ACT.Tanh).then_inc(tanh_done, 1)
            act.wait_ge(w_loaded["A"], 6 * DMA)
            act.wait_ge(w_loaded["C"], 14 * DMA)
            ATTENTION.run(act, turn)
            attention_over(act)

            def expert_turn(t):
                if t.active("A"):
                    k = t.parity("A")
                    act.wait_ge(ex_made["A.x"], t.item("A", 1, 1))
                    if t.later("A", 2):
                        act.wait_ge(ex_made["B.h"], t.item("A", 1, -1))
                    act.activation(tile_inT[:, k, :, :].rearrange("p c t -> p (c t)"), rows_bank[k][:, 0:D],
                                   ACT.Copy).then_inc(ex_taken["A.x"], 1)
                if t.active("B"):
                    k = t.parity("B")
                    act.wait_ge(ex_made["B.h"], t.item("B", 1, 1))
                    if t.later("B", 2):
                        act.wait_ge(ex_made["C.hT"], t.item("B", 1, -1))
                    act.activation(hidden[:, k, :], wide[k][:, 0, 0:F], ACT.Copy).then_inc(ex_taken["B.h"], 1)
                if t.active("D"):
                    k = t.parity("D")
                    act.wait_ge(tile_moved, t.item("D", 1, 1))
                    act.wait_ge(ex_taken["D.y"], t.item("D", 1, 1))
                    if t.later("D", 2):
                        act.wait_ge(out_stored[k], t.dmas("D", 0))
                    act.activation(tile_out[:, k, :], tile_sum[:, k, :], ACT.Copy, scale=tile_ends[:, k, 0:1]).then_inc(tile_done, 1)

            EXPERTS.run(act, expert_turn)

            def join_turn(t):
                if t.active("B"):
                    n, k = t.item("B"), t.parity("B")
                    act.wait_ge(result_steps, t.item("B", 2, 2))
                    act.dma_start(io["out"][bass.ds(n * P, P), :], result[:, k, :]).then_inc(result_stored[k], DMA)

            JOIN.run(act, join_turn)
            for k in range(2):
                act.wait_ge(result_stored[k], JT // 2 * DMA)

        @block.vector
        def _(dve):
            dve.wait_ge(consts, 8)
            for k in range(2):
                dve.memset(values["A"][:, k, :, :, :], 0.0).then_inc(vset, 1)
                dve.memset(values["C"][:, k, :, :, :], 0.0).then_inc(vset, 1)
            dve.wait_ge(vset, 4)
            for k in range(2):
                dve.memset(values["A"][:, k, :, :, HD:HD + 1], 1.0).then_inc(vset, 1)
                dve.memset(values["C"][:, k, :, :, HD:HD + 1], 1.0).then_inc(vset, 1)
            dve.wait_ge(vset, 8)
            dve.wait_ge(w_loaded["A"], 6 * DMA)
            dve.wait_ge(w_loaded["B"], 4 * DMA)
            dve.wait_ge(w_loaded["C"], 14 * DMA)
            dve.wait_ge(tanh_done, 1)

            def measure(t, s, src):
                if t.later(s, 1):
                    if s == "E":
                        dve.wait_ge(gained, t.item(s, 2))
                    else:
                        dve.wait_ge(normed[s], t.item(s))
                dve.bn_stats(stats[s][:, :], src).then_inc(measured[s], 1)
                dve.wait_ge(measured[s], t.item(s, 3, 1))
                alone(dve, spare_dve)
                dve.bn_aggr(moments[s][:, :], stats[s][:, :]).then_inc(measured[s], 1)
                dve.wait_ge(measured[s], t.item(s, 3, 2))
                dve.tensor_scalar(moments[s][:, 1:2], moments[s][:, 1:2], EPS, None, ALU.add).then_inc(measured[s], 1)

            def normalize(t, s, src, dst):
                dve.wait_ge(inverted[s], t.item(s, 1, 1))
                dve.tensor_scalar(dst, src, moments[s][:, 0:1], inv_std[s][:, :], ALU.subtract,
                                  ALU.mult).then_inc(normed[s], 1)

            def narrow_q(t, s, maxima):
                dve.wait_ge(blocked[s], t.item(s, 2, 2))
                if t.later(s, 1):
                    dve.wait_ge(made[maxima], t.item(s, ATTENTION.repeats[maxima]))
                dve.tensor_copy(q_block16[s][:, :, :], q_block[s][:, t.parity(s), :, :]).then_inc(q16[s], 1)

            def narrow_k(t, s, step, maxima):
                dve.wait_ge(taken[step], t.count(step))
                if t.later(s, 1):
                    dve.wait_ge(made[maxima], t.item(s, ATTENTION.repeats[maxima]))
                dve.tensor_copy(kT16[s][:, :, :], kT[s][:, t.parity(s), :, :]).then_inc(k16[s], 1)

            def average(t, s):
                step = s + ".oN"
                dve.wait_ge(made[step], t.count(step))
                heads = turned[0:T, :].rearrange("t (h w) -> t h w", w=VW)
                if t.later(s, 1):
                    dve.wait_ge(made[s + ".aT"], t.item(s))
                dve.reciprocal(inv_sum[s][:, :].unsqueeze(2), heads[:, :, HD:HD + 1]).then_inc(inv_sums[s], 1)
                dve.wait_ge(inv_sums[s], t.item(s, 1, 1))
                dve.tensor_tensor(att[s][:, :].rearrange("t (h w) -> t h w", w=HD), heads[:, :, 0:HD],
                                  inv_sum[s][:, :].unsqueeze(2).to_broadcast([T, H, HD]),
                                  ALU.mult).then_inc(taken[step], 1)

            def turn(t):
                for step in t.steps():
                    s, kind = step[0], kind_of(step)
                    k = t.parity(s)
                    if step == "N.ln":
                        dve.wait_ge(x_loaded[k], t.dmas("N"))
                        if t.later("N", 1):
                            dve.wait_ge(made["A.xT"], t.item("N"))
                        measure(t, "N", x_in[:, k, :])
                        normalize(t, "N", x_in[:, k, :], x_norm[:, :])
                    elif step == "A.v":
                        dve.wait_ge(made["A.v"], t.count(step))
                        if t.later("A", 2):
                            dve.wait_ge(made["B.pv"], t.item("A", ATTENTION.repeats["B.pv"], -ATTENTION.repeats["B.pv"]))
                        b = wide[t.buffer("wide", step)][0:SC, :, :].rearrange("s b n -> s (b n)")
                        dve.tensor_tensor(values["A"][:, k, :, :, 0:HD],
                                          b[:, 0:NSC * D].rearrange("s (j h w) -> s j h w", j=NSC, w=HD),
                                          bxv[0:SC, :].rearrange("s (h w) -> s h w", w=HD).unsqueeze(1)
                                          .to_broadcast([SC, NSC, H, HD]), ALU.add).then_inc(taken["A.v"], 1)
                    elif step == "A.narrow":
                        narrow_k(t, "A", "A.k", "A.max")
                        narrow_q(t, "A", "A.max")
                    elif step == "C.v":
                        dve.wait_ge(made["C.v"], t.count(step))
                        if t.later("C", 2):
                            dve.wait_ge(made["D.pv"], t.item("C", ATTENTION.repeats["D.pv"], -ATTENTION.repeats["D.pv"]))
                        dve.tensor_tensor(values["C"][:, k, 0, :, 0:HD],
                                          turned[0:T, 0:D].rearrange("s (h w) -> s h w", w=HD),
                                          bsv[0:T, :].rearrange("s (h w) -> s h w", w=HD),
                                          ALU.add).then_inc(taken["C.v"], 1)
                    elif step == "C.narrow":
                        narrow_k(t, "C", "C.qk", "C.max")
                        narrow_q(t, "C", "C.max")
                    elif kind == "A.max":
                        i = index_of(step)
                        dve.wait_ge(made[kind], t.count(step))
                        if i == 0 and t.later("A", 1):
                            dve.wait_ge(made["A.mT"], t.item("A"))
                        dve.tensor_reduce(row_max["A"][:, 2 * i:2 * i + 2],
                                          wide[t.buffer("wide", step)][0:T, :, 0:S], AX_X,
                                          ALU.max).then_inc(taken[kind], 1)
                    elif kind == "C.max":
                        i = index_of(step)
                        dve.wait_ge(made[kind], t.count(step))
                        if i == 0 and t.later("C", 1):
                            dve.wait_ge(made["C.mT"], t.item("C"))
                        dve.tensor_reduce(row_max["C"][:, 8 * i:8 * i + 8].rearrange("t (b h) -> t b h", b=2),
                                          wide[t.buffer("wide", step)][0:T, :, 0:GT]
                                          .rearrange("t b (h s) -> t b h s", s=T), AX_X,
                                          ALU.max).then_inc(taken[kind], 1)
                    elif kind in ("A.mT", "C.mT"):
                        dve.wait_ge(made[kind], t.count(step))
                        if t.later(s, 2):
                            u = "B.s" if s == "A" else "D.s"
                            dve.wait_ge(made[u], t.item(s, ATTENTION.repeats[u], -ATTENTION.repeats[u]))
                        dve.tensor_copy(maxT[s][:, k, :], turned[0:H, 0:T]).then_inc(taken[kind], 1)
                    elif kind in ("B.oN", "E.oN"):
                        average(t, s)
                    elif step == "E.gate":
                        dve.wait_ge(made["E.gate"], t.count(step))
                        if t.later("E", 1):
                            dve.wait_ge(gates_exped, t.item("E"))
                        dve.tensor_tensor(logits[:, :], turned[0:T, 0:E], gate_b[0:T, :], ALU.add).then_inc(taken["E.gate"], 1)
                        dve.wait_ge(taken["E.gate"], t.count(step))
                        alone(dve, spare_dve)
                        dve.max(top_logits[:, :], logits[:, :]).then_inc(gate_steps, 1)
                        dve.wait_ge(gate_steps, t.item("E", 9, 1))
                        dve.tensor_scalar(minus_max[:, :], top_logits[:, 0:1], -1.0, None, ALU.mult).then_inc(gate_steps, 1)
                    elif step == "E.pick":
                        dve.wait_ge(gates_exped, t.item("E", 1, 1))
                        dve.reciprocal(gate_inv[:, :], gate_sum[:, :]).then_inc(gate_steps, 1)
                        dve.wait_ge(gate_steps, t.item("E", 9, 3))
                        dve.tensor_scalar(gate[:, :], gate_exp[:, :], gate_inv[:, :], None, ALU.mult).then_inc(gate_steps, 1)
                        dve.wait_ge(gate_steps, t.item("E", 9, 4))
                        alone(dve, spare_dve)
                        dve.max(top_gate[:, :], gate[:, :]).then_inc(gate_steps, 1)
                        dve.wait_ge(gate_steps, t.item("E", 9, 5))
                        alone(dve, spare_dve)
                        dve.max_index(top_expert[:, :], top_gate[:, :], gate[:, :]).then_inc(gate_steps, 1)
                        dve.wait_ge(gate_steps, t.item("E", 9, 6))
                        if t.later("E", 1):
                            dve.wait_ge(made["E.rank"], t.item("E"))
                            dve.wait_ge(row_steps, t.item("E", 6))
                        dve.tensor_copy(route[:, TOP:2 * TOP], top_expert[:, 0:TOP]).then_inc(gate_steps, 1)
                        dve.wait_ge(gate_steps, t.item("E", 9, 7))
                        for i in range(TOP):
                            ins = dve.tensor_scalar(chosen[:, i, :], expert_ids[0:T, :], route[:, TOP + i:TOP + i + 1], None,
                                                    ALU.is_equal)
                        ins.then_inc(gate_steps, 1)
                        dve.wait_ge(gate_steps, t.item("E", 9, 8))
                        dve.tensor_tensor(chosen_any[:, :], chosen[:, 0, :], chosen[:, 1, :], ALU.add).then_inc(gate_steps, 1)
                        if t.later("E", 2):
                            dve.wait_ge(sent[k], t.dmas("E", 0, TOP))
                        dve.tensor_copy(xm[:, k, :, AT_GATE:AT_GATE + 1], top_gate[:, 0:TOP].unsqueeze(2)).then_inc(row_steps, 1)
                        if t.later("E", 1):
                            dve.wait_ge(back_moved, t.item("E"))
                        dve.tensor_copy(xm[:, k, :, AT_BACK:AT_BACK + 1], back_row[:, :].unsqueeze(2)).then_inc(row_steps, 1)
                        dve.wait_ge(row_steps, t.item("E", 6, 2))
                        dve.tensor_scalar(back_row[:, :], back_row[:, :], float(KEPT * T), None, ALU.add).then_inc(back_moved, 1)
                    elif step == "E.rank":
                        dve.wait_ge(made["E.rank"], t.count(step))
                        dve.tensor_tensor(rows_here[:, :], turned[0:T, 0:E], next_row[0:T, :], ALU.add).then_inc(row_steps, 1)
                        dve.wait_ge(row_steps, t.item("E", 6, 3))
                        dve.tensor_tensor(next_row[:, :], turned[:, E:2 * E], next_row[:, :], ALU.add).then_inc(taken["E.rank"], 1)
                        dve.wait_ge(taken["E.rank"], t.count(step))
                        dve.tensor_tensor(rows_pick[:, :, :], chosen[:, :, :], rows_here[:, :].unsqueeze(1)
                                          .to_broadcast([T, TOP, E]), ALU.mult).then_inc(row_steps, 1)
                        dve.wait_ge(row_steps, t.item("E", 6, 4))
                        dve.tensor_reduce(route[:, 0:TOP], rows_pick[:, :, :], AX_X, ALU.add).then_inc(row_steps, 1)
                        dve.wait_ge(row_steps, t.item("E", 6, 5))
                        dve.tensor_copy(send_row[:, k, :], route[:, 0:TOP]).then_inc(row_steps, 1)
                    elif step == "B.out":
                        dve.wait_ge(made["B.out"], t.count(step))
                        if t.later("B", 1):
                            dve.wait_ge(resid, t.item("B"))
                        dve.tensor_tensor(proj[:, :], turned[0:T, 0:D], bxo[0:T, :], ALU.add).then_inc(taken["B.out"], 1)
                        dve.wait_ge(taken["B.out"], t.count(step))
                        dve.wait_ge(res_loaded[k], t.dmas("B"))
                        if t.later("B", 2):
                            dve.wait_ge(normed["B"], t.item("B", 1, -1))
                        dve.scalar_tensor_tensor(x1[:, k, :], proj[:, :], tanh_g[0:T, 0:1], x_res[:, k, :],
                                                 ALU.mult, ALU.add).then_inc(resid, 1)
                        dve.wait_ge(resid, t.item("B", 1, 1))
                        measure(t, "B", x1[:, k, :])
                        if t.later("B", 2):
                            dve.wait_ge(x1_stored[k], t.dmas("B", 0))
                        dve.tensor_tensor(x1_shift[:, k, :], x1[:, k, :], ln2_shift[0:T, :], ALU.add).then_inc(shifted, 1)
                    elif step == "B.norm":
                        if t.later("B", 2):
                            dve.wait_ge(made["C.yT"], t.item("B", 1, -1))
                            dve.wait_ge(y_biased, t.item("B", 1, -1))
                        normalize(t, "B", x1[:, k, :], y[:, k, :])
                    elif step == "E.out":
                        dve.wait_ge(made["E.out"], t.count(step))
                        dve.wait_ge(y_biased, t.item("E", 1, 1))
                        if t.later("E", 1):
                            dve.wait_ge(gained, t.item("E", 2))
                        dve.tensor_tensor(r[:, :], turned[0:T, 0:D], y_bias[:, k, :], ALU.add).then_inc(taken["E.out"], 1)
                        dve.wait_ge(taken["E.out"], t.count(step))
                        measure(t, "E", r[:, :])
                    elif step == "E.norm":
                        if t.later("E", 1):
                            dve.wait_ge(gained, t.item("E", 2))
                        dve.scalar_tensor_tensor(r_gain[:, :], r[:, :], moments["E"][:, 0:1], ln1_g[0:T, :],
                                                 ALU.subtract, ALU.mult).then_inc(gained, 1)
                        dve.wait_ge(gained, t.item("E", 2, 1))
                        dve.wait_ge(inverted["E"], t.item("E", 1, 1))
                        if t.later("E", 2):
                            dve.wait_ge(xm_stored[k], t.dmas("E", 0))
                            dve.wait_ge(sent[k], t.dmas("E", 0, TOP))
                            dve.wait_ge(xm_copied, t.item("E", 1, -1))
                        dve.scalar_tensor_tensor(xm[:, k, 0, 0:D], r_gain[:, :], inv_std["E"][:, :], ln1_b[0:T, :],
                                                 ALU.mult, ALU.add).then_inc(gained, 1)

            dve.wait_ge(consts, 8)
            dve.tensor_copy(expert_ids[:, :], count_up[:, :]).then_inc(vset, 1)
            dve.wait_ge(vset, 9)
            dve.tensor_scalar(region_of[:, :], expert_ids[:, :], float(REGION), None, ALU.mult).then_inc(vset, 1)
            dve.wait_ge(vset, 10)
            dve.tensor_copy(next_row[:, :], region_of[:, :]).then_inc(vset, 1)
            for out, a in ((ln2_gain, ln2_g), (ln2_shift, ln2_b)):
                dve.tensor_scalar(out[:, :], a[:, :], tanh_g[:, 1:2], None, ALU.mult).then_inc(vset, 1)
            dve.tensor_copy(back_row[:, :], back_i[:, :]).then_inc(vset, 1)
            dve.tensor_scalar(spill_row[:, :], tile_no[:, :], float(SPILL + 1), None, ALU.add).then_inc(vset, 1)
            dve.wait_ge(vset, 15)
            ATTENTION.run(dve, turn)
            attention_over(dve)

            def step(*waits):
                dve.wait_ge(plan_steps, *waits)

            dve.tensor_copy(next_i[:, :], next_row[:, :]).then_inc(plan_steps, 1)
            dve.tensor_tensor(counts[:, :], next_row[:, :], region_of[:, :], ALU.subtract).then_inc(plan_steps, 1)
            dve.memset(ones_f[:, :], 1.0).then_inc(plan_steps, 1)
            dve.tensor_copy(tile_f[:, :], tile_no[:, :]).then_inc(plan_steps, 1)
            step(4)
            dve.tensor_scalar(tiles_i[:, :], counts[:, :], float(P - 1), None, ALU.add).then_inc(plan_steps, 1)
            step(5)
            dve.tensor_scalar(tiles_i[:, :], tiles_i[:, :], P.bit_length() - 1, None, ALU.arith_shift_right).then_inc(plan_steps, 1)
            step(6)
            dve.tensor_copy(tiles[:, :], tiles_i[:, :]).then_inc(plan_steps, 1)
            step(7)
            dve.tensor_tensor_scan(tiles_end[:, :], ones_f[:, :], tiles[:, :], 0.0, ALU.mult, ALU.add).then_inc(plan_steps, 1)
            step(8)
            dve.tensor_scalar(past[:, :], tiles_end[:, :], tile_f[:, :], None, ALU.is_le).then_inc(plan_steps, 1)
            dve.tensor_tensor(count_step[:, 0:E - 1], counts[:, 1:E], counts[:, 0:E - 1], ALU.subtract).then_inc(plan_steps, 1)
            step(10)
            for i, (w, out) in enumerate(((ones_f, tile_expert), (tiles, tile_base), (count_step, tile_count))):
                dve.tensor_tensor_reduce(junk[:, i, 0:E - 1], past[:, 0:E - 1], w[:, 0:E - 1], 1.0, 0.0, ALU.mult, ALU.add,
                                         out[:, :]).then_inc(plan_steps, 1)
            step(13)
            dve.tensor_tensor(tile_row[:, :], tile_f[:, :], tile_base[:, :], ALU.subtract).then_inc(plan_steps, 1)
            dve.tensor_tensor(tile_rest[:, :], tile_count[:, :], counts[:, 0:1], ALU.add).then_inc(plan_steps, 1)
            step(15)
            dve.scalar_tensor_tensor(tile_row[:, :], tile_row[:, :], float(P), tile_rest[:, :], ALU.mult,
                                     ALU.min).then_inc(plan_steps, 1)
            step(16)
            dve.scalar_tensor_tensor(tile_row[:, :], tile_expert[:, :], float(REGION), tile_row[:, :], ALU.mult,
                                     ALU.add).then_inc(plan_steps, 1)
            dve.wait_ge(table_turned, 1)
            dve.tensor_copy(table[:, :], turned[0:1, 0:2 * NT]).then_inc(table_ready, 1)
            dve.wait_ge(output_b_loaded, DMA)
            dve.wait_ge(moe_loaded, 3 * E * DMA)
            dve.wait_ge(table_ready, 1)

            def expert_turn(t):
                if t.active("C"):
                    n, k = t.item("C"), t.parity("C")
                    e = dve.value_load(table[0:1, bass.ds(n, 1)], min_val=0, max_val=E - 1)
                    dve.wait_ge(tile_kept, t.item("C", 1, 1))
                    if t.later("C", 2):
                        dve.wait_ge(tile_done, t.item("C", 1, -1))
                        dve.wait_ge(spill_steps, t.item("C", 3, -3))
                    dve.tensor_copy(tile_ends[:, k, :], tile_meta[:, k, :]).then_inc(tile_moved, 1)
                    dve.wait_ge(ex_made["C.hT"], t.item("C", 1, 1))
                    if t.later("C", 2):
                        dve.wait_ge(ex_made["D.y"], t.item("C", 1, -1))
                    for f in range(FC):
                        ins = dve.tensor_scalar(hiddenT[:, k, f, :], score[k][:, f * P:(f + 1) * P],
                                                hidden_b[:, f, bass.ds(e, 1)], 0.0, ALU.add, ALU.max)
                    ins.then_inc(ex_taken["C.hT"], 1)
                if t.active("D"):
                    n, k = t.item("D"), t.parity("D")
                    e = dve.value_load(table[0:1, bass.ds(n, 1)], min_val=0, max_val=E - 1)
                    dve.wait_ge(tile_moved, t.item("D", 1, 1))
                    dve.wait_ge(ex_made["D.y"], t.item("D", 1, 1))
                    if t.later("D", 2):
                        dve.wait_ge(tile_done, t.item("D", 1, -1))
                        dve.wait_ge(out_stored[k], t.dmas("D", 0))
                    if t.later("D", 1):
                        dve.wait_ge(spill_steps, t.item("D", 3))
                    dve.tensor_scalar(is_spill[:, :], tile_ends[:, k, 1:2], 0.0, spill_row[:, :], ALU.is_equal,
                                      ALU.mult).then_inc(spill_steps, 1)
                    dve.wait_ge(spill_steps, t.item("D", 3, 1))
                    dve.tensor_scalar(spill_row[:, :], spill_row[:, :], float(P), None, ALU.add).then_inc(spill_steps, 1)
                    dve.scalar_tensor_tensor(take_back[:, k, :], tile_ends[:, k, 1:2], -1.0, is_spill[:, :], ALU.add,
                                             ALU.add).then_inc(spill_steps, 1)
                    dve.tensor_tensor(tile_sum[:, k, :], wide[k][:, 1, 0:D], output_b[:, bass.ds(e * D, D)],
                                      ALU.add).then_inc(ex_taken["D.y"], 1)

                if t.active("A"):
                    k = t.parity("A")
                    dve.wait_ge(tile_loaded[k], t.dmas("A"))
                    if t.later("A", 2):
                        dve.wait_ge(tile_moved, t.item("A", 1, -1))
                    dve.tensor_copy(tile_meta[:, k, :], tile_in[:, k, D:SENT]).then_inc(tile_kept, 1)

            EXPERTS.run(dve, expert_turn)

            def join_turn(t):
                if t.active("A"):
                    n, k = t.item("A"), t.parity("A")
                    steps = lambda i: t.item("A", 5, i)
                    dve.wait_ge(join_loaded[k], t.dmas("A"))
                    if t.later("A", 2):
                        dve.wait_ge(result_steps, t.item("A", 2, -2))
                    dve.tensor_tensor(added[:, k, 0, :], join_in[:, k, 0, :], join_in[:, k, 1, :],
                                      ALU.add).then_inc(join_steps, 1)
                    dve.wait_ge(join_steps, steps(1))
                    dve.tensor_tensor(added[:, k, 1, :], join_in[:, k, AT_XM, :], added[:, k, 0, :],
                                      ALU.add).then_inc(join_steps, 1)
                    dve.wait_ge(join_steps, steps(2))
                    dve.bn_stats(join_stats[:, :], added[:, k, 1, :]).then_inc(join_steps, 1)
                    dve.wait_ge(join_steps, steps(3))
                    alone(dve, spare_dve)
                    dve.bn_aggr(join_moments[:, k, :], join_stats[:, :]).then_inc(join_steps, 1)
                    dve.wait_ge(join_steps, steps(4))
                    dve.tensor_scalar(join_moments[:, k, 1:2], join_moments[:, k, 1:2], EPS, None, ALU.add).then_inc(join_steps, 1)
                if t.active("B"):
                    k = t.parity("B")
                    steps = lambda i: t.item("B", 2, i)
                    if t.later("B", 1):
                        dve.wait_ge(result_steps, t.item("B", 2))
                    dve.scalar_tensor_tensor(join_gain[:, :], added[:, k, 1, :], join_moments[:, k, 0:1], ln2_gain[:, :],
                                             ALU.subtract, ALU.mult).then_inc(result_steps, 1)
                    dve.wait_ge(result_steps, steps(1))
                    dve.wait_ge(join_inverted, t.item("B", 1, 1))
                    dve.wait_ge(x1_loaded[k], t.dmas("B"))
                    if t.later("B", 2):
                        dve.wait_ge(result_stored[k], t.dmas("B", 0))
                    dve.scalar_tensor_tensor(result[:, k, :], join_gain[:, :], join_inv[:, k, :], x1_in[:, k, :],
                                             ALU.mult, ALU.add).then_inc(result_steps, 1)

            JOIN.run(dve, join_turn)

        @block.tensor
        def _(pe):
            def transpose_cols(t, step, src, rows, n):
                for c in range(n):
                    mm = pe.transpose(turned[:, c * rows:(c + 1) * rows], src[:, c * P:(c + 1) * P],
                                      ident[0:rows, 0:rows])
                mm.then_inc(made[kind_of(step)], 1)

            def project(out, w, actT, m):
                for c in range(DC):
                    mm = pe.matmul(out, w[:, c, m * P:(m + 1) * P], actT[:, c, :], start=c == 0, stop=c == DC - 1)
                return mm

            def scores(t, step, a, rows):
                i = index_of(step)
                g, j = i // (NSC if a == "A" else 1), i % (NSC if a == "A" else 1)
                k = t.parity(step[0])
                if i == 0:
                    pe.wait_ge(taken[a + ".mT"], t.item(step[0], 1, 1))
                buffer_free(pe, t, "score", step, taken)
                b = score[t.buffer("score", step)]
                keys = slice(j * rows, (j + 1) * rows)
                pe.matmul(b[0:rows, 0:GT], kT[a][:, k, g * G // HC, keys],
                          q_block[a][:, k, g * G:(g + 1) * G, :], start=True, stop=False, skip_group_check=True)
                for h in range(G):
                    mm = pe.matmul(b[0:rows, h * T:(h + 1) * T], pick[:, g * G + h, 0:rows], maxT[a][:, k, :],
                                   start=False, stop=h == G - 1, skip_group_check=True)
                mm.then_inc(made[kind_of(step)], 1)

            def weigh(t, step, a, rows):
                i, n = index_of(step), (NSC if a == "A" else 1)
                g, j = i // n, i % n
                k = t.parity(step[0])
                of = step.replace(".pv", ".s")
                pe.wait_ge(taken[kind_of(of)], t.count(of))
                if i == 0:
                    if step[0] == "B" and t.base > 0 and t.last().active("D"):
                        pe.wait_ge(taken["D.pv"], t.last().item("D", 1, 1))
                    elif t.later(step[0], 1):
                        pe.wait_ge(taken[step[0] + ".pv"], t.item(step[0]))
                    if step[0] == "D" and t.active("B"):
                        pe.wait_ge(taken["B.pv"], t.item("B", 1, 1))
                b = t.buffer("probs", of)
                for h in range(G):
                    mm = pe.matmul(sums[h * VW:(h + 1) * VW, g * T:(g + 1) * T], values[a][0:rows, k, j, g * G + h, :],
                                   probs[0:rows, b, h * T:(h + 1) * T], start=j == 0, stop=j == n - 1)
                mm.then_inc(made[kind_of(step)], 1)

            def turn(t):
                for step in t.steps():
                    s, kind = step[0], kind_of(step)
                    k = t.parity(s)
                    if kind in ATTENTION.pools["turned"][1]:
                        buffer_free(pe, t, "turned", step, taken)
                    if kind in ATTENTION.pools["wide"][1]:
                        buffer_free(pe, t, "wide", step, taken)
                        b = wide[t.buffer("wide", step)]
                    if step == "A.ctxT":
                        pe.wait_ge(ctx_loaded[k], t.dmas("A"))
                        for c in range(DC):
                            for j in range(NSC):
                                mm = pe.transpose(b[:, c, j * SC:(j + 1) * SC], ctx_in[:, k, j, c * P:(c + 1) * P],
                                                  ident[0:SC, 0:SC])
                        mm.then_inc(made[kind], 1)
                    elif step == "A.xT":
                        pe.wait_ge(normed["N"], t.item("A", 1, 1))
                        transpose_cols(t, step, x_norm, T, DC)
                    elif step == "A.k":
                        pe.wait_ge(taken["A.ctxT"], t.item("A", 1, 1))
                        for m in range(DC):
                            mm = project(b[:, m, 0:S], wxk, ctxT, m)
                        mm.then_inc(made[kind], 1)
                    elif step == "A.q":
                        pe.wait_ge(taken["A.xT"], t.item("A", 1, 1))
                        for m in range(DC):
                            mm = project(turned[:, m * T:(m + 1) * T], wxq, x_normT, m)
                        mm.then_inc(made[kind], 1)
                    elif step == "A.v":
                        for j in range(NSC):
                            for c in range(DC):
                                mm = pe.matmul(b[0:SC, j // 2, (j % 2) * D:(j % 2 + 1) * D],
                                               ctxT[:, c, j * SC:(j + 1) * SC], wxv[:, c, :],
                                               start=c == 0, stop=c == DC - 1)
                        mm.then_inc(made[kind], 1)
                    elif kind == "A.max":
                        i = index_of(step)
                        if i == 0:
                            pe.wait_ge(k16["A"], t.item("A", 1, 1))
                            pe.wait_ge(q16["A"], t.item("A", 1, 1))
                        for h in range(2 * i, 2 * i + 2):
                            mm = pe.matmul(b[0:T, h % 2, 0:S], q_block16["A"][:, h, :], kT16["A"][:, h // HC, :],
                                           start=True, stop=True)
                        mm.then_inc(made[kind], 1)
                    elif kind == "C.max":
                        i = index_of(step)
                        if i == 0:
                            pe.wait_ge(k16["C"], t.item("C", 1, 1))
                            pe.wait_ge(q16["C"], t.item("C", 1, 1))
                        for h in range(8):
                            mm = pe.matmul(b[0:T, h // G, h % G * T:(h % G + 1) * T], q_block16["C"][:, 8 * i + h, :],
                                           kT16["C"][:, (8 * i + h) // HC, :], start=True, stop=True)
                        mm.then_inc(made[kind], 1)
                    elif kind in ("A.mT", "C.mT"):
                        pe.wait_ge(taken[s + ".max"], t.item(s, ATTENTION.repeats[s + ".max"], ATTENTION.repeats[s + ".max"]))
                        pe.transpose(turned[0:H, 0:T], row_max[s][:, :], ident[0:T, 0:T]).then_inc(made[kind], 1)
                    elif kind == "B.s":
                        scores(t, step, "A", SC)
                    elif kind == "D.s":
                        scores(t, step, "C", T)
                    elif kind == "B.pv":
                        weigh(t, step, "A", SC)
                    elif kind == "D.pv":
                        weigh(t, step, "C", T)
                    elif kind in ("B.oN", "E.oN"):
                        pe.wait_ge(taken["B.pv" if s == "B" else "D.pv"], t.item(s, 1, 1))
                        for g in range(NG):
                            mm = pe.transpose(turned[0:T, g * P:(g + 1) * P], outT[s][:, g * T:(g + 1) * T], ident[:, :])
                        mm.then_inc(made[kind], 1)
                    elif kind in ("B.aT", "E.aT"):
                        pe.wait_ge(taken[s + ".oN"], t.item(s, 1, 1))
                        transpose_cols(t, step, att[s], T, DC)
                    elif kind in ("B.out", "E.out"):
                        pe.wait_ge(taken[s + ".aT"], t.item(s, 1, 1))
                        for c in range(DC):
                            mm = pe.matmul(turned[0:T, 0:D], attT[s][:, c, :], (wxo if s == "B" else wso)[:, c, :],
                                           start=c == 0, stop=c == DC - 1)
                        mm.then_inc(made[kind], 1)
                    elif step == "E.xT":
                        pe.wait_ge(gained, t.item("E", 2, 2))
                        transpose_cols(t, step, xm[:, k, 0, 0:D], T, DC)
                    elif step == "E.gate":
                        pe.wait_ge(taken["E.xT"], t.item("E", 1, 1))
                        for c in range(DC):
                            mm = pe.matmul(turned[0:T, 0:E], xmT[:, c, :], gate_w[:, c, :], start=c == 0, stop=c == DC - 1)
                        mm.then_inc(made[kind], 1)
                    elif step == "E.rank":
                        pe.wait_ge(gate_steps, t.item("E", 9, 9))
                        pe.matmul(turned[0:T, 0:E], below[0:T, 0:T], chosen_any[:, :], start=True, stop=True)
                        pe.matmul(turned[:, E:2 * E], ones[0:T, :], chosen_any[:, :], start=True, stop=True,
                                  skip_group_check=True).then_inc(made[kind], 1)
                    elif step == "C.yT":
                        pe.wait_ge(normed["B"], t.item("C", 1, 1))
                        transpose_cols(t, step, y[:, k, :], T, DC)
                    elif step == "C.qk":
                        pe.wait_ge(taken["C.yT"], t.item("C", 1, 1))
                        for m in range(DC):
                            project(b[:, 0, m * T:(m + 1) * T], wsq, yT, m)
                        for m in range(DC):
                            mm = project(b[:, 1, m * T:(m + 1) * T], wsk, yT, m)
                        mm.then_inc(made[kind], 1)
                    elif step == "C.v":
                        for c in range(DC):
                            mm = pe.matmul(turned[0:T, 0:D], yT[:, c, :], wsv[:, c, :], start=c == 0, stop=c == DC - 1)
                        mm.then_inc(made[kind], 1)

            pe.wait_ge(consts, 8)
            pe.wait_ge(vset, 8)
            pe.wait_ge(w_loaded["A"], 6 * DMA)
            pe.wait_ge(w_loaded["B"], 4 * DMA)
            pe.wait_ge(w_loaded["C"], 14 * DMA)
            ATTENTION.run(pe, turn)
            attention_over(pe)
            pe.wait_ge(plan_steps, 17)
            pe.transpose(turned[0:1, 0:NT], tile_expert[0:NT, :], ident[0:NT, 0:NT])
            pe.transpose(turned[0:1, NT:2 * NT], tile_row[0:NT, :], ident[0:NT, 0:NT]).then_inc(table_turned, 1)
            pe.wait_ge(moe_loaded, 3 * E * DMA)
            pe.wait_ge(table_ready, 1)

            def expert_turn(t):
                if t.active("A"):
                    k = t.parity("A")
                    pe.wait_ge(tile_loaded[k], t.dmas("A"))
                    if t.later("A", 2):
                        pe.wait_ge(ex_taken["A.x"], t.item("A", 1, -1))
                    for c in range(DC):
                        mm = pe.transpose(rows_bank[k][:, c * P:(c + 1) * P], tile_in[:, k, c * P:(c + 1) * P], ident[:, :])
                    mm.then_inc(ex_made["A.x"], 1)
                if t.active("B"):
                    n, k = t.item("B"), t.parity("B")
                    e = pe.value_load(table[0:1, bass.ds(n, 1)], min_val=0, max_val=E - 1)
                    pe.wait_ge(ex_taken["A.x"], t.item("B", 1, 1))
                    if t.later("B", 2):
                        pe.wait_ge(ex_taken["B.h"], t.item("B", 1, -1))
                    for c in range(DC):
                        mm = pe.matmul(wide[k][:, 0, 0:F], tile_inT[:, k, c, :], hidden_w[:, c, bass.ds(e * F, F)],
                                       start=c == 0, stop=c == DC - 1)
                    mm.then_inc(ex_made["B.h"], 1)
                if t.active("C"):
                    k = t.parity("C")
                    pe.wait_ge(ex_taken["B.h"], t.item("C", 1, 1))
                    if t.later("C", 2):
                        pe.wait_ge(ex_taken["C.hT"], t.item("C", 1, -1))
                    for f in range(FC):
                        mm = pe.transpose(score[k][:, f * P:(f + 1) * P], hidden[:, k, f * P:(f + 1) * P], ident[:, :])
                    mm.then_inc(ex_made["C.hT"], 1)
                if t.active("D"):
                    n, k = t.item("D"), t.parity("D")
                    e = pe.value_load(table[0:1, bass.ds(n, 1)], min_val=0, max_val=E - 1)
                    pe.wait_ge(ex_taken["C.hT"], t.item("D", 1, 1))
                    if t.later("D", 2):
                        pe.wait_ge(ex_taken["D.y"], t.item("D", 1, -1))
                    for f in range(FC):
                        mm = pe.matmul(wide[k][:, 1, 0:D], hiddenT[:, k, f, :], output_w[:, f, bass.ds(e * D, D)],
                                       start=f == 0, stop=f == FC - 1)
                    mm.then_inc(ex_made["D.y"], 1)

            EXPERTS.run(pe, expert_turn)


WEIGHTS = {"ln1_g": "L0_ffn_ln1_g", "ln1_b": "L0_ffn_ln1_b", "ln2_g": "L0_ffn_ln2_g", "ln2_b": "L0_ffn_ln2_b",
           "gate_w": "L0_ffn_gW", "gate_b": "L0_ffn_gb", "hidden_w": "L0_ffn_W1", "hidden_b": "L0_ffn_b1",
           "output_w": "L0_ffn_W2", "output_b": "L0_ffn_b2", "g_xattn": "g_xattn", "g_ffn": "g_ffn"}


def kernel(**inputs):
    import numpy as np
    import concourse.bacc as bacc
    from concourse.bass_utils import run_bass_kernel_spmd

    arrays = {"x": np.asarray(inputs["x"]).reshape(NB * T, D), "ctx": np.asarray(inputs["ctx_1024"]).reshape(NB * S, D)}
    for name, source in WEIGHTS.items():
        arrays[name] = np.asarray(inputs[source])
    for c in "qkvo":
        arrays["wx" + c] = np.asarray(inputs["L0_xattn_W" + c]).T
        arrays["bx" + c] = np.asarray(inputs["L0_xattn_b" + c])
        arrays["ws" + c] = np.asarray(inputs["L0_ffn_W" + c])
        arrays["bs" + c] = np.asarray(inputs["L0_ffn_b" + c])
    nc = bacc.Bacc("TRN2", target_bir_lowering=False, num_devices=1)
    io, feed = {}, {}
    for name, a in arrays.items():
        feed[f"in_{name}_dram"] = np.ascontiguousarray(a)
        io[name] = nc.dram_tensor(f"in_{name}_dram", a.shape, F32, kind="ExternalInput").ap()
    io["out"] = nc.dram_tensor("out_dram", (NB * T, D), F32, kind="ExternalOutput").ap()
    for name, rows, columns in (("kept", SPILL + NT * P, D), ("sent", E * REGION, SENT)):
        io[name] = nc.dram_tensor(f"{name}_dram", (rows, columns), F32).ap()
    build(nc, io)
    r = run_bass_kernel_spmd(nc, [feed], core_ids=[0])
    return r.results[0]["out_dram"].reshape(NB, T, D)
```

```python
import concourse.bass as bass
from concourse import mybir
from contextlib import ExitStack

F32 = mybir.dt.float32
I32 = mybir.dt.int32
U32 = mybir.dt.uint32
BF16 = mybir.dt.bfloat16
ALU = mybir.AluOpType
ACT = mybir.ActivationFunctionType
AX_X = mybir.AxisListType.X

NB, T, D = 32, 112, 256
S = 375
H, HD = 16, 16
P = 128
DC = D // P
SC, NSC = 125, 3
HC = P // HD
G = 4
GT = G * T
NG = H // G
VW = 32
BANK = 512
EPS = 1e-5
SCALE = HD ** -0.5
DMA = 16

E = 8
F = 512
FC = F // P
TOP = 2
PARTS = 3
STACK = PARTS * (PARTS + 1) // 2 * HD
SPREADS = {"A": 2 * DC, "C": DC}
STACKS = 2 * PARTS
SENT, AT_GATE, AT_BACK = D + 2, D, D + 1
KEPT, AT_XM, AT_X1 = TOP + 2, TOP, TOP + 1
SPILL = NB * T * KEPT
REGION = NB * T + P
NT = 64
assert NT >= NB * T * TOP // P + E - 1 and NT % 2 == 0


def kind_of(step):
    return step.rstrip("0123456789")


def index_of(step):
    return int(step[len(kind_of(step)):] or 0)


class Plan:

    def __init__(self, items, peeled, lag, order, pools):
        self.items, self.peeled, self.lag, self.order, self.pools = items, peeled, lag, order, pools
        self.turns = items + max(lag.values())
        self.passes = (items - peeled) // 2
        assert (items - peeled) % 2 == 0
        self.repeats = {kind_of(s): sum(kind_of(x) == kind_of(s) for x in order) for s in order}

    def run(self, eng, do):
        for b in range(self.peeled):
            do(Turn(self, b))
        with eng.Fori(0, self.passes) as p:
            for b in range(self.peeled, self.peeled + 2):
                do(Turn(self, b, p))
        for b in range(self.items, self.turns):
            do(Turn(self, b))


class Turn:

    def __init__(self, plan, base, p=None):
        self.plan, self.base, self.p = plan, base, p

    def last(self):
        return Turn(self.plan, self.base - 1, self.p)

    def active(self, stage):
        return 0 <= self.base - self.plan.lag[stage] < self.plan.items

    def steps(self):
        return [s for s in self.plan.order if self.active(s[0])]

    def item(self, stage, times=1, plus=0):
        const = (self.base - self.plan.lag[stage]) * times + plus
        return const if self.p is None else self.p * (2 * times) + const

    def later(self, stage, lag):
        return self.base - self.plan.lag[stage] >= lag

    def parity(self, stage):
        return (self.base - self.plan.lag[stage]) % 2

    def dmas(self, stage, plus=1, each=1):
        const = ((self.base - self.plan.lag[stage]) // 2 + plus) * DMA * each
        return const if self.p is None else self.p * (DMA * each) + const

    def count(self, step, plus=1):
        return self.item(step[0], self.plan.repeats[kind_of(step)], index_of(step) + plus)

    def uses(self, pool, step):
        kinds = self.plan.pools[pool][1]
        uses = [(b, s) for b in range(self.base + 1) for s in Turn(self.plan, b).steps() if kind_of(s) in kinds]
        return uses[:uses.index((self.base, step)) + 1]

    def buffer(self, pool, step):
        return (len(self.uses(pool, step)) - 1) % self.plan.pools[pool][0]

    def before(self, pool, step):
        uses = self.uses(pool, step)
        depth = self.plan.pools[pool][0]
        if len(uses) <= depth:
            return None
        b, s = uses[-1 - depth]
        return Turn(self.plan, b, self.p), s


ATTENTION = Plan(
    NB, 8, {"N": 0, "A": 1, "B": 2, "C": 3, "D": 4, "E": 5, "F": 3},
    ["F.oN", "A.ctxT0", "A.ctxT1", "F.aT", "D.s0", "D.s1", "A.xT", "F.out", "A.k0", "A.k1", "E.oN", "D.s2", "F.norm",
     "D.s3", "A.q", "E.aT", "D.pv", "A.split", "C.yT", "A.v0", "E.out", "C.qk0", "A.v1", "A.spread", "C.qk1",
     "A.stack", "E.norm", "B.s0", "B.s1", "C.split", "E.xT", "B.pv0", "B.s2", "B.s3", "B.pv1", "E.gate",
     "E.pick", "B.pv2", "B.pv3", "B.s4", "B.s5", "B.pv4", "C.v", "E.rank", "C.spread", "B.pv5", "A.max0",
     "A.max1", "B.s6", "B.s7", "A.max2", "A.max3", "B.pv6", "C.stack", "A.max4", "A.max5", "B.pv7", "A.max6",
     "A.max7", "N.ln", "B.s8", "B.s9", "B.pv8", "A.max8", "B.s10", "A.max9", "A.max10", "A.max11", "C.max0",
     "C.max1", "C.max2", "B.pv9", "C.max3", "A.max12", "B.s11", "B.pv10", "C.mT", "A.max13", "A.max14",
     "B.pv11", "A.max15", "A.mT", "C.top", "E.send", "A.top"],
    {"bank": (3, {"A.ctxT", "A.k", "A.v", "A.xT", "A.q", "A.mT", "F.oN", "F.aT", "F.out", "C.yT", "C.qk", "C.v",
                  "C.mT", "E.oN", "E.aT", "E.out", "E.xT", "E.gate", "E.rank", "D.pv"}),
     "max": (2, {"A.max", "C.max"}),
     "score": (2, {"B.s", "D.s"}),
     "probs": (4, {"B.s", "D.s"})})

EXPERTS = Plan(NT, 6, {"A": 0, "B": 1, "C": 2, "D": 3}, ["A.x", "B.h", "C.hT", "D.y"], {})

JT = NB * T // P
JOIN = Plan(JT, 4, {"A": 0, "B": 1}, ["A.add", "B.norm"], {})


def build(nc, io):
    ctx = ExitStack()
    with ctx:
        def sb(name, shape, dt=F32):
            return ctx.enter_context(nc.sbuf_tensor(name, shape, dt))

        def sem(name):
            return ctx.enter_context(nc.semaphore(name))

        ident = sb("ident", [P, P])
        minus_ones = sb("minus_ones", [SC, 2 * H * S // SC], BF16)
        minus_half, zero = sb("minus_half", [P, 1]), sb("zero", [P, 1])
        spare_dve, spare_pool = sb("spare_dve", [P, 3]), sb("spare_pool", [P, 3])
        tile_no = sb("tile_no", [P, 1], I32)
        wxq, wxk, wxv, wxo = (sb(n, [P, DC, D]) for n in ("wxq", "wxk", "wxv", "wxo"))
        wsq, wsk, wsv, wso = (sb(n, [P, DC, D]) for n in ("wsq", "wsk", "wsv", "wso"))
        bxq, bxk, bsq, bsk = (sb(n, [P, DC]) for n in ("bxq", "bxk", "bsq", "bsk"))
        bxv, bxo, bsv, bso = (sb(n, [P, D]) for n in ("bxv", "bxo", "bsv", "bso"))
        ln1_g, ln1_b = sb("ln1_g", [P, D]), sb("ln1_b", [P, D])
        ln2_g, ln2_b = sb("ln2_g", [P, D]), sb("ln2_b", [P, D])
        ln2_gain, ln2_shift = sb("ln2_gain", [P, D]), sb("ln2_shift", [P, D])
        gates = sb("gates", [P, 2])
        tanh_g = sb("tanh_g", [P, 2])

        gate_w = sb("gate_w", [P, DC, E])
        gate_b = sb("gate_b", [P, E])
        hidden_w = sb("hidden_w", [P, DC, E * F])
        hidden_b = sb("hidden_b", [P, FC, E])
        output_w = [sb("output_w0", [P, FC // 2, E * D])]
        below = sb("below", [P, P], BF16)
        ones = sb("ones", [P, P], BF16)
        count_up = sb("count_up", [P, E], I32)
        expert_ids = sb("expert_ids", [P, E])
        region_of = sb("region_of", [P, E])
        next_row = sb("next_row", [P, E])
        back_row = sb("back_row", [T, TOP])
        back_i = sb("back_i", [T, TOP], I32)
        spill_row = sb("spill_row", [P, 1])

        banks = [ctx.enter_context(nc.psum_tensor(f"bank{i}", [P, BANK], F32)) for i in range(3)]
        max_banks = [ctx.enter_context(nc.psum_tensor(f"max_bank{i}", [P, BANK], F32)) for i in range(2)]
        score = [ctx.enter_context(nc.psum_tensor(f"score{i}", [P, BANK], F32)) for i in range(2)]
        sums = ctx.enter_context(nc.psum_tensor("sums", [P, BANK], F32))

        rows_bank, hidden_bank, output_bank = [banks[0], sums], [banks[1], banks[2]], max_banks

        scope = ExitStack()

        def sb(name, shape, dt=F32):
            return scope.enter_context(nc.sbuf_tensor(name, shape, dt))

        k_f, k_rest = sb("k_f", [P, DC, S]), sb("k_rest", [P, DC, S])
        k_parts = sb("k_parts", [P, PARTS, DC, S], BF16)
        ctx_in = sb("ctx_in", [SC, 2, NSC, D])
        ctxT = sb("ctxT", [P, DC, S])
        x_norm = sb("x_norm", [T, D])
        q_f, q_rest = sb("q_f", [P, DC, T]), sb("q_rest", [P, DC, T])
        q_parts = sb("q_parts", [P, PARTS, DC, T], BF16)
        x_in = sb("x_in", [T, 2, D])
        x_res = sb("x_res", [T, 2, D])
        stats = {s: sb("stats_" + s, [T, 6]) for s in "NFE"}
        moments = {s: sb("moments_" + s, [T, 2]) for s in "NFE"}
        inv_std = {s: sb("inv_std_" + s, [T, 1]) for s in "NFE"}
        x_normT = sb("x_normT", [P, DC, T])
        qk_f, qk_rest = sb("qk_f", [P, 2, DC, T]), sb("qk_rest", [P, 2, DC, T])
        qk_parts = sb("qk_parts", [P, 2 * PARTS, DC, T], BF16)
        q_stack = {s: sb("q_stack_" + s, [STACK + 1, 2, H, T], BF16) for s in "AC"}
        k_stack = {"A": sb("k_stack_A", [STACK + 1, 2, H, S], BF16),
                   "C": sb("k_stack_C", [STACK + 1, 2, H, T], BF16)}
        values = {"A": sb("values_A", [SC, 2, NSC, H, VW]), "C": sb("values_C", [T, 2, 1, H, VW])}
        row_max = {s: sb("row_max_" + s, [T, H]) for s in "AC"}
        maxT = {s: sb("maxT_" + s, [H, 2, T], BF16) for s in "AC"}
        probs = sb("probs", [SC, ATTENTION.pools["probs"][0], GT])
        outT = {s: sb("outT_" + s, [P, GT]) for s in "FE"}
        inv_sum = {s: sb("inv_sum_" + s, [T, H]) for s in "FE"}
        att = {s: sb("att_" + s, [T, D]) for s in "FE"}
        attT = {s: sb("attT_" + s, [P, DC, T]) for s in "FE"}
        proj = sb("proj", [T, D])
        x1 = sb("x1", [T, 2, D])
        x1_shift = sb("x1_shift", [T, 2, D])
        y = sb("y", [T, 2, D])
        yT = sb("yT", [P, DC, T])
        y_bias = sb("y_bias", [T, 2, D])
        r = sb("r", [T, D])
        r_gain = sb("r_gain", [T, D])
        xm = sb("xm", [T, 2, TOP, SENT])

        xmT = sb("xmT", [P, DC, T])
        logits = sb("logits", [T, E])
        top_logits = sb("top_logits", [T, 8])
        minus_max = sb("minus_max", [T, 1])
        gate_exp = sb("gate_exp", [T, E])
        gate_sum = sb("gate_sum", [T, 1])
        gate_inv = sb("gate_inv", [T, 1])
        gate = sb("gate", [T, E])
        top_gate = sb("top_gate", [T, 8])
        top_expert = sb("top_expert", [T, 8], U32)
        chosen = sb("chosen", [T, TOP, E])
        chosen_any = sb("chosen_any", [T, E], BF16)
        rows_here = sb("rows_here", [T, E])
        rows_pick = sb("rows_pick", [T, TOP, E])
        route = sb("route", [T, 2 * TOP])
        send_row = sb("send_row", [T, 2, TOP], U32)

        scope.close()
        scope = ctx.enter_context(ExitStack())
        output_w.append(sb("output_w1", [P, FC // 2, E * D]))
        output_b = sb("output_b", [P, E * D])
        zero_rows = sb("zero_rows", [P, SENT])
        counts = sb("counts", [P, E])
        tiles_i = sb("tiles_i", [P, E], I32)
        tiles = sb("tiles", [P, E])
        tiles_end = sb("tiles_end", [P, E])
        ones_f = sb("ones_f", [P, E])
        next_i = sb("next_i", [P, E], I32)
        tile_f = sb("tile_f", [P, 1])
        past = sb("past", [P, E])
        count_step = sb("count_step", [P, E])
        junk = sb("junk", [P, 3, E])
        tile_expert, tile_base, tile_count = (sb(n, [P, 1]) for n in ("tile_expert", "tile_base", "tile_count"))
        tile_row, tile_rest = sb("tile_row", [P, 1]), sb("tile_rest", [P, 1])
        table = sb("table", [1, 2 * NT], I32)
        tile_in = sb("tile_in", [P, 2, SENT])
        tile_meta = sb("tile_meta", [P, 2, 2])
        tile_ends = sb("tile_ends", [P, 2, 2])
        tile_inT = sb("tile_inT", [P, 2, DC, P])
        hidden = sb("hidden", [P, 2, F])
        hiddenT = sb("hiddenT", [P, 2, FC, P])
        tile_sum = sb("tile_sum", [P, 2, D])
        tile_out = sb("tile_out", [P, 2, D])
        is_spill = sb("is_spill", [P, 1])
        take_back = sb("take_back", [P, 2, 1], U32)
        join_in = sb("join_in", [P, 2, AT_X1, D])
        x1_in = sb("x1_in", [P, 2, D])
        added = sb("added", [P, 2, TOP, D])
        join_stats = sb("join_stats", [P, 6])
        join_moments = sb("join_moments", [P, 2, 2])
        join_inv = sb("join_inv", [P, 2, 1])
        join_gain = sb("join_gain", [P, D])
        result = sb("result", [P, 2, D])

        in_psum = [k for k in ATTENTION.repeats if k.split(".")[1] not in
                   ("ln", "norm", "split", "spread", "stack", "top", "pick", "send")]
        made = {k: sem("made_" + k.replace(".", "_")) for k in in_psum}
        taken = {k: sem("taken_" + k.replace(".", "_")) for k in in_psum}
        gates_exped = sem("gates_exped")
        gate_steps = sem("gate_steps")
        row_steps = sem("row_steps")
        sent = [sem(f"sent{i}") for i in range(2)]
        moe_loaded = sem("moe_loaded")
        output_b_loaded = sem("output_b_loaded")
        output_w_loaded = sem("output_w_loaded")
        plan_steps = sem("plan_steps")
        zero_set = sem("zero_set")
        tails_zeroed = sem("tails_zeroed")
        xm_copied = sem("xm_copied")
        back_moved = sem("back_moved")
        spill_steps = sem("spill_steps")
        scatter_begun = sem("scatter_begun")
        tile_done = sem("tile_done")
        tile_kept = sem("tile_kept")
        tile_moved = sem("tile_moved")
        table_turned = sem("table_turned")
        table_ready = sem("table_ready")
        tile_loaded = [sem(f"tile_loaded{i}") for i in range(2)]
        out_stored = [sem(f"out_stored{i}") for i in range(2)]
        ex_made = {k: sem("ex_made_" + k.replace(".", "_")) for k in EXPERTS.repeats}
        ex_taken = {k: sem("ex_taken_" + k.replace(".", "_")) for k in EXPERTS.repeats}
        x1_loaded = [sem(f"x1_loaded{i}") for i in range(2)]
        join_loaded = [sem(f"join_loaded{i}") for i in range(2)]
        result_stored = [sem(f"result_stored{i}") for i in range(2)]
        join_steps = sem("join_steps")
        join_inverted = sem("join_inverted")
        result_steps = sem("result_steps")
        w_loaded = {n: sem("w_loaded_" + n) for n in ("A", "B", "C")}
        x_loaded = [sem(f"x_loaded{i}") for i in range(2)]
        ctx_loaded = [sem(f"ctx_loaded{i}") for i in range(2)]
        res_loaded = [sem(f"res_loaded{i}") for i in range(2)]
        x1_stored = [sem(f"x1_stored{i}") for i in range(2)]
        xm_stored = [sem(f"xm_stored{i}") for i in range(2)]
        zeroed = sem("zeroed")
        vset = sem("vset")
        consts = sem("consts")
        tanh_done = sem("tanh_done")
        ones_set = sem("ones_set")
        last_rows_set = sem("last_rows_set")
        measured = {s: sem("measured_" + s) for s in "NFE"}
        inverted = {s: sem("inverted_" + s) for s in "NFE"}
        normed = {s: sem("normed_" + s) for s in "NFE"}
        k_split = sem("k_split")
        q_split = sem("q_split")
        qk_split = sem("qk_split")
        spread = {s: [sem(f"spread_{s}{i}") for i in range(2)] for s in "AC"}
        stacked = {s: [sem(f"stacked_{s}{i}") for i in range(2)] for s in "AC"}
        topped = {s: [sem(f"topped_{s}{i}") for i in range(2)] for s in "AC"}
        inv_sums = {s: sem("inv_sums_" + s) for s in "FE"}
        resid = sem("resid")
        y_biased = sem("y_biased")
        shifted = sem("shifted")
        gained = sem("gained")

        W_COUNTS = {"A": 6, "B": 4, "C": 14}

        def weights(eng, t, *stages):
            for stage in stages:
                if t.base == ATTENTION.lag[stage]:
                    eng.wait_ge(w_loaded[stage], W_COUNTS[stage] * DMA)

        def bank_of(t, step):
            return banks[t.buffer("bank", step)] if kind_of(step) in ATTENTION.pools["bank"][1] else None

        def buffer_free(eng, t, pool, step, by):
            last = t.before(pool, step)
            if last is not None:
                eng.wait_ge(by[kind_of(last[1])], last[0].count(last[1]))

        def alone(eng, spare):
            return eng.tensor_tensor(spare[0:1, 0:1], spare[0:1, 1:2], spare[0:1, 2:3], ALU.add)

        kept = io["kept"][0:SPILL, :].rearrange("(n r) d -> n r d", r=KEPT)

        def kept_rows(n, row):
            return kept[bass.ds(n * T, T), row, :]

        def stacks_free(eng, t, s):
            if t.later(s, 2):
                scores = "B.s" if s == "A" else "D.s"
                eng.wait_ge(stacked[s][t.parity(s)], t.dmas(s, 0, STACKS))
                eng.wait_ge(made[scores], t.item(s, ATTENTION.repeats[scores], -ATTENTION.repeats[scores]))

        def attention_over(eng):
            for k in range(2):
                eng.wait_ge(sent[k], NB // 2 * DMA * TOP)

        def experts_over(eng):
            for k in range(2):
                eng.wait_ge(out_stored[k], NT // 2 * DMA)

        block = ctx.enter_context(nc.Block())

        @block.sync
        def _(sp):
            def square(w, a):
                return sp.dma_start(w[:, :, :], a.rearrange("(c p) n -> p c n", p=P))

            def column(b, a):
                return sp.dma_start(b[:, :], a.rearrange("(c p) -> p c", p=P), allow_slow_non_contiguous=True)

            def row(b, a):
                return sp.dma_start(b[:, :], a.partition_broadcast(P))

            def load_output_w(e, half, loaded):
                sp.dma_start(output_w[half][:, :, e * D:(e + 1) * D],
                             io["output_w"][e, half * F // 2:(half + 1) * F // 2, :].rearrange("(c p) d -> p c d", p=P)
                             ).then_inc(loaded, DMA)

            def load(t):
                n, k = t.item("N"), t.parity("N")
                if t.later("N", 2):
                    sp.wait_ge(normed["N"], t.item("N", 1, -1))
                sp.dma_start(x_in[:, k, :], io["x"][bass.ds(n * T, T), :]).then_inc(x_loaded[k], DMA)
                if t.later("N", 2):
                    sp.wait_ge(made["A.ctxT"], t.item("N", 2, -2))
                sp.dma_start(ctx_in[:, k, :, :],
                             io["ctx"][bass.ds(n * S, S), :].rearrange("(j p) d -> p j d", p=SC)
                             ).then_inc(ctx_loaded[k], DMA)

            def read_stack(stack, k, source, sem_):
                row_no = 0
                for lo, hi in source[1]:
                    rows = (hi - lo) * HD
                    sp.dma_start(stack[row_no:row_no + rows, k, :, :].rearrange("p (c h) s -> p c (h s)", c=DC),
                                 source[0][:, lo:hi].rearrange("c q d h s -> (q d) c (h s)")).then_inc(sem_[k], DMA)
                    row_no += rows

            Q_RUNS = [(0, 3), (0, 2), (0, 1)]
            K_RUNS = [(0, 3), (1, 3), (2, 3)]

            def move_parts(t):
                for step in t.steps():
                    s = step[0]
                    k = t.parity(s)
                    if step == "A.spread":
                        sp.wait_ge(k_split, t.item("A", 3, 3))
                        for c in range(DC):
                            sp.dma_start(io[f"k_parts_A{k}"][c].rearrange("q d h s -> (d h) q s"),
                                         k_parts[:, :, c, :]).then_inc(spread["A"][k], DMA)
                        sp.wait_ge(q_split, t.item("A", 4, 4))
                        for c in range(DC):
                            sp.dma_start(io[f"q_parts_A{k}"][c].rearrange("q d h s -> (d h) q s"),
                                         q_parts[:, :, c, :]).then_inc(spread["A"][k], DMA)
                    elif step == "C.spread":
                        sp.wait_ge(qk_split, t.item("C", 4, 4))
                        for c in range(DC):
                            sp.dma_start(io[f"qk_parts_C{k}"][c].rearrange("q d h s -> (d h) q s"),
                                         qk_parts[:, :, c, :]).then_inc(spread["C"][k], DMA)
                    elif step in ("A.stack", "C.stack"):
                        sp.wait_ge(spread[s][k], t.dmas(s, 1, SPREADS[s]))
                        if s == "A":
                            read_stack(k_stack["A"], k, (io[f"k_parts_A{k}"], K_RUNS), stacked["A"])
                            read_stack(q_stack["A"], k, (io[f"q_parts_A{k}"], Q_RUNS), stacked["A"])
                        else:
                            read_stack(k_stack["C"], k, (io[f"qk_parts_C{k}"][:, PARTS:2 * PARTS], K_RUNS), stacked["C"])
                            read_stack(q_stack["C"], k, (io[f"qk_parts_C{k}"][:, 0:PARTS], Q_RUNS), stacked["C"])
                    elif step in ("A.top", "C.top"):
                        sp.wait_ge(taken[s + ".mT"], t.item(s, 1, 1))
                        sp.dma_start(q_stack[s][STACK:STACK + 1, k, :, :].rearrange("p h t -> p (h t)"),
                                     maxT[s][:, k, :]).then_inc(topped[s][k], DMA)
                    elif step == "E.norm":
                        n = t.item("E")
                        sp.wait_ge(gained, t.item("E", 2, 2))
                        sp.dma_start(kept_rows(n, AT_XM), xm[:, k, 0, 0:D]).then_inc(xm_stored[k], DMA)

            def load_weights(stage):
                if stage == "A":
                    square(wxk, io["wxk"]).then_inc(w_loaded["A"], DMA)
                    square(wxq, io["wxq"]).then_inc(w_loaded["A"], DMA)
                    square(wxv, io["wxv"]).then_inc(w_loaded["A"], DMA)
                    column(bxk, io["bxk"]).then_inc(w_loaded["A"], DMA)
                    column(bxq, io["bxq"]).then_inc(w_loaded["A"], DMA)
                    row(bxv, io["bxv"]).then_inc(w_loaded["A"], DMA)
                if stage == "B":
                    square(wxo, io["wxo"]).then_inc(w_loaded["B"], DMA)
                    row(bxo, io["bxo"]).then_inc(w_loaded["B"], DMA)
                    sp.dma_start(gates[:, 0:1], io["g_xattn"].partition_broadcast(P)).then_inc(w_loaded["B"], DMA)
                    sp.dma_start(gates[:, 1:2], io["g_ffn"].partition_broadcast(P)).then_inc(w_loaded["B"], DMA)
                if stage == "C":
                    for w, a in ((wsq, "wsq"), (wsk, "wsk"), (wsv, "wsv"), (wso, "wso")):
                        square(w, io[a]).then_inc(w_loaded["C"], DMA)
                    for b, a in ((bsq, "bsq"), (bsk, "bsk")):
                        column(b, io[a]).then_inc(w_loaded["C"], DMA)
                    for b, a in ((bsv, "bsv"), (bso, "bso"), (gate_b, "gate_b"), (ln1_g, "ln1_g"), (ln1_b, "ln1_b"),
                                 (ln2_g, "ln2_g"), (ln2_b, "ln2_b")):
                        row(b, io[a]).then_inc(w_loaded["C"], DMA)
                    sp.dma_start(gate_w[:, :, :], io["gate_w"].rearrange("(c p) e -> p c e", p=P)).then_inc(w_loaded["C"], DMA)

            def turn(t):
                if t.active("N"):
                    load(t)
                for stage in ("AB", "C")[t.base] if t.base < 2 else ():
                    load_weights(stage)
                if t.base == 3:
                    for e in range(E):
                        sp.dma_start(hidden_w[:, :, e * F:(e + 1) * F],
                                     io["hidden_w"][e].rearrange("(c p) f -> p c f", p=P)).then_inc(moe_loaded, DMA)
                        load_output_w(e, 0, moe_loaded)
                        sp.dma_start(hidden_b[:, :, e:e + 1], io["hidden_b"][e].rearrange("(c p one) -> p c one", p=P, one=1),
                                     allow_slow_non_contiguous=True).then_inc(moe_loaded, DMA)
                if t.base == NB + ATTENTION.lag["A"]:
                    sp.wait_ge(normed["N"], NB)
                    for step in ("A.xT", "A.ctxT", "A.v"):
                        sp.wait_ge(made[step], NB * ATTENTION.repeats[step])
                    sp.wait_ge(k_split, 3 * NB)
                    sp.wait_ge(q_split, 4 * NB)
                    for k in range(2):
                        sp.wait_ge(spread["A"][k], NB // 2 * SPREADS["A"] * DMA)
                    for e in range(E):
                        load_output_w(e, 1, output_w_loaded)
                    sp.dma_start(output_b[:, :], io["output_b"].rearrange("e d -> (e d)").partition_broadcast(P)
                                 ).then_inc(output_b_loaded, DMA)
                if t.active("B"):
                    n, k = t.item("B"), t.parity("B")
                    if t.later("B", 2):
                        sp.wait_ge(resid, t.item("B", 1, -1))
                    sp.dma_start(x_res[:, k, :], io["x"][bass.ds(n * T, T), :]).then_inc(res_loaded[k], DMA)
                move_parts(t)
                if t.active("F"):
                    n, k = t.item("F"), t.parity("F")
                    sp.wait_ge(shifted, t.item("F", 1, 1))
                    sp.dma_start(kept_rows(n, AT_X1), x1_shift[:, k, :]).then_inc(x1_stored[k], DMA)

            sp.wait_ge(ones_set, 1)
            for s in "AC":
                row_of = k_stack[s][STACK:STACK + 1, :, :, :].rearrange("p k h s -> p (k h s)")
                rows = S // 3 if s == "A" else T
                sp.dma_start(row_of, minus_ones[0:rows, 0:row_of.shape[1] // rows]).then_inc(last_rows_set, DMA)
            ATTENTION.run(sp, turn)
            attention_over(sp)
            sp.wait_ge(zero_set, 1)
            sp.wait_ge(plan_steps, 1)
            for e in range(E):
                row_no = sp.value_load(next_i[0:1, e:e + 1], min_val=e * REGION, max_val=e * REGION + NB * T)
                sp.dma_start(io["sent"][bass.ds(row_no, P), :], zero_rows[:, :]).then_inc(tails_zeroed, DMA)
            sp.wait_ge(tails_zeroed, E * DMA)
            sp.wait_ge(table_ready, 1)

            def expert_turn(t):
                if t.active("A"):
                    n, k = t.item("A"), t.parity("A")
                    first = sp.value_load(table[0:1, bass.ds(n + NT, 1)], min_val=0, max_val=E * REGION - P)
                    if t.later("A", 2):
                        sp.wait_ge(ex_made["A.x"], t.item("A", 1, -1))
                        sp.wait_ge(tile_kept, t.item("A", 1, -1))
                    sp.dma_start(tile_in[:, k, :], io["sent"][bass.ds(first, P), :]).then_inc(tile_loaded[k], DMA)

            EXPERTS.run(sp, expert_turn)
            experts_over(sp)
            for k in range(2):
                sp.wait_ge(x1_stored[k], NB // 2 * DMA)
                sp.wait_ge(xm_stored[k], NB // 2 * DMA)

            def join_turn(t):
                if t.active("A"):
                    n, k = t.item("A"), t.parity("A")
                    if t.later("A", 2):
                        sp.wait_ge(join_steps, t.item("A", 5, -8))
                    sp.dma_start(join_in[:, k, :, :], kept[bass.ds(n * P, P), 0:AT_X1, :]).then_inc(join_loaded[k], DMA)
                    if t.later("A", 2):
                        sp.wait_ge(result_steps, t.item("A", 2, -2))
                    sp.dma_start(x1_in[:, k, :], kept[bass.ds(n * P, P), AT_X1, :]).then_inc(x1_loaded[k], DMA)

            JOIN.run(sp, join_turn)

        @block.gpsimd
        def _(pool):
            pool.memset(ident[:, :], 0.0).then_inc(zeroed, 1)
            pool.memset(below[:, :], 1.0).then_inc(zeroed, 1)
            pool.memset(ones[:, :], 1.0).then_inc(zeroed, 1)
            pool.memset(spare_dve[:, :], 0.0).then_inc(zeroed, 1)
            pool.memset(zero[:, :], 0.0).then_inc(zeroed, 1)
            pool.memset(minus_ones[:, :], -1.0).then_inc(ones_set, 1)
            pool.memset(spare_pool[:, :], 0.0).then_inc(zeroed, 1)
            pool.memset(minus_half[:, :], -0.5).then_inc(consts, 1)
            pool.wait_ge(zeroed, 6)
            pool.affine_select(out=ident[:, :], in_=ident[:, :], compare_op=ALU.not_equal, fill=1.0, base=0,
                               pattern=[[-1, P]], channel_multiplier=1).then_inc(consts, 1)
            pool.affine_select(out=below[:, :], in_=below[:, :], compare_op=ALU.is_gt, fill=0.0, base=0,
                               pattern=[[1, P]], channel_multiplier=-1).then_inc(consts, 1)
            pool.iota(count_up[:, :], pattern=[[1, E]], base=0, channel_multiplier=0).then_inc(consts, 1)
            pool.iota(tile_no[:, :], pattern=[[0, 1]], base=0, channel_multiplier=1).then_inc(consts, 1)
            pool.iota(back_i[:, :], pattern=[[1, TOP]], base=1, channel_multiplier=KEPT).then_inc(consts, 1)
            pool.wait_ge(consts, 6)

            def invert(t, s):
                pool.wait_ge(measured[s], t.item(s, 3, 3))
                if t.later(s, 1):
                    if s == "E":
                        pool.wait_ge(gained, t.item(s, 2))
                    else:
                        pool.wait_ge(normed[s], t.item(s))
                pool.tensor_tensor(inv_std[s][:, :], moments[s][:, 1:2], minus_half[0:T, :],
                                   ALU.pow).then_inc(inverted[s], 1)

            def split(t, s, source, rest, zeros, steps, high, mid, low):
                step = lambda i: pool.wait_ge(steps, t.item(s, 4, i))
                pool.tensor_tensor(high, source, zeros, ALU.add).then_inc(steps, 1)
                step(1)
                pool.tensor_tensor(rest, source, high, ALU.subtract).then_inc(steps, 1)
                step(2)
                pool.tensor_tensor(mid, rest, zeros, ALU.add).then_inc(steps, 1)
                step(3)
                pool.tensor_tensor(low, rest, mid, ALU.subtract).then_inc(steps, 1)

            def turn(t):
                for step in t.steps():
                    if step == "N.ln":
                        invert(t, "N")
                    elif step == "A.split":
                        pool.wait_ge(taken["A.q"], t.item("A", 1, 1))
                        stacks_free(pool, t, "A")
                        if t.later("A", 1):
                            pool.wait_ge(q_split, t.item("A", 4))
                            pool.wait_ge(spread["A"][1 - t.parity("A")], t.last().dmas("A", 1, SPREADS["A"]))
                        split(t, "A", q_f[:, :, :], q_rest[:, :, :],
                              zero[:, :].unsqueeze(2).to_broadcast([P, DC, T]), q_split, q_parts[:, 0, :, :],
                              q_parts[:, 1, :, :], q_parts[:, 2, :, :])
                    elif step == "C.split":
                        pool.wait_ge(taken["C.qk"], t.item("C", 2, 2))
                        stacks_free(pool, t, "C")
                        if t.later("C", 1):
                            pool.wait_ge(qk_split, t.item("C", 4))
                            pool.wait_ge(spread["C"][1 - t.parity("C")], t.last().dmas("C", 1, SPREADS["C"]))
                        split(t, "C", qk_f[:, :, :, :], qk_rest[:, :, :, :],
                              zero[:, :].unsqueeze(2).unsqueeze(3).to_broadcast([P, 2, DC, T]), qk_split,
                              qk_parts[:, 0:6:5, :, :], qk_parts[:, 1:5:3, :, :], qk_parts[:, 2:4, :, :])
                    elif step == "E.norm":
                        invert(t, "E")
                    elif step == "C.v":
                        k = t.parity("C")
                        if t.base == ATTENTION.lag["C"]:
                            pool.wait_ge(w_loaded["C"], W_COUNTS["C"] * DMA)
                        pool.wait_ge(normed["F"], t.item("C", 1, 1))
                        if t.later("C", 2):
                            pool.wait_ge(taken["E.out"], t.item("C", 1, -1))
                        pool.tensor_tensor(y_bias[:, k, :], y[:, k, :], bso[0:T, :], ALU.add).then_inc(y_biased, 1)
                    elif step == "E.send":
                        n, k = t.item("E"), t.parity("E")
                        pool.wait_ge(xm_copied, t.item("E", 1, 1))
                        pool.wait_ge(row_steps, t.item("E", 6, 6))
                        alone(pool, spare_pool)
                        for i in range(TOP):
                            pool.indirect_dma_start(out=io["sent"], out_offset=bass.IndirectOffsetOnAxis(
                                ap=send_row[:, k, i:i + 1], axis=0), in_=xm[:, k, i, :], in_offset=None).then_inc(sent[k], DMA)
                    elif step == "F.norm":
                        invert(t, "F")

            ATTENTION.run(pool, turn)
            attention_over(pool)
            pool.memset(zero_rows[:, :], 0.0).then_inc(zero_set, 1)

            def expert_turn(t):
                if t.active("D"):
                    k = t.parity("D")
                    if t.later("D", 1):
                        pool.wait_ge(scatter_begun, t.item("D"))
                    pool.wait_ge(spill_steps, t.item("D", 3, 3))
                    pool.wait_ge(tile_done, t.item("D", 1, 1))
                    alone(pool, spare_pool).then_inc(scatter_begun, 1)
                    pool.indirect_dma_start(out=io["kept"], out_offset=bass.IndirectOffsetOnAxis(
                        ap=take_back[:, k, :], axis=0), in_=tile_out[:, k, :], in_offset=None).then_inc(out_stored[k], DMA)

            EXPERTS.run(pool, expert_turn)

            def join_turn(t):
                if t.active("B"):
                    k = t.parity("B")
                    pool.wait_ge(join_steps, t.item("B", 5, 5))
                    if t.later("B", 2):
                        pool.wait_ge(result_steps, t.item("B", 2, -2))
                    pool.tensor_tensor(join_inv[:, k, :], join_moments[:, k, 1:2], minus_half[:, :],
                                       ALU.pow).then_inc(join_inverted, 1)

            JOIN.run(pool, join_turn)

        @block.scalar
        def _(act):
            def drain(t, step, out, in_, bias=None, last=True, first=True):
                if first:
                    act.wait_ge(made[kind_of(step)], t.count(step))
                if bias is None:
                    ins = act.activation(out, in_, ACT.Copy)
                else:
                    ins = act.activation(out, in_, ACT.Identity, bias=bias)
                if last:
                    ins.then_inc(taken[kind_of(step)], 1)

            def exps(t, step, rows):
                act.wait_ge(made[kind_of(step)], t.count(step))
                last = t.before("probs", step)
                if last is not None:
                    pv = last[1].replace(".s", ".pv") if last[1][0] == "B" else "D.pv"
                    act.wait_ge(made[kind_of(pv)], last[0].count(pv))
                act.activation(probs[0:rows, t.buffer("probs", step), :],
                               score[t.buffer("score", step)][0:rows, 0:GT], ACT.Exp,
                               scale=SCALE).then_inc(taken[kind_of(step)], 1)

            def turn(t):
                weights(act, t, "A", "B", "C")
                if t.base == ATTENTION.lag["B"]:
                    act.activation(tanh_g[:, :], gates[:, :], ACT.Tanh).then_inc(tanh_done, 1)
                for step in t.steps():
                    s, kind = step[0], kind_of(step)
                    k, bank = t.parity(s), bank_of(t, step)
                    n1 = lambda: t.item(s)
                    if kind == "A.ctxT":
                        c = index_of(step)
                        if t.later("A", 1):
                            act.wait_ge(made["A.v"], t.item("A", ATTENTION.repeats["A.v"]))
                        drain(t, step, ctxT[:, c, :], bank[:, 0:S])
                    elif step == "A.xT":
                        if t.later("A", 1):
                            act.wait_ge(made["A.q"], n1())
                        drain(t, step, x_normT[:, :, :].rearrange("p c t -> p (c t)"), bank[:, 0:DC * T])
                    elif kind == "A.k":
                        c = index_of(step)
                        if t.later("A", 1):
                            act.wait_ge(k_split, t.item("A", 3))
                            act.wait_ge(spread["A"][1 - k], t.last().dmas("A", 1, SPREADS["A"]))
                        drain(t, step, k_f[:, c, :], bank[:, 0:S], bxk[:, c:c + 1], last=False)
                        drain(t, step, k_parts[:, PARTS - 1, c, :], bank[:, 0:S], bxk[:, c:c + 1], first=False)
                    elif step == "A.q":
                        if t.later("A", 1):
                            act.wait_ge(q_split, t.item("A", 4))
                        for c in range(DC):
                            drain(t, step, q_f[:, c, :], bank[:, c * T:(c + 1) * T], bxq[:, c:c + 1],
                                  last=c == DC - 1, first=c == 0)
                    elif step == "C.yT":
                        if t.later("C", 1):
                            act.wait_ge(made["C.v"], n1())
                        drain(t, step, yT[:, :, :].rearrange("p c t -> p (c t)"), bank[:, 0:DC * T])
                    elif kind == "C.qk":
                        i = index_of(step)
                        if t.later("C", 1):
                            act.wait_ge(qk_split, t.item("C", 4))
                        for c in range(DC):
                            drain(t, step, qk_f[:, i, c, :], bank[:, c * T:(c + 1) * T], (bsq, bsk)[i][:, c:c + 1],
                                  last=c == DC - 1, first=c == 0)
                    elif step == "E.xT":
                        act.wait_ge(gained, t.item("E", 2, 2))
                        if t.later("E", 2):
                            act.wait_ge(sent[k], t.dmas("E", 0, TOP))
                        act.activation(xm[:, k, 1, 0:D], xm[:, k, 0, 0:D], ACT.Copy).then_inc(xm_copied, 1)
                        if t.later("E", 1):
                            act.wait_ge(made["E.gate"], n1())
                        drain(t, step, xmT[:, :, :].rearrange("p c t -> p (c t)"), bank[:, 0:DC * T])
                    elif step == "E.gate":
                        act.wait_ge(gate_steps, t.item("E", 9, 2))
                        act.activation(gate_exp[:, :], logits[:, :], ACT.Exp, bias=minus_max[:, :],
                                       accum_out=gate_sum[:, :]).then_inc(gates_exped, 1)
                    elif kind == "B.s":
                        exps(t, step, SC)
                    elif kind == "D.s":
                        exps(t, step, T)
                    elif step in ("B.pv11", "D.pv"):
                        o = "F" if s == "B" else "E"
                        act.wait_ge(made[kind], t.count(step))
                        if t.later(s, 1):
                            act.wait_ge(made[o + ".oN"], n1())
                        act.activation(outT[o][:, :], (sums if s == "B" else bank)[:, 0:GT], ACT.Copy).then_inc(taken[kind], 1)
                    elif kind in ("F.aT", "E.aT"):
                        if t.later(s, 1):
                            act.wait_ge(made[s + ".out"], n1())
                        drain(t, step, attT[s][:, :, :].rearrange("p c t -> p (c t)"), bank[:, 0:DC * T])

            ATTENTION.run(act, turn)
            attention_over(act)

            def expert_turn(t):
                if t.active("A"):
                    k = t.parity("A")
                    act.wait_ge(ex_made["A.x"], t.item("A", 1, 1))
                    if t.later("A", 2):
                        act.wait_ge(ex_made["B.h"], t.item("A", 1, -1))
                    act.activation(tile_inT[:, k, :, :].rearrange("p c t -> p (c t)"), rows_bank[k][:, 0:D],
                                   ACT.Copy).then_inc(ex_taken["A.x"], 1)
                if t.active("B"):
                    k = t.parity("B")
                    act.wait_ge(ex_made["B.h"], t.item("B", 1, 1))
                    if t.later("B", 2):
                        act.wait_ge(ex_made["C.hT"], t.item("B", 1, -1))
                    act.activation(hidden[:, k, :], hidden_bank[k][:, 0:F], ACT.Copy).then_inc(ex_taken["B.h"], 1)
                if t.active("D"):
                    k = t.parity("D")
                    act.wait_ge(tile_moved, t.item("D", 1, 1))
                    act.wait_ge(ex_taken["D.y"], t.item("D", 1, 1))
                    if t.later("D", 2):
                        act.wait_ge(out_stored[k], t.dmas("D", 0))
                    act.activation(tile_out[:, k, :], tile_sum[:, k, :], ACT.Copy, scale=tile_ends[:, k, 0:1]).then_inc(tile_done, 1)

            EXPERTS.run(act, expert_turn)

            def join_turn(t):
                if t.active("B"):
                    n, k = t.item("B"), t.parity("B")
                    act.wait_ge(result_steps, t.item("B", 2, 2))
                    act.dma_start(io["out"][bass.ds(n * P, P), :], result[:, k, :]).then_inc(result_stored[k], DMA)

            JOIN.run(act, join_turn)
            for k in range(2):
                act.wait_ge(result_stored[k], JT // 2 * DMA)

        @block.vector
        def _(dve):
            dve.wait_ge(consts, 6)
            for k in range(2):
                dve.memset(values["A"][:, k, :, :, :], 0.0).then_inc(vset, 1)
                dve.memset(values["C"][:, k, :, :, :], 0.0).then_inc(vset, 1)
            dve.wait_ge(vset, 4)
            for k in range(2):
                dve.memset(values["A"][:, k, :, :, HD:HD + 1], 1.0).then_inc(vset, 1)
                dve.memset(values["C"][:, k, :, :, HD:HD + 1], 1.0).then_inc(vset, 1)
            dve.wait_ge(vset, 8)

            def measure(t, s, src):
                if t.later(s, 1):
                    if s == "E":
                        dve.wait_ge(gained, t.item(s, 2))
                    else:
                        dve.wait_ge(normed[s], t.item(s))
                dve.bn_stats(stats[s][:, :], src).then_inc(measured[s], 1)
                dve.wait_ge(measured[s], t.item(s, 3, 1))
                alone(dve, spare_dve)
                dve.bn_aggr(moments[s][:, :], stats[s][:, :]).then_inc(measured[s], 1)
                dve.wait_ge(measured[s], t.item(s, 3, 2))
                dve.tensor_scalar(moments[s][:, 1:2], moments[s][:, 1:2], EPS, None, ALU.add).then_inc(measured[s], 1)

            def normalize(t, s, src, dst):
                dve.wait_ge(inverted[s], t.item(s, 1, 1))
                dve.tensor_scalar(dst, src, moments[s][:, 0:1], inv_std[s][:, :], ALU.subtract,
                                  ALU.mult).then_inc(normed[s], 1)

            def average(t, s):
                step = s + ".oN"
                dve.wait_ge(made[step], t.count(step))
                heads = bank_of(t, step)[0:T, :].rearrange("t (h w) -> t h w", w=VW)
                if t.later(s, 1):
                    dve.wait_ge(made[s + ".aT"], t.item(s))
                dve.reciprocal(inv_sum[s][:, :].unsqueeze(2), heads[:, :, HD:HD + 1]).then_inc(inv_sums[s], 1)
                dve.wait_ge(inv_sums[s], t.item(s, 1, 1))
                dve.tensor_tensor(att[s][:, :].rearrange("t (h w) -> t h w", w=HD), heads[:, :, 0:HD],
                                  inv_sum[s][:, :].unsqueeze(2).to_broadcast([T, H, HD]),
                                  ALU.mult).then_inc(taken[step], 1)

            def turn(t):
                weights(dve, t, "A", "B")
                if t.base == ATTENTION.lag["B"]:
                    dve.wait_ge(tanh_done, 1)
                    dve.wait_ge(w_loaded["C"], W_COUNTS["C"] * DMA)
                    for out, a in ((ln2_gain, ln2_g), (ln2_shift, ln2_b)):
                        dve.tensor_scalar(out[:, :], a[:, :], tanh_g[:, 1:2], None, ALU.mult).then_inc(vset, 1)
                    dve.wait_ge(vset, 15)
                for step in t.steps():
                    s, kind = step[0], kind_of(step)
                    k, bank = t.parity(s), bank_of(t, step)
                    if step == "N.ln":
                        dve.wait_ge(x_loaded[k], t.dmas("N"))
                        if t.later("N", 1):
                            dve.wait_ge(made["A.xT"], t.item("N"))
                        measure(t, "N", x_in[:, k, :])
                        normalize(t, "N", x_in[:, k, :], x_norm[:, :])
                    elif kind == "A.v":
                        dve.wait_ge(made["A.v"], t.count(step))
                        if t.later("A", 2):
                            dve.wait_ge(made["B.pv"], t.item("A", ATTENTION.repeats["B.pv"], -ATTENTION.repeats["B.pv"]))
                        j, n = ((0, 2), (2, 1))[index_of(step)]
                        dve.tensor_tensor(values["A"][:, k, j:j + n, :, 0:HD],
                                          bank[0:SC, 0:n * D].rearrange("s (j h w) -> s j h w", j=n, w=HD),
                                          bxv[0:SC, :].rearrange("s (h w) -> s h w", w=HD).unsqueeze(1)
                                          .to_broadcast([SC, n, H, HD]), ALU.add).then_inc(taken["A.v"], 1)
                    elif step == "A.split":
                        steps = lambda i: dve.wait_ge(k_split, t.item("A", 3, i))
                        dve.wait_ge(taken["A.k"], t.item("A", DC, DC))
                        stacks_free(dve, t, "A")
                        if t.later("A", 1):
                            steps(0)
                            dve.wait_ge(spread["A"][1 - k], t.last().dmas("A", 1, SPREADS["A"]))
                        dve.tensor_tensor(k_rest[:, :, :], k_f[:, :, :], k_parts[:, 2, :, :], ALU.subtract).then_inc(k_split, 1)
                        steps(1)
                        dve.tensor_copy(k_parts[:, 1, :, :], k_rest[:, :, :]).then_inc(k_split, 1)
                        steps(2)
                        dve.tensor_tensor(k_parts[:, 0, :, :], k_rest[:, :, :], k_parts[:, 1, :, :],
                                          ALU.subtract).then_inc(k_split, 1)
                    elif step == "C.v":
                        dve.wait_ge(made["C.v"], t.count(step))
                        if t.later("C", 2):
                            dve.wait_ge(made["D.pv"], t.item("C", ATTENTION.repeats["D.pv"], -ATTENTION.repeats["D.pv"]))
                        dve.tensor_tensor(values["C"][:, k, 0, :, 0:HD],
                                          bank[0:T, 0:D].rearrange("s (h w) -> s h w", w=HD),
                                          bsv[0:T, :].rearrange("s (h w) -> s h w", w=HD),
                                          ALU.add).then_inc(taken["C.v"], 1)
                    elif kind == "A.max":
                        i = index_of(step)
                        dve.wait_ge(made[kind], t.count(step))
                        if i == 0 and t.later("A", 1):
                            dve.wait_ge(made["A.mT"], t.item("A"))
                        dve.tensor_reduce(row_max["A"][:, i:i + 1], max_banks[t.buffer("max", step)][0:T, 0:S], AX_X,
                                          ALU.max).then_inc(taken[kind], 1)
                    elif kind == "C.max":
                        i = index_of(step)
                        dve.wait_ge(made[kind], t.count(step))
                        if i == 0 and t.later("C", 1):
                            dve.wait_ge(made["C.mT"], t.item("C"))
                        dve.tensor_reduce(row_max["C"][:, G * i:G * (i + 1)],
                                          max_banks[t.buffer("max", step)][0:T, 0:GT].rearrange("t (h s) -> t h s", s=T),
                                          AX_X, ALU.max).then_inc(taken[kind], 1)
                    elif kind in ("A.mT", "C.mT"):
                        dve.wait_ge(made[kind], t.count(step))
                        if t.later(s, 2):
                            dve.wait_ge(topped[s][k], t.dmas(s, 0))
                        dve.tensor_copy(maxT[s][:, k, :], bank[0:H, 0:T]).then_inc(taken[kind], 1)
                    elif kind in ("F.oN", "E.oN"):
                        average(t, s)
                    elif step == "E.gate":
                        dve.wait_ge(made["E.gate"], t.count(step))
                        if t.later("E", 1):
                            dve.wait_ge(gates_exped, t.item("E"))
                        dve.tensor_tensor(logits[:, :], bank[0:T, 0:E], gate_b[0:T, :], ALU.add).then_inc(taken["E.gate"], 1)
                        dve.wait_ge(taken["E.gate"], t.count(step))
                        alone(dve, spare_dve)
                        dve.max(top_logits[:, :], logits[:, :]).then_inc(gate_steps, 1)
                        dve.wait_ge(gate_steps, t.item("E", 9, 1))
                        dve.tensor_scalar(minus_max[:, :], top_logits[:, 0:1], -1.0, None, ALU.mult).then_inc(gate_steps, 1)
                    elif step == "E.pick":
                        dve.wait_ge(gates_exped, t.item("E", 1, 1))
                        dve.reciprocal(gate_inv[:, :], gate_sum[:, :]).then_inc(gate_steps, 1)
                        dve.wait_ge(gate_steps, t.item("E", 9, 3))
                        dve.tensor_scalar(gate[:, :], gate_exp[:, :], gate_inv[:, :], None, ALU.mult).then_inc(gate_steps, 1)
                        dve.wait_ge(gate_steps, t.item("E", 9, 4))
                        alone(dve, spare_dve)
                        dve.max(top_gate[:, :], gate[:, :]).then_inc(gate_steps, 1)
                        dve.wait_ge(gate_steps, t.item("E", 9, 5))
                        alone(dve, spare_dve)
                        dve.max_index(top_expert[:, :], top_gate[:, :], gate[:, :]).then_inc(gate_steps, 1)
                        dve.wait_ge(gate_steps, t.item("E", 9, 6))
                        if t.later("E", 1):
                            dve.wait_ge(made["E.rank"], t.item("E"))
                            dve.wait_ge(row_steps, t.item("E", 6))
                        dve.tensor_copy(route[:, TOP:2 * TOP], top_expert[:, 0:TOP]).then_inc(gate_steps, 1)
                        dve.wait_ge(gate_steps, t.item("E", 9, 7))
                        for i in range(TOP):
                            ins = dve.tensor_scalar(chosen[:, i, :], expert_ids[0:T, :], route[:, TOP + i:TOP + i + 1], None,
                                                    ALU.is_equal)
                        ins.then_inc(gate_steps, 1)
                        dve.wait_ge(gate_steps, t.item("E", 9, 8))
                        dve.tensor_tensor(chosen_any[:, :], chosen[:, 0, :], chosen[:, 1, :], ALU.add).then_inc(gate_steps, 1)
                        if t.later("E", 2):
                            dve.wait_ge(sent[k], t.dmas("E", 0, TOP))
                        dve.tensor_copy(xm[:, k, :, AT_GATE:AT_GATE + 1], top_gate[:, 0:TOP].unsqueeze(2)).then_inc(row_steps, 1)
                        if t.later("E", 1):
                            dve.wait_ge(back_moved, t.item("E"))
                        dve.tensor_copy(xm[:, k, :, AT_BACK:AT_BACK + 1], back_row[:, :].unsqueeze(2)).then_inc(row_steps, 1)
                        dve.wait_ge(row_steps, t.item("E", 6, 2))
                        dve.tensor_scalar(back_row[:, :], back_row[:, :], float(KEPT * T), None, ALU.add).then_inc(back_moved, 1)
                    elif step == "E.rank":
                        dve.wait_ge(made["E.rank"], t.count(step))
                        dve.tensor_tensor(rows_here[:, :], bank[0:T, 0:E], next_row[0:T, :], ALU.add).then_inc(row_steps, 1)
                        dve.wait_ge(row_steps, t.item("E", 6, 3))
                        dve.tensor_tensor(next_row[:, :], bank[:, E:2 * E], next_row[:, :], ALU.add).then_inc(taken["E.rank"], 1)
                        dve.wait_ge(taken["E.rank"], t.count(step))
                        dve.tensor_tensor(rows_pick[:, :, :], chosen[:, :, :], rows_here[:, :].unsqueeze(1)
                                          .to_broadcast([T, TOP, E]), ALU.mult).then_inc(row_steps, 1)
                        dve.wait_ge(row_steps, t.item("E", 6, 4))
                        dve.tensor_reduce(route[:, 0:TOP], rows_pick[:, :, :], AX_X, ALU.add).then_inc(row_steps, 1)
                        dve.wait_ge(row_steps, t.item("E", 6, 5))
                        dve.tensor_copy(send_row[:, k, :], route[:, 0:TOP]).then_inc(row_steps, 1)
                    elif step == "F.out":
                        dve.wait_ge(made["F.out"], t.count(step))
                        if t.later("F", 1):
                            dve.wait_ge(resid, t.item("F"))
                        dve.tensor_tensor(proj[:, :], bank[0:T, 0:D], bxo[0:T, :], ALU.add).then_inc(taken["F.out"], 1)
                        dve.wait_ge(taken["F.out"], t.count(step))
                        dve.wait_ge(res_loaded[k], t.dmas("F"))
                        if t.later("F", 2):
                            dve.wait_ge(normed["F"], t.item("F", 1, -1))
                        dve.scalar_tensor_tensor(x1[:, k, :], proj[:, :], tanh_g[0:T, 0:1], x_res[:, k, :],
                                                 ALU.mult, ALU.add).then_inc(resid, 1)
                        dve.wait_ge(resid, t.item("F", 1, 1))
                        measure(t, "F", x1[:, k, :])
                        if t.later("F", 2):
                            dve.wait_ge(x1_stored[k], t.dmas("F", 0))
                        dve.tensor_tensor(x1_shift[:, k, :], x1[:, k, :], ln2_shift[0:T, :], ALU.add).then_inc(shifted, 1)
                    elif step == "F.norm":
                        if t.later("F", 2):
                            dve.wait_ge(made["C.yT"], t.item("F", 1, -1))
                            dve.wait_ge(y_biased, t.item("F", 1, -1))
                        normalize(t, "F", x1[:, k, :], y[:, k, :])
                    elif step == "E.out":
                        dve.wait_ge(made["E.out"], t.count(step))
                        dve.wait_ge(y_biased, t.item("E", 1, 1))
                        if t.later("E", 1):
                            dve.wait_ge(gained, t.item("E", 2))
                        dve.tensor_tensor(r[:, :], bank[0:T, 0:D], y_bias[:, k, :], ALU.add).then_inc(taken["E.out"], 1)
                        dve.wait_ge(taken["E.out"], t.count(step))
                        measure(t, "E", r[:, :])
                    elif step == "E.norm":
                        if t.later("E", 1):
                            dve.wait_ge(gained, t.item("E", 2))
                        dve.scalar_tensor_tensor(r_gain[:, :], r[:, :], moments["E"][:, 0:1], ln1_g[0:T, :],
                                                 ALU.subtract, ALU.mult).then_inc(gained, 1)
                        dve.wait_ge(gained, t.item("E", 2, 1))
                        dve.wait_ge(inverted["E"], t.item("E", 1, 1))
                        if t.later("E", 2):
                            dve.wait_ge(xm_stored[k], t.dmas("E", 0))
                            dve.wait_ge(sent[k], t.dmas("E", 0, TOP))
                            dve.wait_ge(xm_copied, t.item("E", 1, -1))
                        dve.scalar_tensor_tensor(xm[:, k, 0, 0:D], r_gain[:, :], inv_std["E"][:, :], ln1_b[0:T, :],
                                                 ALU.mult, ALU.add).then_inc(gained, 1)

            dve.wait_ge(consts, 6)
            dve.tensor_copy(expert_ids[:, :], count_up[:, :]).then_inc(vset, 1)
            dve.wait_ge(vset, 9)
            dve.tensor_scalar(region_of[:, :], expert_ids[:, :], float(REGION), None, ALU.mult).then_inc(vset, 1)
            dve.wait_ge(vset, 10)
            dve.tensor_copy(next_row[:, :], region_of[:, :]).then_inc(vset, 1)
            dve.tensor_copy(back_row[:, :], back_i[:, :]).then_inc(vset, 1)
            dve.tensor_scalar(spill_row[:, :], tile_no[:, :], float(SPILL + 1), None, ALU.add).then_inc(vset, 1)
            dve.wait_ge(vset, 13)
            ATTENTION.run(dve, turn)
            attention_over(dve)

            def step(*waits):
                dve.wait_ge(plan_steps, *waits)

            dve.tensor_copy(next_i[:, :], next_row[:, :]).then_inc(plan_steps, 1)
            dve.tensor_tensor(counts[:, :], next_row[:, :], region_of[:, :], ALU.subtract).then_inc(plan_steps, 1)
            dve.memset(ones_f[:, :], 1.0).then_inc(plan_steps, 1)
            dve.tensor_copy(tile_f[:, :], tile_no[:, :]).then_inc(plan_steps, 1)
            step(4)
            dve.tensor_scalar(tiles_i[:, :], counts[:, :], float(P - 1), None, ALU.add).then_inc(plan_steps, 1)
            step(5)
            dve.tensor_scalar(tiles_i[:, :], tiles_i[:, :], P.bit_length() - 1, None, ALU.arith_shift_right).then_inc(plan_steps, 1)
            step(6)
            dve.tensor_copy(tiles[:, :], tiles_i[:, :]).then_inc(plan_steps, 1)
            step(7)
            dve.tensor_tensor_scan(tiles_end[:, :], ones_f[:, :], tiles[:, :], 0.0, ALU.mult, ALU.add).then_inc(plan_steps, 1)
            step(8)
            dve.tensor_scalar(past[:, :], tiles_end[:, :], tile_f[:, :], None, ALU.is_le).then_inc(plan_steps, 1)
            dve.tensor_tensor(count_step[:, 0:E - 1], counts[:, 1:E], counts[:, 0:E - 1], ALU.subtract).then_inc(plan_steps, 1)
            step(10)
            for i, (w, out) in enumerate(((ones_f, tile_expert), (tiles, tile_base), (count_step, tile_count))):
                dve.tensor_tensor_reduce(junk[:, i, 0:E - 1], past[:, 0:E - 1], w[:, 0:E - 1], 1.0, 0.0, ALU.mult, ALU.add,
                                         out[:, :]).then_inc(plan_steps, 1)
            step(13)
            dve.tensor_tensor(tile_row[:, :], tile_f[:, :], tile_base[:, :], ALU.subtract).then_inc(plan_steps, 1)
            dve.tensor_tensor(tile_rest[:, :], tile_count[:, :], counts[:, 0:1], ALU.add).then_inc(plan_steps, 1)
            step(15)
            dve.scalar_tensor_tensor(tile_row[:, :], tile_row[:, :], float(P), tile_rest[:, :], ALU.mult,
                                     ALU.min).then_inc(plan_steps, 1)
            step(16)
            dve.scalar_tensor_tensor(tile_row[:, :], tile_expert[:, :], float(REGION), tile_row[:, :], ALU.mult,
                                     ALU.add).then_inc(plan_steps, 1)
            dve.wait_ge(table_turned, 1)
            dve.tensor_copy(table[:, :], rows_bank[0][0:1, 0:2 * NT]).then_inc(table_ready, 1)
            dve.wait_ge(output_b_loaded, DMA)
            dve.wait_ge(moe_loaded, 3 * E * DMA)
            dve.wait_ge(table_ready, 1)

            def expert_turn(t):
                if t.active("C"):
                    n, k = t.item("C"), t.parity("C")
                    e = dve.value_load(table[0:1, bass.ds(n, 1)], min_val=0, max_val=E - 1)
                    dve.wait_ge(tile_kept, t.item("C", 1, 1))
                    if t.later("C", 2):
                        dve.wait_ge(tile_done, t.item("C", 1, -1))
                        dve.wait_ge(spill_steps, t.item("C", 3, -3))
                    dve.tensor_copy(tile_ends[:, k, :], tile_meta[:, k, :]).then_inc(tile_moved, 1)
                    dve.wait_ge(ex_made["C.hT"], t.item("C", 1, 1))
                    if t.later("C", 2):
                        dve.wait_ge(ex_made["D.y"], t.item("C", 1, -1))
                    for f in range(FC):
                        ins = dve.tensor_scalar(hiddenT[:, k, f, :], score[k][:, f * P:(f + 1) * P],
                                                hidden_b[:, f, bass.ds(e, 1)], 0.0, ALU.add, ALU.max)
                    ins.then_inc(ex_taken["C.hT"], 1)
                if t.active("D"):
                    n, k = t.item("D"), t.parity("D")
                    e = dve.value_load(table[0:1, bass.ds(n, 1)], min_val=0, max_val=E - 1)
                    dve.wait_ge(tile_moved, t.item("D", 1, 1))
                    dve.wait_ge(ex_made["D.y"], t.item("D", 1, 1))
                    if t.later("D", 2):
                        dve.wait_ge(tile_done, t.item("D", 1, -1))
                        dve.wait_ge(out_stored[k], t.dmas("D", 0))
                    if t.later("D", 1):
                        dve.wait_ge(spill_steps, t.item("D", 3))
                    dve.tensor_scalar(is_spill[:, :], tile_ends[:, k, 1:2], 0.0, spill_row[:, :], ALU.is_equal,
                                      ALU.mult).then_inc(spill_steps, 1)
                    dve.wait_ge(spill_steps, t.item("D", 3, 1))
                    dve.tensor_scalar(spill_row[:, :], spill_row[:, :], float(P), None, ALU.add).then_inc(spill_steps, 1)
                    dve.scalar_tensor_tensor(take_back[:, k, :], tile_ends[:, k, 1:2], -1.0, is_spill[:, :], ALU.add,
                                             ALU.add).then_inc(spill_steps, 1)
                    dve.tensor_tensor(tile_sum[:, k, :], output_bank[k][:, 0:D], output_b[:, bass.ds(e * D, D)],
                                      ALU.add).then_inc(ex_taken["D.y"], 1)

                if t.active("A"):
                    k = t.parity("A")
                    dve.wait_ge(tile_loaded[k], t.dmas("A"))
                    if t.later("A", 2):
                        dve.wait_ge(tile_moved, t.item("A", 1, -1))
                    dve.tensor_copy(tile_meta[:, k, :], tile_in[:, k, D:SENT]).then_inc(tile_kept, 1)

            EXPERTS.run(dve, expert_turn)

            def join_turn(t):
                a, b = t.active("A"), t.active("B")
                kA, kB = t.parity("A"), t.parity("B")
                a_done = lambda i: dve.wait_ge(join_steps, t.item("A", 5, i))
                b_done = lambda i: dve.wait_ge(result_steps, t.item("B", 2, i))
                if a:
                    dve.wait_ge(join_loaded[kA], t.dmas("A"))
                    if t.later("A", 2):
                        dve.wait_ge(result_steps, t.item("A", 2, -2))
                    dve.tensor_tensor(added[:, kA, 0, :], join_in[:, kA, 0, :], join_in[:, kA, 1, :],
                                      ALU.add).then_inc(join_steps, 1)
                if b:
                    if t.later("B", 1):
                        b_done(0)
                    dve.scalar_tensor_tensor(join_gain[:, :], added[:, kB, 1, :], join_moments[:, kB, 0:1], ln2_gain[:, :],
                                             ALU.subtract, ALU.mult).then_inc(result_steps, 1)
                if a:
                    a_done(1)
                    dve.tensor_tensor(added[:, kA, 1, :], join_in[:, kA, AT_XM, :], added[:, kA, 0, :],
                                      ALU.add).then_inc(join_steps, 1)
                if b:
                    b_done(1)
                    dve.wait_ge(join_inverted, t.item("B", 1, 1))
                    dve.wait_ge(x1_loaded[kB], t.dmas("B"))
                    if t.later("B", 2):
                        dve.wait_ge(result_stored[kB], t.dmas("B", 0))
                    dve.scalar_tensor_tensor(result[:, kB, :], join_gain[:, :], join_inv[:, kB, :], x1_in[:, kB, :],
                                             ALU.mult, ALU.add).then_inc(result_steps, 1)
                if a:
                    a_done(2)
                    dve.bn_stats(join_stats[:, :], added[:, kA, 1, :]).then_inc(join_steps, 1)
                    a_done(3)
                    alone(dve, spare_dve)
                    dve.bn_aggr(join_moments[:, kA, :], join_stats[:, :]).then_inc(join_steps, 1)
                    a_done(4)
                    dve.tensor_scalar(join_moments[:, kA, 1:2], join_moments[:, kA, 1:2], EPS, None, ALU.add).then_inc(join_steps, 1)

            JOIN.run(dve, join_turn)

        @block.tensor
        def _(pe):
            def transpose_cols(t, step, src, rows, n):
                bank = bank_of(t, step)
                for c in range(n):
                    mm = pe.transpose(bank[:, c * rows:(c + 1) * rows], src[:, c * P:(c + 1) * P],
                                      ident[0:rows, 0:rows])
                mm.then_inc(made[kind_of(step)], 1)

            def project(out, w, actT, m):
                for c in range(DC):
                    mm = pe.matmul(out, w[:, c, m * P:(m + 1) * P], actT[:, c, :], start=c == 0, stop=c == DC - 1)
                return mm

            def scores(t, step, a, rows):
                i = index_of(step)
                g, j = i // (NSC if a == "A" else 1), i % (NSC if a == "A" else 1)
                k = t.parity(step[0])
                if i == 0:
                    pe.wait_ge(topped[a][k], t.dmas(step[0]))
                buffer_free(pe, t, "score", step, taken)
                b = score[t.buffer("score", step)]
                keys = slice(j * rows, (j + 1) * rows)
                for h in range(G):
                    mm = pe.matmul(b[0:rows, h * T:(h + 1) * T], k_stack[a][:, k, g * G + h, keys],
                                   q_stack[a][:, k, g * G + h, :], start=True, stop=True)
                mm.then_inc(made[kind_of(step)], 1)

            def weigh(t, of, a, rows, out):
                i, n = index_of(of), (NSC if a == "A" else 1)
                g, j = i // n, i % n
                k, b = t.parity(of[0]), t.buffer("probs", of)
                for h in range(G):
                    mm = pe.matmul(out[h * VW:(h + 1) * VW, g * T:(g + 1) * T], values[a][0:rows, k, j, g * G + h, :],
                                   probs[0:rows, b, h * T:(h + 1) * T], start=j == 0, stop=j == n - 1)
                return mm

            def turn(t):
                weights(pe, t, "A", "B", "C")
                if t.base == ATTENTION.lag["B"]:
                    pe.wait_ge(last_rows_set, 2 * DMA)
                for step in t.steps():
                    s, kind = step[0], kind_of(step)
                    k, bank = t.parity(s), bank_of(t, step)
                    bank = bank_of(t, step)
                    for pool in ("bank", "max"):
                        if kind in ATTENTION.pools[pool][1]:
                            buffer_free(pe, t, pool, step, taken)
                    if kind == "A.ctxT":
                        pe.wait_ge(ctx_loaded[k], t.dmas("A"))
                        c = index_of(step)
                        for j in range(NSC):
                            mm = pe.transpose(bank[:, j * SC:(j + 1) * SC], ctx_in[:, k, j, c * P:(c + 1) * P],
                                              ident[0:SC, 0:SC])
                        mm.then_inc(made[kind], 1)
                    elif step == "A.xT":
                        pe.wait_ge(normed["N"], t.item("A", 1, 1))
                        transpose_cols(t, step, x_norm, T, DC)
                    elif kind == "A.k":
                        pe.wait_ge(taken["A.ctxT"], t.item("A", DC, DC))
                        project(bank[:, 0:S], wxk, ctxT, index_of(step)).then_inc(made[kind], 1)
                    elif step == "A.q":
                        pe.wait_ge(taken["A.xT"], t.item("A", 1, 1))
                        for m in range(DC):
                            mm = project(bank[:, m * T:(m + 1) * T], wxq, x_normT, m)
                        mm.then_inc(made[kind], 1)
                    elif kind == "A.v":
                        first, n = ((0, 2), (2, 1))[index_of(step)]
                        for j in range(first, first + n):
                            for c in range(DC):
                                mm = pe.matmul(bank[0:SC, (j - first) * D:(j - first + 1) * D],
                                               ctxT[:, c, j * SC:(j + 1) * SC], wxv[:, c, :],
                                               start=c == 0, stop=c == DC - 1)
                        mm.then_inc(made[kind], 1)
                    elif kind == "A.max":
                        i = index_of(step)
                        if i == 0:
                            pe.wait_ge(stacked["A"][k], t.dmas("A", 1, STACKS))
                        mm = pe.matmul(max_banks[t.buffer("max", step)][0:T, 0:S], q_stack["A"][0:STACK, k, i, :],
                                       k_stack["A"][0:STACK, k, i, :], start=True, stop=True)
                        mm.then_inc(made[kind], 1)
                    elif kind == "C.max":
                        i = index_of(step)
                        if i == 0:
                            pe.wait_ge(stacked["C"][k], t.dmas("C", 1, STACKS))
                        for h in range(G):
                            mm = pe.matmul(max_banks[t.buffer("max", step)][0:T, h * T:(h + 1) * T],
                                           q_stack["C"][0:STACK, k, G * i + h, :],
                                           k_stack["C"][0:STACK, k, G * i + h, :], start=True, stop=True)
                        mm.then_inc(made[kind], 1)
                    elif kind in ("A.mT", "C.mT"):
                        pe.wait_ge(taken[s + ".max"], t.item(s, ATTENTION.repeats[s + ".max"], ATTENTION.repeats[s + ".max"]))
                        pe.transpose(bank[0:H, 0:T], row_max[s][:, :], ident[0:T, 0:T]).then_inc(made[kind], 1)
                    elif kind == "B.s":
                        scores(t, step, "A", SC)
                    elif kind == "D.s":
                        scores(t, step, "C", T)
                    elif kind == "B.pv":
                        of = step.replace(".pv", ".s")
                        pe.wait_ge(taken["B.s"], t.count(of))
                        if index_of(step) == 0 and t.later("B", 1):
                            pe.wait_ge(taken["B.pv"], t.item("B"))
                        weigh(t, of, "A", SC, sums).then_inc(made[kind], 1)
                    elif kind == "D.pv":
                        pe.wait_ge(taken["D.s"], t.item("D", NG, NG))
                        for g in range(NG):
                            mm = weigh(t, f"D.s{g}", "C", T, bank)
                        mm.then_inc(made[kind], 1)
                    elif kind in ("F.oN", "E.oN"):
                        pe.wait_ge(taken["B.pv" if s == "F" else "D.pv"], t.item(s, 1, 1))
                        for g in range(NG):
                            mm = pe.transpose(bank[0:T, g * P:(g + 1) * P], outT[s][:, g * T:(g + 1) * T], ident[:, :])
                        mm.then_inc(made[kind], 1)
                    elif kind in ("F.aT", "E.aT"):
                        pe.wait_ge(taken[s + ".oN"], t.item(s, 1, 1))
                        transpose_cols(t, step, att[s], T, DC)
                    elif kind in ("F.out", "E.out"):
                        pe.wait_ge(taken[s + ".aT"], t.item(s, 1, 1))
                        for c in range(DC):
                            mm = pe.matmul(bank[0:T, 0:D], attT[s][:, c, :], (wxo if s == "F" else wso)[:, c, :],
                                           start=c == 0, stop=c == DC - 1)
                        mm.then_inc(made[kind], 1)
                    elif step == "E.xT":
                        pe.wait_ge(gained, t.item("E", 2, 2))
                        transpose_cols(t, step, xm[:, k, 0, 0:D], T, DC)
                    elif step == "E.gate":
                        pe.wait_ge(taken["E.xT"], t.item("E", 1, 1))
                        for c in range(DC):
                            mm = pe.matmul(bank[0:T, 0:E], xmT[:, c, :], gate_w[:, c, :], start=c == 0, stop=c == DC - 1)
                        mm.then_inc(made[kind], 1)
                    elif step == "E.rank":
                        pe.wait_ge(gate_steps, t.item("E", 9, 9))
                        pe.matmul(bank[0:T, 0:E], below[0:T, 0:T], chosen_any[:, :], start=True, stop=True)
                        pe.matmul(bank[:, E:2 * E], ones[0:T, :], chosen_any[:, :], start=True, stop=True,
                                  skip_group_check=True).then_inc(made[kind], 1)
                    elif step == "C.yT":
                        pe.wait_ge(normed["F"], t.item("C", 1, 1))
                        transpose_cols(t, step, y[:, k, :], T, DC)
                    elif kind == "C.qk":
                        pe.wait_ge(taken["C.yT"], t.item("C", 1, 1))
                        for m in range(DC):
                            mm = project(bank[:, m * T:(m + 1) * T], (wsq, wsk)[index_of(step)], yT, m)
                        mm.then_inc(made[kind], 1)
                    elif step == "C.v":
                        for c in range(DC):
                            mm = pe.matmul(bank[0:T, 0:D], yT[:, c, :], wsv[:, c, :], start=c == 0, stop=c == DC - 1)
                        mm.then_inc(made[kind], 1)

            pe.wait_ge(consts, 6)
            pe.wait_ge(vset, 8)
            ATTENTION.run(pe, turn)
            attention_over(pe)
            pe.wait_ge(plan_steps, 17)
            pe.transpose(rows_bank[0][0:1, 0:NT], tile_expert[0:NT, :], ident[0:NT, 0:NT])
            pe.transpose(rows_bank[0][0:1, NT:2 * NT], tile_row[0:NT, :], ident[0:NT, 0:NT]).then_inc(table_turned, 1)
            pe.wait_ge(moe_loaded, 3 * E * DMA)
            pe.wait_ge(table_ready, 1)

            def expert_turn(t):
                if t.active("A"):
                    k = t.parity("A")
                    pe.wait_ge(tile_loaded[k], t.dmas("A"))
                    if t.later("A", 2):
                        pe.wait_ge(ex_taken["A.x"], t.item("A", 1, -1))
                    for c in range(DC):
                        mm = pe.transpose(rows_bank[k][:, c * P:(c + 1) * P], tile_in[:, k, c * P:(c + 1) * P], ident[:, :])
                    mm.then_inc(ex_made["A.x"], 1)
                if t.active("B"):
                    n, k = t.item("B"), t.parity("B")
                    e = pe.value_load(table[0:1, bass.ds(n, 1)], min_val=0, max_val=E - 1)
                    pe.wait_ge(ex_taken["A.x"], t.item("B", 1, 1))
                    if t.later("B", 2):
                        pe.wait_ge(ex_taken["B.h"], t.item("B", 1, -1))
                    for c in range(DC):
                        mm = pe.matmul(hidden_bank[k][:, 0:F], tile_inT[:, k, c, :], hidden_w[:, c, bass.ds(e * F, F)],
                                       start=c == 0, stop=c == DC - 1)
                    mm.then_inc(ex_made["B.h"], 1)
                if t.active("C"):
                    k = t.parity("C")
                    pe.wait_ge(ex_taken["B.h"], t.item("C", 1, 1))
                    if t.later("C", 2):
                        pe.wait_ge(ex_taken["C.hT"], t.item("C", 1, -1))
                    for f in range(FC):
                        mm = pe.transpose(score[k][:, f * P:(f + 1) * P], hidden[:, k, f * P:(f + 1) * P], ident[:, :])
                    mm.then_inc(ex_made["C.hT"], 1)
                if t.base == EXPERTS.lag["D"]:
                    pe.wait_ge(output_w_loaded, E * DMA)
                if t.active("D"):
                    n, k = t.item("D"), t.parity("D")
                    e = pe.value_load(table[0:1, bass.ds(n, 1)], min_val=0, max_val=E - 1)
                    pe.wait_ge(ex_taken["C.hT"], t.item("D", 1, 1))
                    if t.later("D", 2):
                        pe.wait_ge(ex_taken["D.y"], t.item("D", 1, -1))
                    for f in range(FC):
                        mm = pe.matmul(output_bank[k][:, 0:D], hiddenT[:, k, f, :],
                                       output_w[f // (FC // 2)][:, f % (FC // 2), bass.ds(e * D, D)],
                                       start=f == 0, stop=f == FC - 1)
                    mm.then_inc(ex_made["D.y"], 1)

            EXPERTS.run(pe, expert_turn)


WEIGHTS = {"ln1_g": "L0_ffn_ln1_g", "ln1_b": "L0_ffn_ln1_b", "ln2_g": "L0_ffn_ln2_g", "ln2_b": "L0_ffn_ln2_b",
           "gate_w": "L0_ffn_gW", "gate_b": "L0_ffn_gb", "hidden_w": "L0_ffn_W1", "hidden_b": "L0_ffn_b1",
           "output_w": "L0_ffn_W2", "output_b": "L0_ffn_b2", "g_xattn": "g_xattn", "g_ffn": "g_ffn"}


def kernel(**inputs):
    import numpy as np
    import concourse.bacc as bacc
    from concourse.bass_utils import run_bass_kernel_spmd

    arrays = {"x": np.asarray(inputs["x"]).reshape(NB * T, D), "ctx": np.asarray(inputs["ctx_1024"]).reshape(NB * S, D)}
    for name, source in WEIGHTS.items():
        arrays[name] = np.asarray(inputs[source])
    for c in "qkvo":
        arrays["wx" + c] = np.asarray(inputs["L0_xattn_W" + c]).T
        arrays["bx" + c] = np.asarray(inputs["L0_xattn_b" + c])
        arrays["ws" + c] = np.asarray(inputs["L0_ffn_W" + c])
        arrays["bs" + c] = np.asarray(inputs["L0_ffn_b" + c])
    for name in ("wxq", "wxk", "wsq", "wsk", "bxq", "bxk", "bsq", "bsk"):
        a = arrays[name]
        arrays[name] = a.reshape(-1, DC, HC, HD).transpose(0, 1, 3, 2).reshape(a.shape)
    nc = bacc.Bacc("TRN2", target_bir_lowering=False, num_devices=1)
    io, feed = {}, {}
    for name, a in arrays.items():
        feed[f"in_{name}_dram"] = np.ascontiguousarray(a)
        io[name] = nc.dram_tensor(f"in_{name}_dram", a.shape, F32, kind="ExternalInput").ap()
    io["out"] = nc.dram_tensor("out_dram", (NB * T, D), F32, kind="ExternalOutput").ap()
    for name, rows, columns in (("kept", SPILL + NT * P, D), ("sent", E * REGION, SENT)):
        io[name] = nc.dram_tensor(f"{name}_dram", (rows, columns), F32).ap()
    for k in range(2):
        for name, parts, columns in ((f"k_parts_A{k}", PARTS, S), (f"q_parts_A{k}", PARTS, T), (f"qk_parts_C{k}", 2 * PARTS, T)):
            io[name] = nc.dram_tensor(f"{name}_dram", (DC, parts, HD, HC, columns), BF16).ap()
    build(nc, io)
    r = run_bass_kernel_spmd(nc, [feed], core_ids=[0])
    return r.results[0]["out_dram"].reshape(NB, T, D)
```
